# Optimizing a Trainium2 kernel written in Bass

```python
import numpy as np
import jax
import jax.numpy as jnp

def _softmax(x, axis=-1):
    return jax.nn.softmax(x, axis=axis)

def _gelu(x):
    return jax.nn.gelu(x, approximate=True)

def _silu(x):
    return jax.nn.silu(x)

def _sigmoid(x):
    return jax.nn.sigmoid(x)

def _layernorm(x, axis=-1, eps=1e-05):
    m = jnp.mean(x, axis=axis, keepdims=True)
    v = jnp.var(x, axis=axis, keepdims=True)
    return (x - m) / jnp.sqrt(v + eps)

def _scatter_add(tgt, idx, src, axis=0):
    return tgt.at[idx].add(src)

def _segment_sum(src, seg, n):
    return jax.ops.segment_sum(src, seg, n)
kernel_name = 'mk_seq_postln_d1_jaxref_r4_eff9ad'

def setup_inputs(seed: int=0):
    np.random.seed(seed)
    _w = jnp.asarray

    def _L0_attn_setup():
        import jax, jax.numpy as jnp
        import numpy as np
        import math

        def _alibi_slopes(n_heads):

            def pow2(n):
                start = 2 ** (-2 ** (-(math.log2(n) - 3)))
                return [start ** i for i in range(n)]
            if math.log2(n_heads).is_integer():
                slopes = pow2(n_heads)
            else:
                closest = 2 ** math.floor(math.log2(n_heads))
                slopes = pow2(closest) + _alibi_slopes(2 * closest).tolist()[0::2][:n_heads - closest]
            return np.asarray(slopes, dtype=np.float32)
        key = jax.random.key(seed)
        ks = jax.random.split(key, 4)
        B, L, D = (2, 512, 256)
        s = 1.0 / math.sqrt(D)
        return {'x': jax.random.normal(ks[0], (B, L, D), jnp.float32), 'Wqkv': jax.random.normal(ks[1], (D, 3 * D), jnp.float32) * s, 'bqkv': jnp.zeros((3 * D,), jnp.float32), 'Wout': jax.random.normal(ks[2], (D, D), jnp.float32) * s, 'bout': jnp.zeros((D,), jnp.float32)}
    _L0_attn_in = _L0_attn_setup()

    def _L0_ffn_setup():
        import math
        import jax, jax.numpy as jnp
        import numpy as np
        NUM_EXPERTS = 8
        TOP_K = 2
        CAPACITY_FACTOR = 1.0
        B, S, H, I = (4, 512, 256, 1024)
        key = jax.random.key(seed)
        k_x, k_rw, k_wi, k_wo = jax.random.split(key, 4)
        x = jax.random.normal(k_x, (B, S, H), dtype=jnp.float32)
        lim = math.sqrt(6.0 / (H + NUM_EXPERTS))
        router_w = jax.random.uniform(k_rw, (NUM_EXPERTS, H), minval=-lim, maxval=lim, dtype=jnp.float32)
        router_b = jnp.zeros((NUM_EXPERTS,), dtype=jnp.float32)
        experts_inter = jax.random.normal(k_wi, (NUM_EXPERTS - 1, H, I), dtype=jnp.float32) / math.sqrt(H)
        experts_out = jax.random.normal(k_wo, (NUM_EXPERTS - 1, I, H), dtype=jnp.float32) / math.sqrt(I)
        return {'x': x, 'router_w': router_w, 'router_b': router_b, 'experts_inter': experts_inter, 'experts_out': experts_out}
    _L0_ffn_in = _L0_ffn_setup()
    _d = {'L0_attn_x': _L0_attn_in['x'], 'L0_attn_Wqkv': _L0_attn_in['Wqkv'], 'L0_attn_bqkv': _L0_attn_in['bqkv'], 'L0_attn_Wout': _L0_attn_in['Wout'], 'L0_attn_bout': _L0_attn_in['bout'], 'L0_ffn_router_w': _L0_ffn_in['router_w'], 'L0_ffn_router_b': _L0_ffn_in['router_b'], 'L0_ffn_experts_inter': _L0_ffn_in['experts_inter'], 'L0_ffn_experts_out': _L0_ffn_in['experts_out']}
    _x0 = _d['L0_attn_x']
    _d['L0_attn_x'] = jax.random.normal(jax.random.fold_in(jax.random.key(seed), 1), (2, 2048, 256), dtype=_x0.dtype)
    del _x0
    return _d

def reference(L0_attn_x, L0_attn_Wqkv, L0_attn_bqkv, L0_attn_Wout, L0_attn_bout, L0_ffn_router_w, L0_ffn_router_b, L0_ffn_experts_inter, L0_ffn_experts_out):

    def _L0_attn_ref(x, Wqkv, bqkv, Wout, bout):
        import jax, jax.numpy as jnp
        import numpy as np
        import math

        def _alibi_slopes(n_heads):

            def pow2(n):
                start = 2 ** (-2 ** (-(math.log2(n) - 3)))
                return [start ** i for i in range(n)]
            if math.log2(n_heads).is_integer():
                slopes = pow2(n_heads)
            else:
                closest = 2 ** math.floor(math.log2(n_heads))
                slopes = pow2(closest) + _alibi_slopes(2 * closest).tolist()[0::2][:n_heads - closest]
            return np.asarray(slopes, dtype=np.float32)
        n_heads = 16
        B, L, D = x.shape
        head_dim = D // n_heads
        qkv = (x @ Wqkv + bqkv).reshape(B, L, 3, n_heads, head_dim)
        q, k, v = (qkv[:, :, 0], qkv[:, :, 1], qkv[:, :, 2])
        scores = jnp.einsum('bqhd,bkhd->bhqk', q, k) / math.sqrt(head_dim)
        pos = jnp.arange(L)
        bias = -jnp.abs(pos[None, :] - pos[:, None]).astype(jnp.float32)
        slopes = jnp.asarray(_alibi_slopes(n_heads))
        scores = scores + slopes[None, :, None, None] * bias[None, None]
        probs = jax.nn.softmax(scores, axis=-1)
        out = jnp.einsum('bhqk,bkhd->bqhd', probs, v).reshape(B, L, D)
        return out @ Wout + bout

    def _L0_ffn_ref(x, router_w, router_b, experts_inter, experts_out):
        import math
        import jax, jax.numpy as jnp
        import numpy as np
        NUM_EXPERTS = 8
        TOP_K = 2
        CAPACITY_FACTOR = 1.0
        B, S, H, I = (4, 512, 256, 1024)
        batch, seq, hidden = x.shape
        n_exp = router_w.shape[0]
        n_tok = batch * seq
        cap = math.ceil(n_tok / n_exp * CAPACITY_FACTOR)
        logits = jnp.einsum('bsh,eh->bse', x, router_w) + router_b
        weights_flat = jax.nn.softmax(logits, axis=-1).reshape(n_tok, n_exp)
        x_flat = x.reshape(n_tok, hidden)
        topk_vals, topk_idx = jax.lax.top_k(weights_flat, TOP_K)
        rows = jnp.arange(n_tok)[:, None]
        topk_flat = jnp.zeros_like(weights_flat).at[rows, topk_idx].set(topk_vals)
        routing_mask = (topk_flat > 0).astype(jnp.int32)
        noop_w = topk_flat[:, -1]
        noop_mask = routing_mask[:, -1].astype(x.dtype)
        expert_w = topk_flat[:, :-1]
        expert_mask = routing_mask[:, :-1]
        sorted_indices = jnp.argsort(-expert_mask, axis=0)[:cap]
        sorted_mask = jnp.take_along_axis(expert_mask, sorted_indices, axis=0)
        used_idx = (sorted_indices * sorted_mask).reshape(-1)
        inputs = x_flat[used_idx] * sorted_mask.reshape(-1).astype(x.dtype)[:, None]
        inputs = inputs.reshape(cap, n_exp - 1, hidden)
        in_w = jnp.take_along_axis(expert_w, sorted_indices, axis=0)
        h = jax.nn.relu(jnp.einsum('ceh,ehi->cei', inputs, experts_inter))
        out = jnp.einsum('cei,eih->ceh', h, experts_out) * in_w[..., None]
        combined = jnp.zeros_like(x_flat).at[used_idx].add(out.reshape(-1, hidden))
        combined = combined + x_flat * (noop_w * noop_mask)[:, None]
        return combined.reshape(batch, seq, hidden)
    x = L0_attn_x
    x = _layernorm(x + _L0_attn_ref(x, L0_attn_Wqkv, L0_attn_bqkv, L0_attn_Wout, L0_attn_bout), axis=-1)
    x = _layernorm(x + _L0_ffn_ref(x, L0_ffn_router_w, L0_ffn_router_b, L0_ffn_experts_inter, L0_ffn_experts_out), axis=-1)
    return x

_drawn_inputs = setup_inputs


def setup_inputs(seed=0):
    import zlib

    import numpy as np

    out = dict(_drawn_inputs(seed))
    spreads = {'L0_attn_bqkv': (0.0, 0.1), 'L0_attn_bout': (0.0, 0.1), 'L0_ffn_router_b': (0.0, 0.1)}
    factors = {}
    for name, (base, spread) in spreads.items():
        noise = np.random.default_rng([zlib.crc32(name.encode()), seed]).standard_normal(out[name].shape)
        drawn = base * np.exp(spread * noise) if base else spread * noise
        out[name] = jnp.asarray(drawn.astype(out[name].dtype))
    for name, factor in factors.items():
        out[name] = (out[name] * factor).astype(out[name].dtype)
    return out
```

```python
import concourse.bass as bass
from concourse import mybir
from contextlib import ExitStack

F32 = mybir.dt.float32
BF16 = mybir.dt.bfloat16
I32 = mybir.dt.int32
ALU = mybir.AluOpType
ACT = mybir.ActivationFunctionType
AX = mybir.AxisListType

B, L, D, H = 2, 2048, 256, 16
HD = D // H
T = B * L
E, EX, F = 8, 7, 1024
CAP = T // E
EPS = 1e-5
P = 128
CH = 512
NCH = T // CH
TPC = CH // P
NT = T // P
KB = L // P
QG = L // CH

POS = 12
PAIRS = 6
ROW_M = POS + PAIRS * HD
ROWS = ROW_M + 3
Q_PART = [0, 0, 0, 1, 1, 2]
K_PART = [0, 1, 2, 0, 1, 0]
RIGHT, LEFT, DIAG = range(3)

SLOT_BANKS = 3
TILES = KB * QG
CHUNKS = -(-TILES // SLOT_BANKS)
RING = 6
PV_LAG = 3

ST = CAP // P
LOT_PLACE, LOT_TILE, LOT_TAKEN, LOT_W = 0, 1, 2, 3
LOT = 6


def chunk_tiles(ch):
    return [(n // QG, n % QG) for n in range(ch * SLOT_BANKS, min((ch + 1) * SLOT_BANKS, TILES))]


def blocks_done(ch):
    return min((ch + 1) * SLOT_BANKS, TILES) // QG if ch >= 0 else 0


def ring_user_before(b, ch):
    if ch >= RING:
        return b, ch - RING
    last = max(c for c in range(CHUNKS) if c % RING == ch % RING)
    return b - 1, last


def project_phase(nc, outer, t, x, wqkv, bqkv, parts_dram, ps):
    with ExitStack() as ctx:
        def sb(name, shape, dt):
            return ctx.enter_context(nc.sbuf_tensor(name, shape, dt))

        def sem(name):
            return ctx.enter_context(nc.semaphore(name))

        xin = [sb(f"xin{p}", [P, TPC, D], F32) for p in range(2)]
        xT = [sb(f"xT{p}", [P, 2, CH], F32) for p in range(2)]
        w = sb("w_qkv", [P, 2, 3 * D], F32)
        bcol = sb("bias_qk_columns", [P, 4], F32)
        bv = sb("bias_v_rows", [P, 2, D], F32)
        split = [sb(f"split{m}", [P, 3, CH], BF16) for m in range(4)]
        rest = [sb(f"rest{m}", [P, CH], F32) for m in range(4)]

        w_in = sem("w_in")
        x_in = [sem(f"x_in{p}") for p in range(2)]
        scaled = sem("scaled")
        xT_mm = sem("xT_mm")
        xT_a = sem("xT_evacuated_by_act")
        xT_v = sem("xT_evacuated_by_dve")
        qk_mm = sem("qk_mm")
        hi_done = sem("hi_part_done")
        rest_done = sem("rest_done")
        mid_done = sem("mid_part_done")
        lo_done = sem("lo_part_done")
        parts_out = [sem(f"parts_out{m}") for m in range(4)]
        v_mm = sem("v_mm")
        v_done = sem("v_done")
        block = ctx.enter_context(nc.Block())


        @block.sync
        def _(sp):
            sp.dma_start(w[:, :, :], wqkv.rearrange("(k p) n -> p k n", p=P)).then_inc(w_in, 16)
            sp.dma_start(bcol[:, :], bqkv[0:2 * D].rearrange("(m p) -> p m", p=P),
                         allow_slow_non_contiguous=True).then_inc(w_in, 16)
            for r in range(2):
                sp.dma_start(bv[:, r, :], bqkv[2 * D:3 * D].rearrange("(a n) -> a n", a=1).broadcast_to([P, D]))\
                  .then_inc(w_in, 16)
            with sp.Fori(0, NCH // 2) as i:
                for par in range(2):
                    sp.wait_ge(xT_mm, i * 4 + 2 * par + 2)
                    sp.dma_start(xin[par][:, :, :],
                                 x[bass.ds((i * 2 + par) * TPC, TPC), :, :].rearrange("t p n -> p t n"))\
                      .then_inc(x_in[par], 16)
                for par in range(2):
                    for m in range(4):
                        sp.wait_ge(lo_done, i * 8 + par * 4 + m + 5)
                        for part in range(3):
                            sp.dma_start(parts_dram[m // 2, (m % 2) * 8:(m % 2) * 8 + 8, part, :,
                                                    bass.ds((i * 2 + par) * CH, CH)],
                                         split[m][:, part, :]).then_inc(parts_out[m], 16)
            for m in range(4):
                sp.wait_ge(parts_out[m], 48 * (NCH + 1))

        @block.tensor
        def _(pe):
            pe.sem_inc(xT_mm, 4)
            pe.sem_inc(v_mm, 4)
            pe.wait_ge(t["ident_done"], 2)
            pe.wait_ge(scaled, 2)
            with pe.Fori(0, NCH // 2) as i:
                for par in range(2):
                    pe.wait_ge(x_in[par], i * 16 + 16)
                    for k in range(2):
                        pe.wait_ge(xT_a if k == 0 else xT_v, i * 2 + par + 1)
                        for s in range(TPC):
                            mm = pe.transpose(ps[:, k, s * P:(s + 1) * P], xin[par][:, s, k * P:(k + 1) * P],
                                              t["ident"][:, :])
                        mm.then_inc(xT_mm, 1)
                    pe.wait_ge(xT_a, i * 2 + par + 2)
                    pe.wait_ge(xT_v, i * 2 + par + 2)
                    for m in range(4):
                        pe.wait_ge(rest_done, i * 8 + par * 4 + m + 1)
                        for k in range(2):
                            mm = pe.matmul(ps[:, 2 + m, :], w[:, k, m * P:(m + 1) * P], xT[par][:, k, :],
                                           start=(k == 0), stop=(k == 1))
                        mm.then_inc(qk_mm, 1)
                    for pair in range(2):
                        pe.wait_ge(v_done, i * 4 + par * 2 + pair + 1)
                        for s in range(2):
                            tok = (pair * 2 + s) * P
                            for k in range(2):
                                mm = pe.matmul(ps[:, 6 + pair, s * D:(s + 1) * D], xT[par][:, k, tok:tok + P],
                                               w[:, k, 2 * D:3 * D], start=(k == 0), stop=(k == 1))
                        mm.then_inc(v_mm, 1)

        @block.scalar
        def _(act):
            act.sem_inc(xT_a, 1)

            def hi(i, par, m):
                act.wait_ge(qk_mm, i * 8 + par * 4 + m + 1)
                act.wait_ge(parts_out[m], (i * 2 + par) * 48 + 48)
                act.activation(split[m][:, 0, :], ps[:, 2 + m, :], ACT.Identity, bias=bcol[:, m:m + 1])\
                   .then_inc(hi_done, 1)

            def mid(i, par, m):
                act.wait_ge(rest_done, i * 8 + par * 4 + m + 5)
                act.activation(split[m][:, 1, :], rest[m][:, :], ACT.Copy).then_inc(mid_done, 1)

            act.wait_ge(scaled, 2)
            with act.Fori(0, NCH // 2) as i:
                for par in range(2):
                    act.wait_ge(xT_mm, i * 4 + par * 2 + 5)
                    act.wait_ge(v_mm, i * 4 + par * 2 + 2)
                    act.activation(xT[par][:, 0, :], ps[:, 0, :], ACT.Copy).then_inc(xT_a, 1)
                    hi(i, par, 0)
                    for m in range(1, 4):
                        hi(i, par, m)
                        mid(i, par, m - 1)
                    mid(i, par, 3)

        @block.vector
        def _(dve):
            dve.sem_inc(xT_v, 1)
            dve.sem_inc(rest_done, 4)
            dve.sem_inc(lo_done, 4)
            dve.sem_inc(v_done, 2)
            for m in range(4):
                dve.sem_inc(parts_out[m], 48)
            dve.wait_ge(w_in, 64)
            dve.tensor_scalar(w[:, :, 0:D], w[:, :, 0:D], HD ** -0.5, None, ALU.mult).then_inc(scaled, 1)
            dve.tensor_scalar(bcol[:, 0:2], bcol[:, 0:2], HD ** -0.5, None, ALU.mult).then_inc(scaled, 1)
            dve.wait_ge(scaled, 2)

            def take_rest(i, par, m):
                dve.wait_ge(hi_done, i * 8 + par * 4 + m + 1)
                dve.wait_ge(lo_done, i * 8 + par * 4 + m + 1)
                dve.scalar_tensor_tensor(out=rest[m][:, :], in0=ps[:, 2 + m, :], scalar=bcol[:, m:m + 1],
                                         in1=split[m][:, 0, :], op0=ALU.add, op1=ALU.subtract)\
                   .then_inc(rest_done, 1)

            def lo(i, par, m):
                dve.wait_ge(mid_done, i * 8 + par * 4 + m + 1)
                dve.tensor_tensor(split[m][:, 2, :], rest[m][:, :], split[m][:, 1, :], ALU.subtract)\
                   .then_inc(lo_done, 1)

            with dve.Fori(0, NCH // 2) as i:
                for par in range(2):
                    dve.wait_ge(xT_mm, i * 4 + par * 2 + 6)
                    dve.wait_ge(v_mm, i * 4 + par * 2 + 2)
                    dve.tensor_copy(xT[par][:, 1, :], ps[:, 1, :]).then_inc(xT_v, 1)
                    take_rest(i, par, 0)
                    for m in range(1, 4):
                        take_rest(i, par, m)
                        lo(i, par, m - 1)
                    lo(i, par, 3)
                    for pair in range(2):
                        dve.wait_ge(v_mm, i * 4 + par * 2 + pair + 5)
                        dve.tensor_tensor(t["v"][:, bass.ds((i * 2 + par) * TPC + pair * 2, 2), :],
                                          ps[:, 6 + pair, :].rearrange("p (s n) -> p s n", s=2), bv[:, :, :],
                                          ALU.add).then_inc(v_done, 1)

        @block.gpsimd
        def _(pool):
            ident, step = t["ident"], t["ident_done"]
            pool.memset(ident[:, :], 0.0).then_inc(step, 1)
            pool.wait_ge(step, 1)
            pool.affine_select(out=ident[:, :], in_=ident[:, :], compare_op=ALU.not_equal, fill=1.0, base=0,
                               pattern=[[-1, P]], channel_multiplier=1).then_inc(step, 1)


def attention_phase(nc, outer, t, parts_dram, heads_dram, q_pos, k_pos, slopes, ps):
    with ExitStack() as ctx:
        def sb(name, shape, dt):
            return ctx.enter_context(nc.sbuf_tensor(name, shape, dt))

        def sem(name):
            return ctx.enter_context(nc.semaphore(name))

        q_st = [sb(f"q_stack{b}", [ROWS, L], BF16) for b in range(B)]
        k_st = [sb(f"k_stack{b}", [ROWS, 3, L], BF16) for b in range(B)]
        prob = sb("prob", [P, RING, SLOT_BANKS * CH], F32)
        vh = [sb(f"v_head{b}", [P, KB, 32], F32) for b in range(B)]
        dist = sb("distance", [P, P], F32)
        nslope = sb("minus_slopes", [P, H], F32)
        near = sb("near_bias", [P, H, P], F32)
        unit_max = sb("unit_max", [P, KB, 2], F32)
        row_max = sb("row_max", [P, KB], F32)
        neg_max = sb("neg_max", [KB, P], F32)
        max_rest = sb("max_rest", [KB, P], F32)
        max_parts = sb("max_parts", [KB, 3, P], BF16)
        o_sb = sb("o_sum", [P, CH], F32)
        o_den = sb("o_den", [P, CH], F32)
        o_rec = sb("o_rec", [P, CH], F32)
        o_out = [sb(f"o_out{b}", [P, CH], F32) for b in range(B)]

        consts_in = sem("attn_consts_in")
        ones_done = sem("ones_done")
        dist_done = sem("dist_done")
        near_done = sem("near_done")
        stack_in = [sem(f"stack_in{b}") for b in range(B)]
        unit_mm = sem("unit_mm")
        unit_bias = sem("unit_bias")
        unit_done = sem("unit_done")
        max_step = sem("max_step")
        max_T = sem("max_T")
        max_ready = sem("max_ready")
        max_in = [sem(f"max_in{b}") for b in range(B)]
        vh_done = sem("vh_done")
        scored = sem("scored")
        expd = sem("expd")
        diag_done = sem("diag_done")
        pv_done = sem("pv_done")
        o_read = sem("o_read")
        o_step = sem("o_step")
        o_ready = sem("o_ready")
        hold = sem("attn_hold")
        o_stored = [sem(f"o_stored{b}") for b in range(B)]
        block = ctx.enter_context(nc.Block())

        LOADS = (1 + 6) + 3 * (1 + 3)

        @block.sync
        def _(sp):
            sp.dma_start(nslope[:, :], slopes).then_inc(consts_in, 16)
            for b in range(B):
                for ver in range(3):
                    sp.dma_start(k_st[b][ROW_M:ROWS, ver, :], k_pos[0, ver, POS:POS + 3, :]).then_inc(consts_in, 16)
            with sp.Fori(0, H) as h:
                for b in range(B):
                    sp.wait_ge(scored, h * (2 * CHUNKS) + (b + 1) * CHUNKS)
                    load = lambda dst, src: sp.dma_start(dst, src).then_inc(stack_in[b], 16)
                    load(q_st[b][0:POS, :], q_pos[bass.ds(h, 1), :, :].rearrange("h r n -> (h r) n"))

                    def part_rows(side, part0, parts):
                        return parts_dram[side, bass.ds(h, 1), part0:part0 + parts, :, b * L:(b + 1) * L]\
                            .rearrange("h p d n -> (h p d) n")

                    for g, part in enumerate(Q_PART):
                        r0 = POS + g * HD
                        load(q_st[b][r0:r0 + HD, :], part_rows(0, part, 1))
                    for ver in range(3):
                        load(k_st[b][0:POS, ver, :], k_pos[bass.ds(h, 1), ver, 0:POS, :].rearrange("h r n -> (h r) n"))
                        r0 = POS
                        for n in (3, 2, 1):
                            load(k_st[b][r0:r0 + n * HD, ver, :], part_rows(1, 0, n))
                            r0 += n * HD
                    sp.wait_ge(max_ready, h * 2 + b + 1)
                    for part in range(3):
                        sp.dma_start(q_st[b][ROW_M + part:ROW_M + part + 1, :].rearrange("r (t n) -> r t n", t=KB),
                                     max_parts[:, part, :]).then_inc(max_in[b], 16)
                    sp.wait_ge(o_ready, h * 2 + b + 1)
                    for g in range(QG):
                        sp.dma_start(heads_dram[b, bass.ds(h * HD, HD), g * CH:(g + 1) * CH],
                                     o_out[b][32 * g:32 * g + HD, :]).then_inc(o_stored[b], 16)
            for b in range(B):
                sp.wait_ge(o_stored[b], 64 * (H + 1))

        @block.tensor
        def _(pe):
            pe.sem_inc(scored, 2 * CHUNKS)
            pe.sem_inc(pv_done, 2 * KB)
            pe.wait_ge(consts_in, 16 * 7)
            with pe.Fori(0, H) as h:
                for b in range(B):
                    pe.wait_ge(stack_in[b], h * (16 * LOADS) + 16 * LOADS)
                    pe.wait_ge(expd, h * (2 * CHUNKS) + (b + 2) * CHUNKS)
                    for u in range(2 * KB):
                        i, half = divmod(u, 2)
                        if u >= 3:
                            pe.wait_ge(unit_done, h * (4 * KB) + b * 2 * KB + u - 2)
                        for bank in range(2):
                            k0 = half * 1024 + bank * CH
                            cuts = sorted({k0, k0 + CH, *(c for c in (i * P, i * P + P) if k0 < c < k0 + CH)})
                            for a, z in zip(cuts, cuts[1:]):
                                ver = RIGHT if z <= i * P else LEFT if a >= i * P + P else DIAG
                                mm = pe.matmul(ps[:, 2 * (u % 3) + bank, a - k0:z - k0],
                                               q_st[b][0:ROW_M, i * P:(i + 1) * P], k_st[b][0:ROW_M, ver, a:z],
                                               start=True, stop=True)
                        mm.then_inc(unit_mm, 1)
                    pe.wait_ge(max_step, h * 10 + b * 5 + 1)
                    pe.transpose(ps[0:KB, 0, 0:P], row_max[:, :], t["ident"][:, :]).then_inc(max_T, 1)
                    pe.wait_ge(max_in[b], h * 48 + 48)
                    pe.wait_ge(vh_done, h * 2 + b + 3)

                    def score(ch):
                        if ch >= 2:
                            pe.wait_ge(expd, h * (2 * CHUNKS) + (b + 2) * CHUNKS + ch - 1)
                        for n, (kb, g) in enumerate(chunk_tiles(ch)):
                            bank = SLOT_BANKS * (ch % 2) + n
                            q0, k0 = g * CH, kb * P
                            cuts = sorted({q0, q0 + CH, *(c for c in (k0, k0 + P) if q0 < c < q0 + CH)})
                            for a, z in zip(cuts, cuts[1:]):
                                ver = LEFT if z <= k0 else RIGHT if a >= k0 + P else DIAG
                                mm = pe.matmul(ps[:, bank, a - q0:z - q0], k_st[b][0:ROWS, ver, k0:k0 + P],
                                               q_st[b][0:ROWS, a:z], start=True, stop=True)
                        mm.then_inc(scored, 1)

                    def pv(kb):
                        if kb == 0:
                            pe.wait_ge(o_read, h * 2 + b + 1)
                        last = (QG * kb + QG - 1) // SLOT_BANKS
                        pe.wait_ge(expd, h * (2 * CHUNKS) + (b + 2) * CHUNKS + last + 1)
                        pe.wait_ge(diag_done, h * (2 * KB) + b * KB + kb + 1)
                        for g in range(QG):
                            n = QG * kb + g
                            ch, c = divmod(n, SLOT_BANKS)
                            mm = pe.matmul(ps[32 * g:32 * g + 32, 6 + b, :], vh[b][:, kb, :],
                                           prob[:, ch % RING, c * CH:(c + 1) * CH],
                                           start=(kb == 0), stop=(kb == KB - 1))
                        mm.then_inc(pv_done, 1)

                    for ch in range(CHUNKS):
                        score(ch)
                        for kb in range(blocks_done(ch - PV_LAG - 1), blocks_done(ch - PV_LAG)):
                            pv(kb)
                    for kb in range(blocks_done(CHUNKS - 1 - PV_LAG), KB):
                        pv(kb)

        @block.scalar
        def _(act):
            act.sem_inc(expd, 2 * CHUNKS)
            act.wait_ge(consts_in, 16 * 7)
            act.wait_ge(dist_done, 3)
            for h in range(H):
                act.activation(near[:, h, :], dist[:, :], ACT.Exp, scale=nslope[:, h:h + 1]).then_inc(near_done, 1)
            with act.Fori(0, H) as h:
                for b in range(B):
                    for ch in range(CHUNKS):
                        act.wait_ge(scored, h * (2 * CHUNKS) + (b + 2) * CHUNKS + ch + 1)
                        pb, pch = ring_user_before(b, ch)
                        act.wait_ge(pv_done, h * (2 * KB) + (pb + 2) * KB
                                    + (min(pch * SLOT_BANKS + SLOT_BANKS, TILES) - 1) // QG + 1)
                        n = len(chunk_tiles(ch))
                        bank = SLOT_BANKS * (ch % 2)
                        act.activation(prob[:, ch % RING, 0:n * CH],
                                       ps[:, bank:bank + n, :].rearrange("p c n -> p (c n)"),
                                       ACT.Exp).then_inc(expd, 1)

        @block.vector
        def _(dve):
            dve.sem_inc(o_read, 2)
            for b in range(B):
                dve.sem_inc(o_stored[b], 64)
            for b in range(B):
                dve.memset(vh[b][:, :, HD:32], 1.0).then_inc(ones_done, 1)
            dve.wait_ge(dist_done, 2)
            dve.scalar_tensor_tensor(out=dist[:, :], in0=near[:, 0, :], scalar=-1.0, in1=near[:, 0, :],
                                     op0=ALU.mult, op1=ALU.max).then_inc(dist_done, 1)
            dve.wait_ge(near_done, H)
            with dve.Fori(0, H) as h:
                for b in range(B):
                    for u in range(2 * KB):
                        i, half = divmod(u, 2)
                        dve.wait_ge(unit_mm, h * (4 * KB) + b * 2 * KB + u + 1)
                        if i * P // 1024 == half:
                            bank, a = divmod(i * P - half * 1024, CH)
                            here = ps[:, 2 * (u % 3) + bank, a:a + P]
                            dve.scalar_tensor_tensor(out=here, in0=dist[:, :], scalar=nslope[:, bass.ds(h, 1)],
                                                     in1=here, op0=ALU.mult, op1=ALU.add).then_inc(unit_bias, 1)
                            dve.wait_ge(unit_bias, h * (2 * KB) + b * KB + i + 1)
                        dve.tensor_reduce(unit_max[:, i, half:half + 1],
                                          ps[:, 2 * (u % 3):2 * (u % 3) + 2, :].rearrange("p c n -> p (c n)"),
                                          AX.X, ALU.max).then_inc(unit_done, 1)
                    dve.wait_ge(unit_done, h * (4 * KB) + (b + 1) * 2 * KB)
                    step = h * 10 + b * 5
                    dve.tensor_tensor(row_max[:, :], unit_max[:, :, 0], unit_max[:, :, 1], ALU.max)\
                       .then_inc(max_step, 1)
                    dve.wait_ge(max_T, h * 2 + b + 1)
                    dve.tensor_scalar(neg_max[:, :], ps[0:KB, 0, 0:P], -1.0, None, ALU.mult).then_inc(max_step, 1)
                    dve.wait_ge(max_step, step + 2)
                    dve.tensor_copy(max_parts[:, 0, :], neg_max[:, :]).then_inc(max_step, 1)
                    dve.wait_ge(max_step, step + 3)
                    dve.tensor_tensor(max_rest[:, :], neg_max[:, :], max_parts[:, 0, :], ALU.subtract)\
                       .then_inc(max_step, 1)
                    dve.wait_ge(max_step, step + 4)
                    dve.tensor_copy(max_parts[:, 1, :], max_rest[:, :]).then_inc(max_step, 1)
                    dve.wait_ge(max_step, step + 5)
                    dve.tensor_tensor(max_parts[:, 2, :], max_rest[:, :], max_parts[:, 1, :], ALU.subtract)\
                       .then_inc(max_ready, 1)
                    for kb in range(KB):
                        g, off = divmod(kb * P, CH)
                        n = QG * kb + g
                        ch, c = divmod(n, SLOT_BANKS)
                        dve.wait_ge(expd, h * (2 * CHUNKS) + (b + 2) * CHUNKS + ch + 1)
                        here = prob[:, ch % RING, c * CH + off:c * CH + off + P]
                        dve.tensor_tensor(here, here, near[:, bass.ds(h, 1), :].rearrange("p a n -> p (a n)"),
                                          ALU.mult).then_inc(diag_done, 1)
                    dve.wait_ge(pv_done, h * (2 * KB) + (b + 3) * KB)
                    dve.tensor_copy(o_sb[:, :], ps[:, 6 + b, :]).then_inc(o_read, 1)
                    dve.wait_ge(o_read, h * 2 + b + 3)
                    dve.sem_inc(hold, 1)
                    dve.stream_shuffle(o_den[:, :], o_sb[:, :], [HD] * 32).then_inc(o_step, 1)
                    dve.wait_ge(o_step, h * 4 + b * 2 + 1)
                    dve.reciprocal(o_rec[:, :], o_den[:, :]).then_inc(o_step, 1)
                    dve.wait_ge(o_step, h * 4 + b * 2 + 2)
                    dve.wait_ge(o_stored[b], h * 64 + 64)
                    dve.tensor_tensor(o_out[b][:, :], o_sb[:, :], o_rec[:, :], ALU.mult).then_inc(o_ready, 1)
                    dve.wait_ge(o_ready, h * 2 + b + 1)

        @block.gpsimd
        def _(pool):
            pool.iota(t["token_ids"][:, 0:P], [[1, P]], base=0, channel_multiplier=-1).then_inc(dist_done, 1)
            pool.wait_ge(dist_done, 1)
            pool.tensor_copy(near[:, 0, :], t["token_ids"][:, 0:P]).then_inc(dist_done, 1)
            pool.sem_inc(vh_done, 2)
            pool.wait_ge(ones_done, 2)
            with pool.Fori(0, H) as h:
                for b in range(B):
                    pool.wait_ge(pv_done, h * (2 * KB) + (b + 1) * KB)
                    pool.tensor_copy(vh[b][:, :, 0:HD], t["v"][:, b * KB:(b + 1) * KB, bass.ds(h * HD, HD)])\
                        .then_inc(vh_done, 1)


def prefix_ones(pool, upper, ones, step):
    pool.memset(ones[:, :], 1.0).then_inc(step, 1)
    pool.memset(upper[:, :], 1.0).then_inc(step, 1)
    pool.wait_ge(step, 2)
    pool.affine_select(out=upper[:, :], in_=upper[:, :], compare_op=ALU.is_gt, fill=0.0, base=0,
                       pattern=[[1, P]], channel_multiplier=-1).then_inc(step, 1)


def route_phase(nc, t, x, heads_dram, wout, bout, router_w, router_b, x1_dram, acc_dram, ps):
    with ExitStack() as ctx:
        def sb(name, shape, dt):
            return ctx.enter_context(nc.sbuf_tensor(name, shape, dt))

        def sem(name):
            return ctx.enter_context(nc.semaphore(name))

        wo = sb("w_out", [P, 2, D], F32)
        bo = sb("b_out", [P, TPC, D], F32)
        rw = sb("router_wT", [P, 2, E], F32)
        rb = sb("router_bias", [P, TPC, E], F32)
        oc = [sb(f"heads_chunk{p}", [P, 2, CH], F32) for p in range(2)]
        xc = [sb(f"x_chunk{p}", [P, TPC, D], F32) for p in range(2)]
        y = [sb(f"y{p}", [P, TPC, D], F32) for p in range(2)]
        x1T = [sb(f"x1T{p}", [P, 2, CH], F32) for p in range(2)]
        stats = sb("stats", [P, TPC, 6], F32)
        mv = sb("mean_var", [P, TPC, 2], F32)
        sd = sb("std", [P, TPC], F32)
        rstd = sb("rstd", [P, TPC], F32)
        eps = sb("eps", [P, 1], F32)
        x1 = sb("x1", [P, NT, D], F32)
        logits = sb("logits", [P, NT, E], F32)
        shape = [P, NT, E]
        ex = sb("ex", shape, F32)
        wgt = sb("weights", shape, F32)
        left = sb("weights_left", shape, F32)
        tmp = sb("tmp", shape, F32)
        pick = [sb(f"pick{k}", shape, F32) for k in range(2)]
        mask = sb("mask", shape, F32)
        before = sb("before", shape, F32)
        valid = sb("valid", shape, F32)
        tot = sb("totals", shape, F32)
        scan = sb("scan", shape, F32)
        expert_id = sb("expert_id", shape, F32)
        top = sb("top", [P, NT], F32)
        den = sb("den", [P, NT], F32)
        idx = [sb(f"choice{k}", [P, NT], F32) for k in range(2)]
        upper = sb("upper", [P, P], F32)
        ones = sb("ones", [P, P], F32)
        iota_i = sb("iota_i", shape, I32)
        tile_id = sb("tile_id", [P, NT], F32)
        place = sb("place", [P, NT], F32)
        in_tile = sb("slot_in_tile", shape, F32)
        of_tile = sb("slot_tile", shape, F32)
        lot_w = [sb(f"lot_w{n}", shape, BF16) for n in range(3)]
        lots = sb("lots", [P, NT, E, ST * LOT], BF16)
        columns = sb("columns", [P, P], F32)
        hits = [sb(f"hits{n}", [P, P], BF16) for n in range(4)]
        lot = sb("lot", [P, ST, LOT], F32)
        free = sb("free", [P, ST], F32)
        acc = [sb(f"acc{p}", [P, TPC, D], F32) for p in range(2)]
        keep = sb("keep", [P, NT], F32)

        w_in = sem("route_w_in")
        hold = sem("route_hold")
        oc_in = [sem(f"oc_in{p}") for p in range(2)]
        xc_in = [sem(f"xc_in{p}") for p in range(2)]
        biased = sem("x_biased")
        y_mm = sem("y_mm")
        y_done = sem("y_done")
        st_done = sem("stats_done")
        mv_done = sem("mean_var_done")
        sd_done = sem("std_done")
        rs_done = sem("rstd_done")
        ln_done = sem("ln_done")
        row_done = sem("row_done")
        x1_mm = sem("x1T_mm")
        x1_done = sem("x1T_done")
        lg_mm = sem("logits_mm")
        lg_done = sem("logits_done")
        step = sem("route_step")
        c_step = sem("route_const_step")
        cnt_mm = sem("counts_mm")
        exp_done = sem("router_exp_done")
        eps_done = sem("eps_done")
        kept = sem("kept")
        lots_done = sem("lots_done")
        hit = sem("hit")
        met = sem("met")
        lot_step = sem("lot_step")
        x1_out = [sem(f"x1_out{p}") for p in range(2)]
        acc_done = sem("acc_done")
        acc_out = [sem(f"acc_out{p}") for p in range(2)]
        block = ctx.enter_context(nc.Block())

        @block.sync
        def _(sp):
            sp.dma_start(wo[:, :, :], wout.rearrange("(k p) n -> p k n", p=P)).then_inc(w_in, 16)
            for s in range(TPC):
                sp.dma_start(bo[:, s, :], bout.rearrange("(a n) -> a n", a=1).broadcast_to([P, D])).then_inc(w_in, 16)
                sp.dma_start(rb[:, s, :], router_b.rearrange("(a n) -> a n", a=1).broadcast_to([P, E])).then_inc(w_in, 16)
            for k in range(2):
                sp.dma_start(rw[:, k, :], router_w[:, k * P:(k + 1) * P].rearrange("e p -> p e"),
                             allow_slow_non_contiguous=True).then_inc(w_in, 16)
            with sp.Fori(0, B) as b:
                for c in range(QG):
                    par = c % 2
                    n = b * QG + c
                    sp.wait_ge(y_mm, n * 2 + 2)
                    sp.dma_start(oc[par][:, :, :],
                                 heads_dram[bass.ds(b, 1), :, c * CH:(c + 1) * CH]
                                 .rearrange("b (k p) n -> p (b k) n", p=P)).then_inc(oc_in[par], 16)
                    sp.wait_ge(y_done, n * 2 + 2)
                    sp.dma_start(xc[par][:, :, :], x[bass.ds(n * TPC, TPC), :, :].rearrange("t p n -> p t n"))\
                      .then_inc(xc_in[par], 16)
            with sp.Fori(0, NCH // 2) as i:
                for par in range(2):
                    sp.wait_ge(acc_done, i * 2 + par + 1)
                    sp.dma_start(acc_dram[bass.ds((i * 2 + par) * TPC, TPC), :, :].rearrange("t p n -> p t n"),
                                 acc[par][:, :, :]).then_inc(acc_out[par], 16)
            for par in range(2):
                sp.wait_ge(acc_out[par], 16 * (NCH // 2) + 16)

        @block.tensor
        def _(pe):
            pe.sem_inc(y_mm, 4)
            pe.wait_ge(w_in, 16 * 11)
            with pe.Fori(0, NCH // 2) as i:
                for par in range(2):
                    n = i * 2 + par
                    pe.wait_ge(oc_in[par], i * 16 + 16)
                    for pair in range(2):
                        pe.wait_ge(y_done, n * 2 + pair + 3)
                        for s in range(2):
                            tok = (pair * 2 + s) * P
                            for k in range(2):
                                mm = pe.matmul(ps[:, pair, s * D:(s + 1) * D], oc[par][:, k, tok:tok + P],
                                               wo[:, k, :], start=(k == 0), stop=(k == 1))
                        mm.then_inc(y_mm, 1)
                    pe.wait_ge(ln_done, n * 4 + 8)
                    for k in range(2):
                        pe.wait_ge(x1_done, n * 2 + k + 1)
                        for s in range(TPC):
                            mm = pe.transpose(ps[:, 2 + k, s * P:(s + 1) * P], y[par][:, s, k * P:(k + 1) * P],
                                              t["ident"][:, :])
                        mm.then_inc(x1_mm, 1)
                    pe.wait_ge(x1_done, n * 2 + 4)
                    pe.wait_ge(lg_done, n + 1)
                    for s in range(TPC):
                        for k in range(2):
                            mm = pe.matmul(ps[:, 4, s * E:(s + 1) * E], x1T[par][:, k, s * P:(s + 1) * P],
                                           rw[:, k, :], start=(k == 0), stop=(k == 1))
                    mm.then_inc(lg_mm, 1)
            pe.wait_ge(step, 18)
            pe.wait_ge(c_step, 3)
            flat = mask[:, :, :].rearrange("p a b -> p (a b)")
            pe.matmul(ps[:, 5, 0:NT * E], upper[:, :], flat, start=True, stop=True).then_inc(cnt_mm, 1)
            pe.matmul(ps[:, 6, 0:NT * E], ones[:, :], flat, start=True, stop=True).then_inc(cnt_mm, 1)
            pe.sem_inc(met, 4)
            pe.wait_ge(lots_done, ST * LOT)
            with pe.Fori(0, EX) as e:
                pe.wait_ge(lot_step, e * 7 + 4)
                for n in range(NT):
                    pe.wait_ge(hit, e * NT + n + 1)
                    pe.matmul(ps[:, 7, 0:ST * LOT], hits[n % 4][:, :],
                              lots[:, n, bass.ds(e, 1), :].rearrange("p e l -> p (e l)"),
                              start=(n == 0), stop=(n == NT - 1)).then_inc(met, 1)

        @block.scalar
        def _(act):
            for par in range(2):
                act.sem_inc(x1_out[par], 16)
            act.sem_inc(x1_done, 2)
            act.wait_ge(eps_done, 1)
            with act.Fori(0, NCH // 2) as i:
                for par in range(2):
                    n = i * 2 + par
                    act.wait_ge(mv_done, n * 4 + 4)
                    act.wait_ge(rs_done, n + 1)
                    act.activation(sd[:, :], mv[:, :, 1], ACT.Sqrt, bias=eps[:, 0:1]).then_inc(sd_done, 1)
                    for k in range(2):
                        act.wait_ge(x1_mm, n * 2 + k + 1)
                        act.activation(x1T[par][:, k, :], ps[:, 2 + k, :], ACT.Copy).then_inc(x1_done, 1)
                    act.wait_ge(ln_done, n * 4 + 8)
                    act.dma_start(x1_dram[bass.ds(n * TPC, TPC), :, :].rearrange("t p n -> p t n"), y[par][:, :, :])\
                       .then_inc(x1_out[par], 16)
            for par in range(2):
                act.wait_ge(x1_out[par], 16 * (NCH // 2) + 16)
            act.wait_ge(step, 2)
            act.activation(ex[:, :, :], tmp[:, :, :], ACT.Exp).then_inc(exp_done, 1)

        @block.vector
        def _(dve):
            dve.sem_inc(y_done, 4)
            dve.sem_inc(rs_done, 1)
            dve.sem_inc(ln_done, 4)
            dve.sem_inc(lg_done, 1)
            for par in range(2):
                dve.sem_inc(acc_out[par], 16)
            dve.memset(eps[:, :], EPS).then_inc(eps_done, 1)
            dve.wait_ge(w_in, 16 * 11)
            with dve.Fori(0, NCH // 2) as i:
                for par in range(2):
                    n = i * 2 + par
                    dve.wait_ge(biased, n + 1)
                    dve.wait_ge(row_done, n + 1)
                    dve.wait_ge(x1_out[par], i * 16 + 16)
                    for pair in range(2):
                        dve.wait_ge(y_mm, n * 2 + pair + 5)
                        dve.tensor_tensor(y[par][:, 2 * pair:2 * pair + 2, :],
                                          ps[:, pair, :].rearrange("p (s n) -> p s n", s=2),
                                          xc[par][:, 2 * pair:2 * pair + 2, :], ALU.add).then_inc(y_done, 1)
                    dve.wait_ge(y_done, n * 2 + 6)
                    for s in range(TPC):
                        dve.bn_stats(stats[:, s, :], y[par][:, s, :]).then_inc(st_done, 1)
                    dve.wait_ge(st_done, n * 4 + 4)
                    dve.sem_inc(hold, 1)
                    for s in range(TPC):
                        dve.bn_aggr(mv[:, s, :], stats[:, s, :]).then_inc(mv_done, 1)
                    dve.wait_ge(sd_done, n + 1)
                    dve.reciprocal(rstd[:, :], sd[:, :]).then_inc(rs_done, 1)
                    dve.wait_ge(rs_done, n + 2)
                    for s in range(TPC):
                        dve.tensor_scalar(y[par][:, s, :], y[par][:, s, :], mv[:, s, 0:1], rstd[:, s:s + 1],
                                          ALU.subtract, ALU.mult).then_inc(ln_done, 1)
                    dve.wait_ge(ln_done, n * 4 + 8)
                    dve.wait_ge(lg_mm, n + 1)
                    dve.tensor_tensor(logits[:, bass.ds(n * TPC, TPC), :],
                                      ps[:, 4, 0:TPC * E].rearrange("p (s e) -> p s e", e=E), rb[:, :, :],
                                      ALU.add).then_inc(lg_done, 1)
            count = [0]

            def link(ins):
                ins.then_inc(step, 1)
                count[0] += 1
                dve.wait_ge(step, count[0])

            def wide(a):
                return a[:, :].rearrange("p (t o) -> p t o", o=1).broadcast_to([P, NT, E])

            dve.wait_ge(lg_done, NCH + 1)
            dve.wait_ge(c_step, 13)
            link(dve.tensor_reduce(top[:, :], logits[:, :, :], AX.X, ALU.max))
            link(dve.tensor_tensor(tmp[:, :, :], logits[:, :, :], wide(top), ALU.subtract))
            dve.wait_ge(exp_done, 1)
            link(dve.tensor_reduce(den[:, :], ex[:, :, :], AX.X, ALU.add))
            link(dve.reciprocal(keep[:, :], den[:, :]))
            link(dve.tensor_tensor(wgt[:, :, :], ex[:, :, :], wide(keep), ALU.mult))
            for k in range(2):
                src = (wgt, left)[k]
                link(dve.tensor_reduce(top[:, :], src[:, :, :], AX.X, ALU.max))
                link(dve.tensor_tensor(tmp[:, :, :], src[:, :, :], wide(top), ALU.is_lt))
                link(dve.scalar_tensor_tensor(out=tmp[:, :, :], in0=tmp[:, :, :], scalar=float(E),
                                              in1=expert_id[:, :, :], op0=ALU.mult, op1=ALU.add))
                link(dve.tensor_reduce(idx[k][:, :], tmp[:, :, :], AX.X, ALU.min))
                link(dve.tensor_tensor(pick[k][:, :, :], expert_id[:, :, :], wide(idx[k]), ALU.is_equal))
                if k == 0:
                    link(dve.scalar_tensor_tensor(out=left[:, :, :], in0=pick[0][:, :, :], scalar=-2.0,
                                                  in1=wgt[:, :, :], op0=ALU.mult, op1=ALU.add))
            link(dve.tensor_tensor(tmp[:, :, :], pick[0][:, :, :], pick[1][:, :, :], ALU.add))
            link(dve.scalar_tensor_tensor(out=mask[:, :, :], in0=wgt[:, :, :], scalar=0.0, in1=tmp[:, :, :],
                                          op0=ALU.is_gt, op1=ALU.mult))
            assert count[0] == 18
            dve.wait_ge(cnt_mm, 2)
            link(dve.tensor_copy(tot[:, :, :], ps[:, 6, 0:NT * E].rearrange("p (a b) -> p a b", b=E)))
            for e in range(E):
                dve.tensor_tensor_scan(scan[:, :, e], scan_ones(ones, NT), tot[:, :, e], 0.0, ALU.mult, ALU.add)\
                   .then_inc(step, 1)
            count[0] += E
            dve.wait_ge(step, count[0])
            link(dve.tensor_tensor(before[:, :, :], scan[:, :, :], tot[:, :, :], ALU.subtract))
            link(dve.tensor_tensor(before[:, :, :], ps[:, 5, 0:NT * E].rearrange("p (a b) -> p a b", b=E),
                                   before[:, :, :], ALU.add))
            link(dve.scalar_tensor_tensor(out=valid[:, :, :], in0=before[:, :, :], scalar=float(CAP),
                                          in1=mask[:, :, :], op0=ALU.is_lt, op1=ALU.mult))
            link(dve.tensor_scalar(of_tile[:, :, :], before[:, :, :], float(P), None, ALU.is_ge))
            for n in range(2, ST):
                link(dve.scalar_tensor_tensor(out=of_tile[:, :, :], in0=before[:, :, :], scalar=float(n * P),
                                              in1=of_tile[:, :, :], op0=ALU.is_ge, op1=ALU.add))
            link(dve.scalar_tensor_tensor(out=in_tile[:, :, :], in0=of_tile[:, :, :], scalar=-float(P),
                                          in1=before[:, :, :], op0=ALU.mult, op1=ALU.add))
            link(dve.tensor_tensor(left[:, :, :], wgt[:, :, :], mask[:, :, :], ALU.mult))
            for n in range(3):
                link(dve.tensor_copy(lot_w[n][:, :, :], left[:, :, :]))
                if n < 2:
                    link(dve.tensor_tensor(left[:, :, :], left[:, :, :], lot_w[n][:, :, :], ALU.subtract))
            for a in range(ST):
                link(dve.scalar_tensor_tensor(out=tmp[:, :, :], in0=of_tile[:, :, :], scalar=float(a),
                                              in1=valid[:, :, :], op0=ALU.is_equal, op1=ALU.mult))
                c = a * LOT
                for what, value in ((LOT_PLACE, wide(place)), (LOT_TILE, wide(tile_id)), (LOT_W, lot_w[0][:, :, :]),
                                    (LOT_W + 1, lot_w[1][:, :, :]), (LOT_W + 2, lot_w[2][:, :, :])):
                    dve.tensor_tensor(lots[:, :, :, c + what], tmp[:, :, :], value, ALU.mult).then_inc(lots_done, 1)
                dve.tensor_copy(lots[:, :, :, c + LOT_TAKEN], tmp[:, :, :]).then_inc(lots_done, 1)
                dve.wait_ge(lots_done, (a + 1) * LOT)
            link(dve.tensor_tensor(keep[:, :], wgt[:, :, EX], mask[:, :, EX], ALU.mult))
            dve.tensor_scalar(keep[:, :], keep[:, :], 1.0, None, ALU.add).then_inc(kept, 1)
            dve.sem_inc(lot_step, 4)
            with dve.Fori(0, EX) as e:
                for n in range(NT):
                    dve.wait_ge(met, e * NT + n + 1)
                    dve.tensor_scalar(hits[n % 4][:, :], columns[:, :],
                                      in_tile[:, n, bass.ds(e, 1)], None, ALU.is_equal).then_inc(hit, 1)
                dve.wait_ge(met, e * NT + NT + 4)
                dve.tensor_copy(lot[:, :, :], ps[:, 7, 0:ST * LOT].rearrange("p (a l) -> p a l", l=LOT))\
                   .then_inc(lot_step, 1)
                dve.wait_ge(lot_step, e * 7 + 5)
                w_row = t["slot_weight"][:, bass.ds(e, 1), :].rearrange("p e a -> p (e a)")
                tok = t["slot_token"][:, bass.ds(e, 1), :].rearrange("p e a -> p (e a)")
                dve.tensor_tensor(lot[:, :, LOT_W], lot[:, :, LOT_W], lot[:, :, LOT_W + 1], ALU.add)\
                   .then_inc(lot_step, 1)
                dve.scalar_tensor_tensor(out=lot[:, :, LOT_PLACE], in0=lot[:, :, LOT_TILE], scalar=float(P),
                                         in1=lot[:, :, LOT_PLACE], op0=ALU.mult, op1=ALU.add).then_inc(lot_step, 1)
                dve.scalar_tensor_tensor(out=free[:, :], in0=lot[:, :, LOT_TAKEN], scalar=-1.0,
                                         in1=t["beyond"][:, :], op0=ALU.add, op1=ALU.mult).then_inc(lot_step, 1)
                dve.wait_ge(lot_step, e * 7 + 8)
                dve.tensor_tensor(w_row, lot[:, :, LOT_W], lot[:, :, LOT_W + 2], ALU.add).then_inc(lot_step, 1)
                dve.tensor_tensor(lot[:, :, LOT_TILE], lot[:, :, LOT_PLACE], free[:, :], ALU.subtract)\
                   .then_inc(lot_step, 1)
                dve.wait_ge(lot_step, e * 7 + 10)
                dve.tensor_copy(tok, lot[:, :, LOT_TILE]).then_inc(lot_step, 1)
                dve.wait_ge(lot_step, e * 7 + 11)
            dve.wait_ge(kept, 1)
            dve.wait_ge(row_done, NCH + 2)
            with dve.Fori(0, NCH // 2) as i:
                for par in range(2):
                    n = i * 2 + par
                    dve.wait_ge(acc_out[par], i * 16 + 16)
                    for s in range(TPC):
                        ins = dve.tensor_scalar(acc[par][:, s, :],
                                                x1[:, bass.ds(n * TPC + s, 1), :].rearrange("p a n -> p (a n)"),
                                                keep[:, bass.ds(n * TPC + s, 1)], None, ALU.mult)
                    ins.then_inc(acc_done, 1)

        @block.gpsimd
        def _(pool):
            pool.sem_inc(row_done, 2)
            prefix_ones(pool, upper, ones, c_step)
            flat = iota_i[:, :, :]
            pool.iota(flat, [[0, NT], [1, E]], base=0, channel_multiplier=0).then_inc(c_step, 1)
            pool.wait_ge(c_step, 4)
            pool.tensor_copy(expert_id[:, :, :], flat).then_inc(c_step, 1)
            def numbers(dst, src, pattern, base, mult, at):
                pool.wait_ge(c_step, at)
                pool.iota(src, pattern, base=base, channel_multiplier=mult).then_inc(c_step, 1)
                pool.wait_ge(c_step, at + 1)
                pool.tensor_copy(dst, src).then_inc(c_step, 1)

            ids = t["token_ids"]
            numbers(tile_id[:, :], ids[:, 0:NT], [[1, NT]], 0, 0, 5)
            numbers(place[:, :], ids[:, 0:NT], [[0, NT]], 0, 1, 7)
            numbers(columns[:, :], ids[:, :], [[1, P]], 0, 0, 9)
            numbers(t["beyond"][:, :], ids[:, 0:ST], [[P, ST]], T, 1, 11)
            pool.wait_ge(w_in, 16 * 11)
            with pool.Fori(0, NCH // 2) as i:
                for par in range(2):
                    n = i * 2 + par
                    pool.wait_ge(xc_in[par], i * 16 + 16)
                    pool.tensor_tensor(xc[par][:, :, :], xc[par][:, :, :], bo[:, :, :], ALU.add).then_inc(biased, 1)
                    pool.wait_ge(ln_done, n * 4 + 8)
                    pool.tensor_copy(x1[:, bass.ds(n * TPC, TPC), :], y[par][:, :, :]).then_inc(row_done, 1)


def scan_ones(ones, n):
    return ones[:, 0:n]


def expert_phase(nc, t, w1_dram, w2_dram, x1_rows, acc_dram, acc_rows, out, ps):
    with ExitStack() as ctx:
        def sb(name, shape, dt):
            return ctx.enter_context(nc.sbuf_tensor(name, shape, dt))

        def sem(name):
            return ctx.enter_context(nc.semaphore(name))

        w1 = [sb(f"w1_{p}", [P, 2, F], F32) for p in range(2)]
        w2 = [sb(f"w2_{p}", [P, F // P, D], F32) for p in range(2)]
        xe = [sb(f"xe{p}", [P, ST, D], F32) for p in range(2)]
        tok = [sb(f"tok{p}", [P, ST], I32) for p in range(2)]
        xeT = sb("xeT", [P, 2, CAP], F32)
        hT = sb("hT", [P, F // P, CAP], F32)
        ye = [sb(f"ye{p}", [P, ST, D], F32) for p in range(2)]
        w_in = [sem(f"ew_in{p}") for p in range(2)]
        xe_in = [sem(f"xe_in{p}") for p in range(2)]
        xT_mm = sem("xeT_mm")
        xT_a = sem("xeT_done")
        up_mm = sem("up_mm")
        h_a = sem("relu_by_act")
        h_v = sem("relu_by_dve")
        dn_mm = sem("down_mm")
        ye_done = sem("ye_done")
        tok_done = sem("tok_done")
        added = sem("added")
        folded = sem("folded")
        hold = sem("expert_hold")
        FT = F // P

        def for_experts(eng, body):
            with eng.Fori(0, EX - 2, 2) as e:
                body(e, 0)
                body(e + 1, 1)
            body(EX - 1, 0)

        with nc.Block() as block:
            @block.sync
            def _(sp):
                def load(e, par):
                    sp.wait_ge(dn_mm, e * ST + ST)
                    one = slice(e, e + 1) if isinstance(e, int) else bass.ds(e, 1)
                    sp.dma_start(w1[par][:, :, :], w1_dram[one, :, :].rearrange("e (k p) n -> p (e k) n", p=P))\
                      .then_inc(w_in[par], 16)
                    sp.dma_start(w2[par][:, :, :], w2_dram[one, :, :].rearrange("e (k p) n -> p (e k) n", p=P))\
                      .then_inc(w_in[par], 16)

                for_experts(sp, load)

            @block.tensor
            def _(pe):
                pe.sem_inc(dn_mm, 2 * ST)

                def expert(e, par):
                    half = (e - par) * 8 + 16
                    pe.wait_ge(xe_in[par], half * ST)
                    for k in range(2):
                        pe.wait_ge(xT_a, e * 2 + k + 1)
                        for s in range(ST):
                            mm = pe.transpose(ps[:, k, s * P:(s + 1) * P], xe[par][:, s, k * P:(k + 1) * P],
                                              t["ident"][:, :])
                        mm.then_inc(xT_mm, 1)
                    pe.wait_ge(xT_a, e * 2 + 4)
                    pe.wait_ge(w_in[par], half * 2)
                    for j in range(FT):
                        pe.wait_ge((h_a, h_v)[j % 2], e * (FT // 2) + j // 2 + 1)
                        for k in range(2):
                            mm = pe.matmul(ps[:, 2 + j % 2, :], w1[par][:, k, j * P:(j + 1) * P], xeT[:, k, :],
                                           start=(k == 0), stop=(k == 1))
                        mm.then_inc(up_mm, 1)
                    pe.wait_ge(h_a, e * (FT // 2) + FT // 2 + 1)
                    pe.wait_ge(h_v, e * (FT // 2) + FT // 2 + 1)
                    for s in range(ST):
                        pe.wait_ge(ye_done, e * ST + s + 5)
                        for j in range(FT):
                            mm = pe.matmul(ps[:, 4 + s, 0:D], hT[:, j, s * P:(s + 1) * P], w2[par][:, j, :],
                                           start=(j == 0), stop=(j == FT - 1))
                        mm.then_inc(dn_mm, 1)

                for_experts(pe, expert)

            @block.scalar
            def _(act):
                act.sem_inc(xT_a, 2)
                act.sem_inc(h_a, 1)

                def expert(e, par):
                    for k in range(2):
                        act.wait_ge(xT_mm, e * 2 + k + 5)
                        act.activation(xeT[:, k, :], ps[:, k, :], ACT.Copy).then_inc(xT_a, 1)
                    act.wait_ge(dn_mm, e * ST + 2 * ST)
                    for j in range(0, FT, 2):
                        act.wait_ge(up_mm, e * FT + j + 1)
                        act.activation(hT[:, j, :], ps[:, 2, :], ACT.Relu).then_inc(h_a, 1)

                for_experts(act, expert)

            @block.vector
            def _(dve):
                dve.sem_inc(h_v, 1)
                dve.sem_inc(ye_done, 2 * ST)
                dve.sem_inc(folded, 2 * ST)

                def expert(e, par):
                    one = slice(e, e + 1) if isinstance(e, int) else bass.ds(e, 1)
                    dve.wait_ge(folded, e * ST + ST)
                    dve.wait_ge(dn_mm, e * ST + 2 * ST)
                    for j in range(1, FT, 2):
                        dve.wait_ge(up_mm, e * FT + j + 1)
                        dve.tensor_scalar(hT[:, j, :], ps[:, 3, :], 0.0, None, ALU.max).then_inc(h_v, 1)
                    for s in range(ST):
                        dve.wait_ge(dn_mm, e * ST + 2 * ST + s + 1)
                        dve.tensor_scalar(ye[par][:, s, :], ps[:, 4 + s, 0:D],
                                          t["slot_weight"][:, one, s:s + 1].rearrange("p e a -> p (e a)"), None,
                                          ALU.mult).then_inc(ye_done, 1)

                for_experts(dve, expert)

            @block.gpsimd
            def _(pool):
                def gather(e, par):
                    one = slice(e, e + 1) if isinstance(e, int) else bass.ds(e, 1)
                    pool.wait_ge(xT_mm, e * 2 + 2)
                    pool.sem_inc(hold, 1)
                    pool.tensor_copy(tok[par][:, :], t["slot_token"][:, one, :].rearrange("p e a -> p (e a)"))\
                        .then_inc(tok_done, 1)
                    pool.wait_ge(tok_done, e + 1)
                    pool.sem_inc(hold, 1)
                    for s in range(ST):
                        pool.indirect_dma_start(out=xe[par][:, s, :], out_offset=None, in_=x1_rows,
                                                in_offset=bass.IndirectOffsetOnAxis(ap=tok[par][:, s:s + 1], axis=0),
                                                bounds_check=T + CAP - 1, oob_is_err=False).then_inc(xe_in[par], 16)

                def add(e, par):
                    for s in range(ST):
                        pool.wait_ge(ye_done, e * ST + 2 * ST + s + 1)
                        pool.sem_inc(hold, 1)
                        pool.indirect_dma_start(out=acc_rows, out_offset=bass.IndirectOffsetOnAxis(
                            ap=tok[par][:, s:s + 1], axis=0), in_=ye[par][:, s, :], in_offset=None,
                            bounds_check=T + CAP - 1, oob_is_err=False, compute_op=ALU.add).then_inc(added, 16)
                        pool.wait_ge(added, e * (16 * ST) + 16 * (s + 1))
                        pool.sem_inc(folded, 1)

                pool.sem_inc(xT_mm, 4)
                gather(0, 0)
                with pool.Fori(0, EX - 2, 2) as e:
                    gather(e + 1, 1)
                    add(e, 0)
                    gather(e + 2, 0)
                    add(e + 1, 1)
                add(EX - 1, 0)
                pool.wait_ge(added, 16 * ST * EX)

        a_in = [sem(f"a_in{p}") for p in range(4)]
        ai = [sb(f"sum{p}", [P, TPC, D], F32) for p in range(4)]
        stats = sb("stats2", [P, TPC, 6], F32)
        mv = sb("mean_var2", [P, TPC, 2], F32)
        sd = sb("std2", [P, TPC], F32)
        rstd = sb("rstd2", [P, TPC], F32)
        eps = sb("eps2", [P, 1], F32)
        eps_done = sem("eps_done2")
        st_done = sem("stats_done2")
        mv_done = sem("mean_var_done2")
        sd_done = sem("std_done2")
        rs_done = sem("rstd_done2")
        ln_done = sem("ln_done2")
        stored = [sem(f"stored{p}") for p in range(4)]
        with nc.Block() as block:
            @block.sync
            def _(sp):
                with sp.Fori(0, NCH // 4) as i:
                    for q in range(4):
                        n = i * 4 + q
                        sp.wait_ge(stored[q], i * 16 + 16)
                        sp.dma_start(ai[q][:, :, :], acc_dram[bass.ds(n * TPC, TPC), :, :].rearrange("t p n -> p t n"))\
                          .then_inc(a_in[q], 16)

            @block.scalar
            def _(act):
                for q in range(4):
                    act.sem_inc(stored[q], 16)
                act.wait_ge(eps_done, 1)
                with act.Fori(0, NCH // 4) as i:
                    for q in range(4):
                        n = i * 4 + q
                        act.wait_ge(mv_done, n * 4 + 4)
                        act.wait_ge(rs_done, n + 1)
                        act.activation(sd[:, :], mv[:, :, 1], ACT.Sqrt, bias=eps[:, 0:1]).then_inc(sd_done, 1)
                        act.wait_ge(ln_done, n * 4 + 4)
                        act.dma_start(out[bass.ds(n * TPC, TPC), :, :].rearrange("t p n -> p t n"), ai[q][:, :, :])\
                           .then_inc(stored[q], 16)
                for q in range(4):
                    act.wait_ge(stored[q], 16 * (NCH // 4) + 16)

            @block.vector
            def _(dve):
                dve.sem_inc(rs_done, 1)
                dve.memset(eps[:, :], EPS).then_inc(eps_done, 1)
                with dve.Fori(0, NCH // 4) as i:
                    for q in range(4):
                        n = i * 4 + q
                        dve.wait_ge(a_in[q], i * 16 + 16)
                        for s in range(TPC):
                            dve.bn_stats(stats[:, s, :], ai[q][:, s, :]).then_inc(st_done, 1)
                        dve.wait_ge(st_done, n * 4 + 4)
                        dve.sem_inc(hold, 1)
                        for s in range(TPC):
                            dve.bn_aggr(mv[:, s, :], stats[:, s, :]).then_inc(mv_done, 1)
                        dve.wait_ge(sd_done, n + 1)
                        dve.reciprocal(rstd[:, :], sd[:, :]).then_inc(rs_done, 1)
                        dve.wait_ge(rs_done, n + 2)
                        for s in range(TPC):
                            dve.tensor_scalar(ai[q][:, s, :], ai[q][:, s, :], mv[:, s, 0:1], rstd[:, s:s + 1],
                                              ALU.subtract, ALU.mult).then_inc(ln_done, 1)


def rows_beyond(nc, t, x1_dram, acc_dram):
    with ExitStack() as ctx:
        blank = ctx.enter_context(nc.sbuf_tensor("blank", [P, ST, D], F32))
        zero = ctx.enter_context(nc.semaphore("blank_zero"))
        stored = ctx.enter_context(nc.semaphore("blank_stored"))
        block = ctx.enter_context(nc.Block())

        @block.vector
        def _(dve):
            dve.memset(blank[:, :, :], 0.0).then_inc(zero, 1)

        @block.sync
        def _(sp):
            sp.wait_ge(zero, 1)
            for rows in (x1_dram, acc_dram):
                sp.dma_start(rows[NT:NT + ST, :, :].rearrange("t p n -> p t n"), blank[:, :, :]).then_inc(stored, 16)
            sp.wait_ge(stored, 32)


def build(nc, x, wqkv, bqkv, wout, bout, router_w, router_b, w1, w2, q_pos, k_pos, slopes, out):
    def dram(name, shape, dt):
        return nc.dram_tensor(name, shape, dt, kind="Internal").ap()

    q_pos, k_pos = q_pos.bitcast(BF16), k_pos.bitcast(BF16)

    parts_dram = dram("qk_parts", (2, H, 3, HD, T), BF16)
    heads_dram = dram("head_outputs", (B, D, L), F32)
    x1 = dram("x1_rows", (T + CAP, D), F32)
    x1_dram = x1.rearrange("(t p) n -> t p n", p=P)
    acc = dram("token_sums", (T + CAP, D), F32)
    acc_dram = acc.rearrange("(t p) n -> t p n", p=P)
    x_t = x.rearrange("b (t p) n -> (b t) p n", p=P)
    out_t = out.rearrange("b (t p) n -> (b t) p n", p=P)
    with ExitStack() as ctx:
        t = {
            "ident": ctx.enter_context(nc.sbuf_tensor("ident", [P, P], F32)),
            "token_ids": ctx.enter_context(nc.sbuf_tensor("token_ids", [P, P], I32)),
            "beyond": ctx.enter_context(nc.sbuf_tensor("beyond", [P, ST], F32)),
            "slot_weight": ctx.enter_context(nc.sbuf_tensor("slot_weight", [P, EX, ST], F32)),
            "slot_token": ctx.enter_context(nc.sbuf_tensor("slot_token", [P, EX, ST], I32)),
            "ident_done": ctx.enter_context(nc.semaphore("ident_done")),
        }
        ps = ctx.enter_context(nc.psum_tensor("ps", [P, 8, 512], F32))
        rows_beyond(nc, t, x1_dram, acc_dram)
        with ExitStack() as v_life:
            t["v"] = v_life.enter_context(nc.sbuf_tensor("v", [P, NT, D], F32))
            project_phase(nc, None, t, x_t, wqkv, bqkv, parts_dram, ps)
            attention_phase(nc, None, t, parts_dram, heads_dram, q_pos, k_pos, slopes, ps)
        route_phase(nc, t, x_t, heads_dram, wout, bout, router_w, router_b, x1_dram, acc_dram, ps)
        expert_phase(nc, t, w1, w2, x1, acc_dram, acc, out_t, ps)


_INS = ["L0_attn_x", "L0_attn_Wqkv", "L0_attn_bqkv", "L0_attn_Wout", "L0_attn_bout",
        "L0_ffn_router_w", "L0_ffn_router_b", "L0_ffn_experts_inter", "L0_ffn_experts_out"]


def bf16_bits(a):
    import numpy as np
    u = np.ascontiguousarray(a, np.float32).view(np.uint32)
    return ((u + 0x7FFF + ((u >> 16) & 1)) >> 16).astype(np.uint16)


def bf16_value(bits):
    import numpy as np
    return (bits.astype(np.uint32) << 16).view(np.float32)


def shape_constants():
    import numpy as np
    start = 2 ** (-2 ** (-(np.log2(H) - 3)))
    slopes = np.asarray([start ** i for i in range(H)], np.float32)
    parts, rest = [], slopes.copy()
    for _ in range(3):
        parts.append(bf16_value(bf16_bits(rest)))
        rest = rest - parts[-1]
    pos = np.arange(L)
    hi, lo = (pos // P) * P, pos % P
    q_pos = np.zeros((H, POS, L), np.float32)
    k_pos = np.zeros((H, 3, POS + 3, L), np.float32)
    for p in range(3):
        for r, (part, of_query) in enumerate([(hi, True), (hi, False), (lo, True), (lo, False)]):
            row = 4 * p + r
            for h in range(H):
                s = float(parts[p][h])
                q_pos[h, row] = part if of_query else s
                for ver, sign in ((RIGHT, -1.0), (LEFT, 1.0)):
                    k_pos[h, ver, row] = sign * s if of_query else -sign * part
    k_pos[:, :, POS:, :] = 1
    minus = np.ascontiguousarray(np.broadcast_to(-slopes[None, :], (P, H)), dtype=np.float32)
    return {"q_pos": bf16_bits(q_pos), "k_pos": bf16_bits(k_pos), "minus_slopes": minus}


def kernel(**inputs):
    import numpy as _np
    import concourse.bacc as _bacc
    from concourse import mybir as _mybir
    from concourse.bass_utils import run_bass_kernel_spmd as _run

    nc = _bacc.Bacc("TRN2", target_bir_lowering=False, num_devices=1)
    arrays, args = {}, []
    given = {n: _np.ascontiguousarray(inputs[n]) for n in _INS}
    given.update(shape_constants())
    for name, a in given.items():
        arrays[f"in_{name}_dram"] = a
        args.append(nc.dram_tensor(f"in_{name}_dram", a.shape, _mybir.dt.from_np(a.dtype), kind="ExternalInput").ap())
    args.append(nc.dram_tensor("out_0_dram", (B, L, D), _mybir.dt.float32, kind="ExternalOutput").ap())
    build(nc, *args)
    r = _run(nc, [arrays], core_ids=[0])
    return r.results[0]["out_0_dram"]
```

```python
import concourse.bass as bass
from concourse import mybir
from contextlib import ExitStack
import math

F32 = mybir.dt.float32
BF16 = mybir.dt.bfloat16
I32 = mybir.dt.int32
ALU = mybir.AluOpType
ACT = mybir.ActivationFunctionType
AX = mybir.AxisListType

B, L, D, H = 2, 2048, 256, 16
HD = D // H
T = B * L
E, EX, F = 8, 7, 1024
CAP = T // E
EPS = 1e-5
P = 128
CH = 512
NCH = T // CH
TPC = CH // P
NT = T // P
KB = L // P
QG = L // CH

PAIRS = 6
Q_PARTS = ((0, 3), (1, 2), (2, 1))
K_PARTS = (3, 2, 1)
ROW_M = PAIRS * HD
ROW_POS = ROW_M + 3
POS = 12
ROWS = ROW_POS + POS
RIGHT, LEFT, DIAG = range(3)

SLOT_BANKS = 3
TILES = KB * QG
CHUNKS = -(-TILES // SLOT_BANKS)
RING = 11
PV_LAG = 5

ST = CAP // P
LOT_PLACE, LOT_TILE, LOT_TAKEN, LOT_W = 0, 1, 2, 3
LOT = 6

LIMIT = 40.0
GONE = 104.0


def slope(h):
    return 2.0 ** (-h / 2)


def reach(h):
    return min(KB, math.ceil((LIMIT + GONE) / slope(h) / P))


FULL_FROM = next(h for h in range(H) if reach(h) >= KB - 1)
LOOPED = FULL_FROM + 1


def band_plan(h):
    chunks, at, width = [[]], 0, SLOT_BANKS * CH
    for kb in range(KB):
        a, end = max(0, kb - reach(h)) * P, min(KB, kb + reach(h) + 1) * P
        while a < end:
            z = min(end, (a // CH + 1) * CH, a + width - at)
            chunks[-1].append((kb, a // CH, a, z, at))
            at += z - a
            a = z
            if at == width:
                chunks.append([])
                at = 0
    return [c for c in chunks if c]


PLANS = [band_plan(h) for h in range(LOOPED + 1)]
BEGIN = [[sum(B * len(p) for p in PLANS[:h]) + b * len(PLANS[h]) for b in range(B)] for h in range(LOOPED + 1)]


def chunk_number(h, like, b):
    return h * (B * CHUNKS) + (BEGIN[like][b] - like * B * CHUNKS)


def item_before(h, like, b):
    return (h, like, 0) if b == 1 else (h - 1, like - 1, 1)


def score_cuts(piece):
    kb, g, a, z, at = piece
    k0 = kb * P
    ends = {a, z} | {c for c in (k0, k0 + P) if a < c < z}
    ends |= {a - at + n * CH for n in range(1, SLOT_BANKS) if a < a - at + n * CH < z}
    ends = sorted(ends)
    return [(LEFT if e <= k0 else RIGHT if s >= k0 + P else DIAG, s, e, at + s - a) for s, e in zip(ends, ends[1:])]


def stack_rows(ver):
    return (RIGHT, ROW_POS) if ver == DIAG else (ver, ROWS)


def chunk_tiles(ch):
    return [(n // QG, n % QG) for n in range(ch * SLOT_BANKS, min((ch + 1) * SLOT_BANKS, TILES))]


def blocks_done(ch):
    return min((ch + 1) * SLOT_BANKS, TILES) // QG if ch >= 0 else 0


def ring_user_before(b, ch):
    if ch >= RING:
        return b, ch - RING
    last = max(c for c in range(CHUNKS) if c % RING == ch % RING)
    return b - 1, last


def project_phase(nc, t, x, wqkv, bqkv, parts_dram, shift_dram, ps):
    with ExitStack() as ctx:
        def sb(name, shape, dt):
            return ctx.enter_context(nc.sbuf_tensor(name, shape, dt))

        def sem(name):
            return ctx.enter_context(nc.semaphore(name))

        xin = [sb(f"xin{p}", [P, TPC, D], F32) for p in range(2)]
        xT = [sb(f"xT{p}", [P, 2, CH], F32) for p in range(2)]
        w = sb("w_qkv", [P, 2, 3 * D], F32)
        bcol = sb("bias_qk_columns", [P, 4], F32)
        bv = sb("bias_v_rows", [P, 2, D], F32)
        split = [sb(f"split{m}", [P, 3, CH], BF16) for m in range(4)]
        rest = [sb(f"rest{m}", [P, CH], F32) for m in range(4)]

        w_in = sem("w_in")
        x_in = [sem(f"x_in{p}") for p in range(2)]
        scaled = sem("scaled")
        xT_mm = sem("xT_mm")
        xT_a = sem("xT_evacuated_by_act")
        xT_v = sem("xT_evacuated_by_dve")
        qk_mm = sem("qk_mm")
        hi_done = sem("hi_part_done")
        rest_done = sem("rest_done")
        mid_done = sem("mid_part_done")
        lo_done = sem("lo_part_done")
        parts_out = [sem(f"parts_out{m}") for m in range(4)]
        v_mm = sem("v_mm")
        v_done = sem("v_done")
        square = [sb(f"square{m}", [P, CH], BF16) for m in range(4)]
        heads_of = sb("heads_of_rows", [P, 2, H], BF16)
        norm_max = sb("norm_max", [H, 2, NCH], F32)
        top_norm = sb("top_norm", [H, 2, B], F32)
        bound = sb("bound", [H, B], F32)
        worst = sb("worst", [H, 1], F32)
        okay = sb("okay", [1, 1], F32)
        shift = sb("shift", [H, B], F32)
        shift_rest = sb("shift_rest", [H, B], F32)
        shift_p = sb("shift_parts", [H, 3, B], BF16)
        shift_w = sb("shift_wide", [H, B, 3, CH], BF16)
        zeros = sb("zeros", [H, CH], BF16)
        of_done = sem("heads_of_done")
        sq_done = sem("square_done")
        n_mm = sem("norm_mm")
        n_done = sem("norm_done")
        b_step = sem("bound_step")
        b_sqrt = sem("bound_sqrt")
        b_T = sem("bound_T")
        shift_done = sem("shift_done")
        shift_out = sem("shift_out")
        hold = sem("project_hold")
        block = ctx.enter_context(nc.Block())


        @block.sync
        def _(sp):
            sp.dma_start(w[:, :, :], wqkv.rearrange("(k p) n -> p k n", p=P)).then_inc(w_in, 16)
            sp.dma_start(bcol[:, :], bqkv[0:2 * D].rearrange("(m p) -> p m", p=P),
                         allow_slow_non_contiguous=True).then_inc(w_in, 16)
            for r in range(2):
                sp.dma_start(bv[:, r, :], bqkv[2 * D:3 * D].rearrange("(a n) -> a n", a=1).broadcast_to([P, D]))\
                  .then_inc(w_in, 16)
            with sp.Fori(0, NCH // 2) as i:
                for par in range(2):
                    for m in range(4):
                        sp.wait_ge(lo_done, i * 8 + par * 4 + m + 5)
                        for part in range(3):
                            sp.dma_start(parts_dram[m // 2, (m % 2) * 8:(m % 2) * 8 + 8, part, :,
                                                    bass.ds((i * 2 + par) * CH, CH)],
                                         split[m][:, part, :]).then_inc(parts_out[m], 16)
            for m in range(4):
                sp.wait_ge(parts_out[m], 48 * (NCH + 1))
            sp.wait_ge(shift_done, 1)
            sp.dma_start(shift_dram.rearrange("b h r n -> h b r n"), shift_w[:, :, :, :]).then_inc(shift_out, 16)
            sp.wait_ge(shift_out, 16)

        @block.tensor
        def _(pe):
            pe.sem_inc(xT_mm, 4)
            pe.sem_inc(v_mm, 4)
            pe.sem_inc(n_mm, 2)
            pe.wait_ge(t["ident_done"], 2)
            pe.wait_ge(of_done, 4)
            pe.wait_ge(scaled, 2)
            with pe.Fori(0, NCH // 2) as i:
                for par in range(2):
                    pe.wait_ge(x_in[par], i * 16 + 16)
                    for k in range(2):
                        pe.wait_ge(n_done, i * 4 + par * 2 + k + 1)
                        for s in range(TPC):
                            mm = pe.transpose(ps[:, k, s * P:(s + 1) * P], xin[par][:, s, k * P:(k + 1) * P],
                                              t["ident"][:, :])
                        mm.then_inc(xT_mm, 1)
                    pe.wait_ge(xT_a, i * 2 + par + 2)
                    pe.wait_ge(xT_v, i * 2 + par + 2)
                    for m in range(4):
                        pe.wait_ge(rest_done, i * 8 + par * 4 + m + 1)
                        for k in range(2):
                            mm = pe.matmul(ps[:, 2 + m, :], w[:, k, m * P:(m + 1) * P], xT[par][:, k, :],
                                           start=(k == 0), stop=(k == 1))
                        mm.then_inc(qk_mm, 1)
                    for pair in range(2):
                        pe.wait_ge(v_done, i * 4 + par * 2 + pair + 1)
                        for s in range(2):
                            tok = (pair * 2 + s) * P
                            for k in range(2):
                                mm = pe.matmul(ps[:, 6 + pair, s * D:(s + 1) * D], xT[par][:, k, tok:tok + P],
                                               w[:, k, 2 * D:3 * D], start=(k == 0), stop=(k == 1))
                        mm.then_inc(v_mm, 1)
                    for side in range(2):
                        for m in range(2):
                            pe.wait_ge(sq_done, i * 8 + par * 4 + side * 2 + m + 5)
                            mm = pe.matmul(ps[0:H, side, :], heads_of[:, m, :], square[side * 2 + m][:, :],
                                           start=(m == 0), stop=(m == 1))
                        mm.then_inc(n_mm, 1)
            pe.wait_ge(b_step, 4)
            pe.transpose(ps[0:1, 0, 0:H], worst[:, :], t["ident"][0:H, 0:H]).then_inc(b_T, 1)

        @block.scalar
        def _(act):
            act.sem_inc(xT_a, 1)
            act.sem_inc(sq_done, 4)

            def hi(i, par, m):
                act.wait_ge(qk_mm, i * 8 + par * 4 + m + 1)
                act.wait_ge(parts_out[m], (i * 2 + par) * 48 + 48)
                act.wait_ge(sq_done, i * 8 + par * 4 + m + 1)
                act.activation(split[m][:, 0, :], ps[:, 2 + m, :], ACT.Identity, bias=bcol[:, m:m + 1])\
                   .then_inc(hi_done, 1)

            def mid(i, par, m):
                act.wait_ge(rest_done, i * 8 + par * 4 + m + 5)
                act.activation(split[m][:, 1, :], rest[m][:, :], ACT.Copy).then_inc(mid_done, 1)

            act.wait_ge(scaled, 2)

            def load_x(c, par, free):
                act.wait_ge(xT_mm, free)
                act.dma_start(xin[par][:, :, :], x[bass.ds(c * TPC, TPC), :, :].rearrange("t p n -> p t n"))\
                   .then_inc(x_in[par], 16)

            with act.Fori(0, NCH // 2) as i:
                for par in range(2):
                    load_x(i * 2 + par, par, i * 4 + par * 2 + 2)
                for par in range(2):
                    act.wait_ge(xT_mm, i * 4 + par * 2 + 5)
                    act.wait_ge(v_mm, i * 4 + par * 2 + 2)
                    act.activation(xT[par][:, 0, :], ps[:, 0, :], ACT.Copy).then_inc(xT_a, 1)
                    hi(i, par, 0)
                    for m in range(1, 4):
                        hi(i, par, m)
                        mid(i, par, m - 1)
                    mid(i, par, 3)
            act.wait_ge(b_step, 2)
            act.activation(bound[:, :], shift_rest[:, :], ACT.Sqrt).then_inc(b_sqrt, 1)

        @block.vector
        def _(dve):
            dve.sem_inc(xT_v, 1)
            dve.sem_inc(rest_done, 4)
            dve.sem_inc(lo_done, 4)
            dve.sem_inc(v_done, 2)
            dve.sem_inc(n_done, 2)
            for m in range(4):
                dve.sem_inc(parts_out[m], 48)
            dve.wait_ge(w_in, 64)
            dve.tensor_scalar(w[:, :, 0:D], w[:, :, 0:D], HD ** -0.5, None, ALU.mult).then_inc(scaled, 1)
            dve.tensor_scalar(bcol[:, 0:2], bcol[:, 0:2], HD ** -0.5, None, ALU.mult).then_inc(scaled, 1)
            dve.wait_ge(scaled, 2)

            def take_rest(i, par, m):
                dve.wait_ge(hi_done, i * 8 + par * 4 + m + 1)
                dve.wait_ge(lo_done, i * 8 + par * 4 + m + 1)
                dve.scalar_tensor_tensor(out=rest[m][:, :], in0=ps[:, 2 + m, :], scalar=bcol[:, m:m + 1],
                                         in1=split[m][:, 0, :], op0=ALU.add, op1=ALU.subtract)\
                   .then_inc(rest_done, 1)

            def lo(i, par, m):
                dve.wait_ge(mid_done, i * 8 + par * 4 + m + 1)
                dve.tensor_tensor(split[m][:, 2, :], rest[m][:, :], split[m][:, 1, :], ALU.subtract)\
                   .then_inc(lo_done, 1)

            with dve.Fori(0, NCH // 2) as i:
                for par in range(2):
                    dve.wait_ge(xT_mm, i * 4 + par * 2 + 6)
                    dve.wait_ge(v_mm, i * 4 + par * 2 + 2)
                    dve.tensor_copy(xT[par][:, 1, :], ps[:, 1, :]).then_inc(xT_v, 1)
                    take_rest(i, par, 0)
                    for m in range(1, 4):
                        take_rest(i, par, m)
                        lo(i, par, m - 1)
                    lo(i, par, 3)
                    for pair in range(2):
                        dve.wait_ge(v_mm, i * 4 + par * 2 + pair + 5)
                        dve.tensor_tensor(t["v"][:, bass.ds((i * 2 + par) * TPC + pair * 2, 2), :],
                                          ps[:, 6 + pair, :].rearrange("p (s n) -> p s n", s=2), bv[:, :, :],
                                          ALU.add).then_inc(v_done, 1)
                    for side in range(2):
                        dve.wait_ge(n_mm, i * 4 + par * 2 + side + 3)
                        dve.tensor_reduce(norm_max[:, side, bass.ds(i * 2 + par, 1)], ps[0:H, side, :], AX.X,
                                          ALU.max).then_inc(n_done, 1)
            dve.wait_ge(n_done, 2 * NCH + 2)
            dve.tensor_reduce(top_norm[:, :, :], norm_max[:, :, :].rearrange("h s (b c) -> h s b c", b=B), AX.X,
                              ALU.max).then_inc(b_step, 1)
            dve.wait_ge(b_step, 1)
            dve.tensor_tensor(shift_rest[:, :], top_norm[:, 0, :], top_norm[:, 1, :], ALU.mult).then_inc(b_step, 1)
            dve.wait_ge(b_sqrt, 1)
            dve.tensor_scalar(shift[:, :], bound[:, :], -1.02, None, ALU.mult).then_inc(b_step, 1)
            dve.wait_ge(b_step, 3)
            dve.tensor_reduce(worst[:, :], shift[:, :], AX.X, ALU.min).then_inc(b_step, 1)
            dve.wait_ge(b_T, 1)
            dve.tensor_reduce(okay[:, :], ps[0:1, 0, 0:H], AX.X, ALU.min).then_inc(b_step, 1)
            dve.wait_ge(b_step, 5)
            dve.tensor_scalar(t["bounded"][:, :], okay[:, :], -LIMIT / 2, None, ALU.is_ge).then_inc(b_step, 1)
            dve.tensor_copy(shift_p[:, 0, :], shift[:, :]).then_inc(b_step, 1)
            dve.wait_ge(b_step, 7)
            dve.tensor_tensor(shift_rest[:, :], shift[:, :], shift_p[:, 0, :], ALU.subtract).then_inc(b_step, 1)
            dve.wait_ge(b_step, 8)
            dve.tensor_copy(shift_p[:, 1, :], shift_rest[:, :]).then_inc(b_step, 1)
            dve.wait_ge(b_step, 9)
            dve.tensor_tensor(shift_p[:, 2, :], shift_rest[:, :], shift_p[:, 1, :], ALU.subtract).then_inc(b_step, 1)
            dve.wait_ge(b_step, 10)
            for b in range(B):
                for part in range(3):
                    ins = dve.tensor_tensor(shift_w[:, b, part, :], zeros[:, :],
                                            shift_p[:, part, b:b + 1].broadcast_to([H, CH]), ALU.add)
            ins.then_inc(shift_done, 1)

        @block.gpsimd
        def _(pool):
            ident, step = t["ident"], t["ident_done"]
            pool.memset(ident[:, :], 0.0).then_inc(step, 1)
            pool.wait_ge(step, 1)
            pool.affine_select(out=ident[:, :], in_=ident[:, :], compare_op=ALU.not_equal, fill=1.0, base=0,
                               pattern=[[-1, P]], channel_multiplier=1).then_inc(step, 1)
            pool.memset(zeros[:, :], 0.0).then_inc(of_done, 1)
            pool.memset(heads_of[:, :, :], 1.0).then_inc(of_done, 1)
            pool.wait_ge(of_done, 2)
            pool.affine_select(out=heads_of[:, :, :], in_=heads_of[:, :, :], compare_op=ALU.is_ge, fill=0.0, base=0,
                               pattern=[[P, 2], [-HD, H]], channel_multiplier=1).then_inc(of_done, 1)
            pool.wait_ge(of_done, 3)
            pool.affine_select(out=heads_of[:, :, :], in_=heads_of[:, :, :], compare_op=ALU.is_ge, fill=0.0,
                               base=HD - 1, pattern=[[-P, 2], [HD, H]], channel_multiplier=-1).then_inc(of_done, 1)
            pool.wait_ge(of_done, 4)
            with pool.Fori(0, NCH // 2) as i:
                for par in range(2):
                    for m in range(4):
                        pool.wait_ge(hi_done, i * 8 + par * 4 + m + 1)
                        pool.sem_inc(hold, 1)
                        pool.wait_ge(n_mm, i * 4 + par * 2 + m // 2 + 1)
                        pool.sem_inc(hold, 1)
                        pool.tensor_tensor(square[m][:, :], split[m][:, 0, :], split[m][:, 0, :], ALU.mult)\
                            .then_inc(sq_done, 1)


def attention_phase(nc, t, parts_dram, shift_dram, heads_dram, q_pos, k_pos, slopes, ps):
    with ExitStack() as ctx:
        def sb(name, shape, dt):
            return ctx.enter_context(nc.sbuf_tensor(name, shape, dt))

        def sem(name):
            return ctx.enter_context(nc.semaphore(name))

        q_st = [sb(f"q_stack{b}", [ROWS, L], BF16) for b in range(B)]
        k_st = [sb(f"k_stack{b}", [ROWS, 2, L], BF16) for b in range(B)]
        prob = sb("prob", [P, RING, SLOT_BANKS * CH], F32)
        vh = [sb(f"v_head{b}", [P, KB, 32], F32) for b in range(B)]
        dist = sb("distance", [P, P], F32)
        nslope = sb("minus_slopes", [P, H], F32)
        near = sb("near_bias", [P, H, P], F32)
        unit_max = sb("unit_max", [P, KB, 2], F32)
        row_max = sb("row_max", [P, KB], F32)
        neg_max = sb("neg_max", [KB, P], F32)
        max_rest = sb("max_rest", [KB, P], F32)
        max_parts = sb("max_parts", [KB, 3, P], BF16)
        o_sb = sb("o_sum", [P, CH], F32)
        o_den = sb("o_den", [P, CH], F32)
        o_rec = sb("o_rec", [P, CH], F32)
        o_out = [sb(f"o_out{b}", [P, CH], F32) for b in range(B)]

        consts_in = sem("attn_consts_in")
        ones_done = sem("ones_done")
        dist_done = sem("dist_done")
        near_done = sem("near_done")
        stack_in = [sem(f"stack_in{b}") for b in range(B)]
        unit_mm = sem("unit_mm")
        unit_bias = sem("unit_bias")
        unit_done = sem("unit_done")
        max_step = sem("max_step")
        max_T = sem("max_T")
        max_ready = sem("max_ready")
        max_in = [sem(f"max_in{b}") for b in range(B)]
        vh_done = sem("vh_done")
        scored = sem("scored")
        expd = sem("expd")
        diag_done = sem("diag_done")
        pv_done = sem("pv_done")
        o_read = sem("o_read")
        o_step = sem("o_step")
        o_ready = sem("o_ready")
        hold = sem("attn_hold")
        o_stored = [sem(f"o_stored{b}") for b in range(B)]

        LOADS = (1 + 3) + (1 + 3)

        with nc.Block() as block:
            @block.sync
            def _(sp):
                sp.dma_start(nslope[:, :], slopes).then_inc(consts_in, 16)

            @block.scalar
            def _(act):
                act.wait_ge(consts_in, 16)
                act.wait_ge(dist_done, 3)
                for h in range(H):
                    act.activation(near[:, h, :], dist[:, :], ACT.Exp, scale=nslope[:, h:h + 1]).then_inc(near_done, 1)

            @block.vector
            def _(dve):
                for b in range(B):
                    dve.memset(vh[b][:, :, HD:32], 1.0).then_inc(ones_done, 1)
                dve.wait_ge(dist_done, 2)
                dve.scalar_tensor_tensor(out=dist[:, :], in0=near[:, 0, :], scalar=-1.0, in1=near[:, 0, :],
                                         op0=ALU.mult, op1=ALU.max).then_inc(dist_done, 1)

            @block.gpsimd
            def _(pool):
                pool.iota(t["token_ids"][:, 0:P], [[1, P]], base=0, channel_multiplier=-1).then_inc(dist_done, 1)
                pool.wait_ge(dist_done, 1)
                pool.tensor_copy(near[:, 0, :], t["token_ids"][:, 0:P]).then_inc(dist_done, 1)

        def load_stacks(sp, h, b, q_row):
            head, cols = bass.ds(h, 1), slice(b * L, (b + 1) * L)
            row = 0
            for part, times in Q_PARTS:
                sp.dma_start(q_st[b][row:row + times * HD, :],
                             parts_dram[0, head, part, :, cols].broadcast_to([times, HD, L])).then_inc(stack_in[b], 16)
                row += times * HD
            sp.dma_start(q_st[b][q_row:ROWS, :], q_pos[head, q_row - ROW_M:, :].rearrange("h r n -> (h r) n"))\
              .then_inc(stack_in[b], 16)
            row = 0
            for parts in K_PARTS:
                rows = parts * HD
                sp.dma_start(k_st[b][row:row + rows, :, :],
                             parts_dram[1, head, 0:parts, :, cols].rearrange("h p d n -> (p d) h n")
                             .broadcast_to([rows, 2, L])).then_inc(stack_in[b], 16)
                row += rows
            sp.dma_start(k_st[b][ROW_M:ROWS, :, :], k_pos[head, :, :, :].rearrange("h v r n -> (h r) v n"))\
              .then_inc(stack_in[b], 16)

        def store_heads(sp, h, b):
            for g in range(QG):
                sp.dma_start(heads_dram[b, bass.ds(h * HD, HD), g * CH:(g + 1) * CH],
                             o_out[b][32 * g:32 * g + HD, :]).then_inc(o_stored[b], 16)

        def divide(dve, item):
            dve.stream_shuffle(o_den[:, :], o_sb[:, :], [HD] * 32).then_inc(o_step, 1)
            dve.wait_ge(o_step, item * 2 + 1)
            dve.reciprocal(o_rec[:, :], o_den[:, :]).then_inc(o_step, 1)
            dve.wait_ge(o_step, item * 2 + 2)


        def banded_sync(sp):
            def item(h, like, b):
                if like > 0:
                    before = item_before(h, like, b)
                    sp.wait_ge(scored, chunk_number(*before))
                load_stacks(sp, h, b, ROW_POS)
                sp.dma_start(q_st[b][ROW_M:ROW_POS, :].rearrange("r (g n) -> r g n", g=QG),
                             shift_dram[b, bass.ds(h, 1), :, :].rearrange("h r n -> r h n")
                             .broadcast_to([3, QG, CH])).then_inc(stack_in[b], 16)
                if like > 0:
                    sp.wait_ge(o_ready, h * 2 + b - 1)
                    store_heads(sp, h - 1, b)

            for h in range(LOOPED):
                for b in range(B):
                    item(h, h, b)
            with sp.Fori(LOOPED, H) as h:
                for b in range(B):
                    item(h, LOOPED, b)
            for b in range(B):
                sp.wait_ge(o_ready, H * 2 + b - 1)
                store_heads(sp, H - 1, b)
            for b in range(B):
                sp.wait_ge(o_stored[b], 64 * H)

        def banded_tensor(pe):
            def score(h, like, b, r):
                number, c = chunk_number(h, like, b) + r, BEGIN[like][b] + r
                if r == 0:
                    pe.wait_ge(stack_in[b], h * (16 * LOADS + 16) + (16 * LOADS + 16))
                if c >= 2:
                    pe.wait_ge(expd, number - 1)
                for piece in PLANS[like][r]:
                    kb = piece[0]
                    for ver, a, z, at in score_cuts(piece):
                        ver, rows = stack_rows(ver)
                        bank, col = divmod(at, CH)
                        mm = pe.matmul(ps[:, SLOT_BANKS * (c % 2) + bank, col:col + z - a],
                                       k_st[b][0:rows, ver, kb * P:(kb + 1) * P], q_st[b][0:rows, a:z],
                                       start=True, stop=True)
                mm.then_inc(scored, 1)

            def pv(h, like, b, r):
                plan = PLANS[like]
                number, c = chunk_number(h, like, b) + r, BEGIN[like][b] + r
                pe.wait_ge(expd, number + 1)
                blocks = sum(DIAG == cut[0] for chunk in plan[:r + 1] for piece in chunk for cut in score_cuts(piece))
                pe.wait_ge(diag_done, h * (2 * KB) + (b * KB + blocks))
                if r == 0:
                    pe.wait_ge(vh_done, h * 2 + b + 1)
                    if like > 0:
                        pe.wait_ge(o_read, h * 2 + b - 1)
                pieces = [(n, piece) for n, chunk in enumerate(plan) for piece in chunk]
                for n, piece in pieces:
                    if n != r:
                        continue
                    kb, g, a, z, at = piece
                    of_group = [p for _, p in pieces if p[1] == g]
                    mm = pe.matmul(ps[32 * g:32 * g + 32, 6 + b, a - g * CH:z - g * CH], vh[b][:, kb, :],
                                   prob[:, c % RING, at:at + z - a], start=(piece is of_group[0]),
                                   stop=(piece is of_group[-1]), skip_group_check=True)
                mm.then_inc(pv_done, 1)

            def item(h, like, b):
                for r in range(len(PLANS[like])):
                    score(h, like, b, r)
                    if r >= PV_LAG:
                        pv(h, like, b, r - PV_LAG)
                    elif like > 0 or b > 0:
                        before = item_before(h, like, b)
                        pv(*before, len(PLANS[before[1]]) + r - PV_LAG)

            for h in range(LOOPED):
                for b in range(B):
                    item(h, h, b)
            with pe.Fori(LOOPED, H) as h:
                for b in range(B):
                    item(h, LOOPED, b)
            for r in range(CHUNKS - PV_LAG, CHUNKS):
                pv(H - 1, LOOPED, 1, r)

        def banded_scalar(act):
            def item(h, like, b):
                for r, chunk in enumerate(PLANS[like]):
                    number, c = chunk_number(h, like, b) + r, BEGIN[like][b] + r
                    act.wait_ge(scored, number + 1)
                    if c >= RING:
                        act.wait_ge(pv_done, number - (RING - 1))
                    width = chunk[-1][4] + chunk[-1][3] - chunk[-1][2]
                    bank = SLOT_BANKS * (c % 2)
                    act.activation(prob[:, c % RING, 0:width],
                                   ps[:, bank:bank + SLOT_BANKS, :].rearrange("p c n -> p (c n)")[:, 0:width],
                                   ACT.Exp).then_inc(expd, 1)

            for h in range(LOOPED):
                for b in range(B):
                    item(h, h, b)
            with act.Fori(LOOPED, H) as h:
                for b in range(B):
                    item(h, LOOPED, b)

        def banded_vector(dve):
            def normalise(h, like, b, end):
                dve.wait_ge(pv_done, end)
                dve.tensor_copy(o_sb[:, :], ps[:, 6 + b, :]).then_inc(o_read, 1)
                dve.wait_ge(o_read, h * 2 + b + 1)
                dve.sem_inc(hold, 1)
                divide(dve, h * 2 + b)
                if like > 0:
                    dve.wait_ge(o_stored[b], h * 64)
                dve.tensor_tensor(o_out[b][:, :], o_sb[:, :], o_rec[:, :], ALU.mult).then_inc(o_ready, 1)
                dve.wait_ge(o_ready, h * 2 + b + 1)

            def item(h, like, b):
                for r, chunk in enumerate(PLANS[like]):
                    number, c = chunk_number(h, like, b) + r, BEGIN[like][b] + r
                    own = [(piece, cut) for piece in chunk for cut in score_cuts(piece) if cut[0] == DIAG]
                    if own:
                        dve.wait_ge(expd, number + 1)
                    for _, (_, a, z, at) in own:
                        here = prob[:, c % RING, at:at + P]
                        dve.tensor_tensor(here, here, near[:, bass.ds(h, 1), :].rearrange("p a n -> p (a n)"),
                                          ALU.mult).then_inc(diag_done, 1)
                    if r == PV_LAG - 1 and (like > 0 or b > 0):
                        normalise(*item_before(h, like, b), chunk_number(h, like, b))

            for h in range(LOOPED):
                for b in range(B):
                    item(h, h, b)
            with dve.Fori(LOOPED, H) as h:
                for b in range(B):
                    item(h, LOOPED, b)
            normalise(H - 1, LOOPED, 1, chunk_number(H, LOOPED, 0))

        def banded_gpsimd(pool):
            def item(h, like, b):
                if like > 0:
                    before = item_before(h, like, b)
                    pool.wait_ge(pv_done, chunk_number(*before))
                pool.tensor_copy(vh[b][:, :, 0:HD], t["v"][:, b * KB:(b + 1) * KB, bass.ds(h * HD, HD)])\
                    .then_inc(vh_done, 1)

            for h in range(LOOPED):
                for b in range(B):
                    item(h, h, b)
            with pool.Fori(LOOPED, H) as h:
                for b in range(B):
                    item(h, LOOPED, b)


        def general_sync(sp):
            with sp.Fori(0, H) as h:
                for b in range(B):
                    sp.wait_ge(scored, h * (2 * CHUNKS) + (b + 1) * CHUNKS)
                    load_stacks(sp, h, b, ROW_M)
                    sp.wait_ge(max_ready, h * 2 + b + 1)
                    for part in range(3):
                        sp.dma_start(q_st[b][ROW_M + part:ROW_M + part + 1, :].rearrange("r (t n) -> r t n", t=KB),
                                     max_parts[:, part, :]).then_inc(max_in[b], 16)
                    sp.wait_ge(o_ready, h * 2 + b + 1)
                    store_heads(sp, h, b)
            for b in range(B):
                sp.wait_ge(o_stored[b], 64 * (H + 1))

        def general_tensor(pe):
            pe.sem_inc(scored, 2 * CHUNKS)
            pe.sem_inc(pv_done, 2 * KB)
            with pe.Fori(0, H) as h:
                for b in range(B):
                    pe.wait_ge(stack_in[b], h * (16 * LOADS) + 16 * LOADS)
                    pe.wait_ge(expd, h * (2 * CHUNKS) + (b + 2) * CHUNKS)
                    for u in range(2 * KB):
                        i, half = divmod(u, 2)
                        if u >= 3:
                            pe.wait_ge(unit_done, h * (4 * KB) + b * 2 * KB + u - 2)
                        for bank in range(2):
                            k0 = half * 1024 + bank * CH
                            cuts = sorted({k0, k0 + CH, *(c for c in (i * P, i * P + P) if k0 < c < k0 + CH)})
                            for a, z in zip(cuts, cuts[1:]):
                                ver = RIGHT if z <= i * P else LEFT if a >= i * P + P else DIAG
                                ver, rows = stack_rows(ver)
                                mm = pe.matmul(ps[:, 2 * (u % 3) + bank, a - k0:z - k0],
                                               q_st[b][0:rows, i * P:(i + 1) * P], k_st[b][0:rows, ver, a:z],
                                               start=True, stop=True)
                        mm.then_inc(unit_mm, 1)
                    pe.wait_ge(max_step, h * 10 + b * 5 + 1)
                    pe.transpose(ps[0:KB, 0, 0:P], row_max[:, :], t["ident"][:, :]).then_inc(max_T, 1)
                    pe.wait_ge(max_in[b], h * 48 + 48)
                    pe.wait_ge(vh_done, h * 2 + b + 3)

                    def score(ch):
                        if ch >= 2:
                            pe.wait_ge(expd, h * (2 * CHUNKS) + (b + 2) * CHUNKS + ch - 1)
                        for n, (kb, g) in enumerate(chunk_tiles(ch)):
                            bank = SLOT_BANKS * (ch % 2) + n
                            q0, k0 = g * CH, kb * P
                            cuts = sorted({q0, q0 + CH, *(c for c in (k0, k0 + P) if q0 < c < q0 + CH)})
                            for a, z in zip(cuts, cuts[1:]):
                                ver = LEFT if z <= k0 else RIGHT if a >= k0 + P else DIAG
                                ver, rows = stack_rows(ver)
                                mm = pe.matmul(ps[:, bank, a - q0:z - q0], k_st[b][0:rows, ver, k0:k0 + P],
                                               q_st[b][0:rows, a:z], start=True, stop=True)
                        mm.then_inc(scored, 1)

                    def pv(kb):
                        if kb == 0:
                            pe.wait_ge(o_read, h * 2 + b + 1)
                        last = (QG * kb + QG - 1) // SLOT_BANKS
                        pe.wait_ge(expd, h * (2 * CHUNKS) + (b + 2) * CHUNKS + last + 1)
                        pe.wait_ge(diag_done, h * (2 * KB) + b * KB + kb + 1)
                        for g in range(QG):
                            n = QG * kb + g
                            ch, c = divmod(n, SLOT_BANKS)
                            mm = pe.matmul(ps[32 * g:32 * g + 32, 6 + b, :], vh[b][:, kb, :],
                                           prob[:, ch % RING, c * CH:(c + 1) * CH],
                                           start=(kb == 0), stop=(kb == KB - 1))
                        mm.then_inc(pv_done, 1)

                    for ch in range(CHUNKS):
                        score(ch)
                        for kb in range(blocks_done(ch - PV_LAG - 1), blocks_done(ch - PV_LAG)):
                            pv(kb)
                    for kb in range(blocks_done(CHUNKS - 1 - PV_LAG), KB):
                        pv(kb)

        def general_scalar(act):
            act.sem_inc(expd, 2 * CHUNKS)
            with act.Fori(0, H) as h:
                for b in range(B):
                    for ch in range(CHUNKS):
                        act.wait_ge(scored, h * (2 * CHUNKS) + (b + 2) * CHUNKS + ch + 1)
                        pb, pch = ring_user_before(b, ch)
                        act.wait_ge(pv_done, h * (2 * KB) + (pb + 2) * KB
                                    + (min(pch * SLOT_BANKS + SLOT_BANKS, TILES) - 1) // QG + 1)
                        n = len(chunk_tiles(ch))
                        bank = SLOT_BANKS * (ch % 2)
                        act.activation(prob[:, ch % RING, 0:n * CH],
                                       ps[:, bank:bank + n, :].rearrange("p c n -> p (c n)"),
                                       ACT.Exp).then_inc(expd, 1)

        def general_vector(dve):
            dve.sem_inc(o_read, 2)
            for b in range(B):
                dve.sem_inc(o_stored[b], 64)
            with dve.Fori(0, H) as h:
                for b in range(B):
                    for u in range(2 * KB):
                        i, half = divmod(u, 2)
                        dve.wait_ge(unit_mm, h * (4 * KB) + b * 2 * KB + u + 1)
                        if i * P // 1024 == half:
                            bank, a = divmod(i * P - half * 1024, CH)
                            here = ps[:, 2 * (u % 3) + bank, a:a + P]
                            dve.scalar_tensor_tensor(out=here, in0=dist[:, :], scalar=nslope[:, bass.ds(h, 1)],
                                                     in1=here, op0=ALU.mult, op1=ALU.add).then_inc(unit_bias, 1)
                            dve.wait_ge(unit_bias, h * (2 * KB) + b * KB + i + 1)
                        dve.tensor_reduce(unit_max[:, i, half:half + 1],
                                          ps[:, 2 * (u % 3):2 * (u % 3) + 2, :].rearrange("p c n -> p (c n)"),
                                          AX.X, ALU.max).then_inc(unit_done, 1)
                    dve.wait_ge(unit_done, h * (4 * KB) + (b + 1) * 2 * KB)
                    step = h * 10 + b * 5
                    dve.tensor_tensor(row_max[:, :], unit_max[:, :, 0], unit_max[:, :, 1], ALU.max)\
                       .then_inc(max_step, 1)
                    dve.wait_ge(max_T, h * 2 + b + 1)
                    dve.tensor_scalar(neg_max[:, :], ps[0:KB, 0, 0:P], -1.0, None, ALU.mult).then_inc(max_step, 1)
                    dve.wait_ge(max_step, step + 2)
                    dve.tensor_copy(max_parts[:, 0, :], neg_max[:, :]).then_inc(max_step, 1)
                    dve.wait_ge(max_step, step + 3)
                    dve.tensor_tensor(max_rest[:, :], neg_max[:, :], max_parts[:, 0, :], ALU.subtract)\
                       .then_inc(max_step, 1)
                    dve.wait_ge(max_step, step + 4)
                    dve.tensor_copy(max_parts[:, 1, :], max_rest[:, :]).then_inc(max_step, 1)
                    dve.wait_ge(max_step, step + 5)
                    dve.tensor_tensor(max_parts[:, 2, :], max_rest[:, :], max_parts[:, 1, :], ALU.subtract)\
                       .then_inc(max_ready, 1)
                    for kb in range(KB):
                        g, off = divmod(kb * P, CH)
                        n = QG * kb + g
                        ch, c = divmod(n, SLOT_BANKS)
                        dve.wait_ge(expd, h * (2 * CHUNKS) + (b + 2) * CHUNKS + ch + 1)
                        here = prob[:, ch % RING, c * CH + off:c * CH + off + P]
                        dve.tensor_tensor(here, here, near[:, bass.ds(h, 1), :].rearrange("p a n -> p (a n)"),
                                          ALU.mult).then_inc(diag_done, 1)
                    dve.wait_ge(pv_done, h * (2 * KB) + (b + 3) * KB)
                    dve.tensor_copy(o_sb[:, :], ps[:, 6 + b, :]).then_inc(o_read, 1)
                    dve.wait_ge(o_read, h * 2 + b + 3)
                    dve.sem_inc(hold, 1)
                    divide(dve, h * 2 + b)
                    dve.wait_ge(o_stored[b], h * 64 + 64)
                    dve.tensor_tensor(o_out[b][:, :], o_sb[:, :], o_rec[:, :], ALU.mult).then_inc(o_ready, 1)
                    dve.wait_ge(o_ready, h * 2 + b + 1)

        def general_gpsimd(pool):
            pool.sem_inc(vh_done, 2)
            with pool.Fori(0, H) as h:
                for b in range(B):
                    pool.wait_ge(pv_done, h * (2 * KB) + (b + 1) * KB)
                    pool.tensor_copy(vh[b][:, :, 0:HD], t["v"][:, b * KB:(b + 1) * KB, bass.ds(h * HD, HD)])\
                        .then_inc(vh_done, 1)

        with nc.Block() as block:
            @block.sync
            def _(sp):
                bounded = sp.value_load(t["bounded"][0:1, 0:1], min_val=0, max_val=1)
                with sp.If(bounded == 1):
                    banded_sync(sp)
                with sp.Else():
                    general_sync(sp)

            @block.tensor
            def _(pe):
                bounded = pe.value_load(t["bounded"][0:1, 0:1], min_val=0, max_val=1)
                with pe.If(bounded == 1):
                    banded_tensor(pe)
                with pe.Else():
                    general_tensor(pe)

            @block.scalar
            def _(act):
                bounded = act.value_load(t["bounded"][0:1, 0:1], min_val=0, max_val=1)
                with act.If(bounded == 1):
                    banded_scalar(act)
                with act.Else():
                    general_scalar(act)

            @block.vector
            def _(dve):
                bounded = dve.value_load(t["bounded"][0:1, 0:1], min_val=0, max_val=1)
                with dve.If(bounded == 1):
                    banded_vector(dve)
                with dve.Else():
                    general_vector(dve)

            @block.gpsimd
            def _(pool):
                bounded = pool.value_load(t["bounded"][0:1, 0:1], min_val=0, max_val=1)
                with pool.If(bounded == 1):
                    banded_gpsimd(pool)
                with pool.Else():
                    general_gpsimd(pool)


def prefix_ones(pool, upper, ones, step):
    pool.memset(ones[:, :], 1.0).then_inc(step, 1)
    pool.memset(upper[:, :], 1.0).then_inc(step, 1)
    pool.wait_ge(step, 2)
    pool.affine_select(out=upper[:, :], in_=upper[:, :], compare_op=ALU.is_gt, fill=0.0, base=0,
                       pattern=[[1, P]], channel_multiplier=-1).then_inc(step, 1)


def route_phase(nc, t, x, heads_dram, wout, bout, router_w, router_b, x1_dram, acc_dram, ps):
    with ExitStack() as ctx:
        def sb(name, shape, dt):
            return ctx.enter_context(nc.sbuf_tensor(name, shape, dt))

        def sem(name):
            return ctx.enter_context(nc.semaphore(name))

        wo = sb("w_out", [P, 2, D], F32)
        bo = sb("b_out", [P, TPC, D], F32)
        rw = sb("router_wT", [P, 2, E], F32)
        rb = sb("router_bias", [P, TPC, E], F32)
        oc = [sb(f"heads_chunk{p}", [P, 2, CH], F32) for p in range(2)]
        xc = [sb(f"x_chunk{p}", [P, TPC, D], F32) for p in range(2)]
        y = [sb(f"y{p}", [P, TPC, D], F32) for p in range(2)]
        x1T = [sb(f"x1T{p}", [P, 2, CH], F32) for p in range(2)]
        stats = sb("stats", [P, TPC, 6], F32)
        mv = sb("mean_var", [P, TPC, 2], F32)
        sd = sb("std", [P, TPC], F32)
        rstd = sb("rstd", [P, TPC], F32)
        eps = sb("eps", [P, 1], F32)
        x1 = sb("x1", [P, NT, D], F32)
        logits = sb("logits", [P, NT, E], F32)
        shape = [P, NT, E]
        ex = sb("ex", shape, F32)
        wgt = sb("weights", shape, F32)
        left = sb("weights_left", shape, F32)
        tmp = sb("tmp", shape, F32)
        pick = [sb(f"pick{k}", shape, F32) for k in range(2)]
        mask = sb("mask", shape, F32)
        before = sb("before", shape, F32)
        valid = sb("valid", shape, F32)
        tot = sb("totals", shape, F32)
        scan = sb("scan", shape, F32)
        expert_id = sb("expert_id", shape, F32)
        top = sb("top", [P, NT], F32)
        den = sb("den", [P, NT], F32)
        idx = [sb(f"choice{k}", [P, NT], F32) for k in range(2)]
        upper = sb("upper", [P, P], F32)
        ones = sb("ones", [P, P], F32)
        iota_i = sb("iota_i", shape, I32)
        tile_id = sb("tile_id", [P, NT], F32)
        place = sb("place", [P, NT], F32)
        in_tile = sb("slot_in_tile", shape, F32)
        of_tile = sb("slot_tile", shape, F32)
        lot_w = [sb(f"lot_w{n}", shape, BF16) for n in range(3)]
        lots = sb("lots", [P, NT, E, ST * LOT], BF16)
        columns = sb("columns", [P, P], F32)
        hits = [sb(f"hits{n}", [P, P], BF16) for n in range(4)]
        lot = sb("lot", [P, ST, LOT], F32)
        free = sb("free", [P, ST], F32)
        acc = [sb(f"acc{p}", [P, TPC, D], F32) for p in range(2)]
        keep = sb("keep", [P, NT], F32)

        w_in = sem("route_w_in")
        hold = sem("route_hold")
        oc_in = [sem(f"oc_in{p}") for p in range(2)]
        xc_in = [sem(f"xc_in{p}") for p in range(2)]
        biased = sem("x_biased")
        y_mm = sem("y_mm")
        y_done = sem("y_done")
        st_done = sem("stats_done")
        mv_done = sem("mean_var_done")
        sd_done = sem("std_done")
        rs_done = sem("rstd_done")
        ln_done = sem("ln_done")
        row_done = sem("row_done")
        x1_mm = sem("x1T_mm")
        x1_done = sem("x1T_done")
        lg_mm = sem("logits_mm")
        lg_done = sem("logits_done")
        step = sem("route_step")
        c_step = sem("route_const_step")
        cnt_mm = sem("counts_mm")
        exp_done = sem("router_exp_done")
        eps_done = sem("eps_done")
        kept = sem("kept")
        lots_done = sem("lots_done")
        hit = sem("hit")
        met = sem("met")
        lot_step = sem("lot_step")
        x1_out = [sem(f"x1_out{p}") for p in range(2)]
        acc_done = sem("acc_done")
        acc_out = [sem(f"acc_out{p}") for p in range(2)]
        block = ctx.enter_context(nc.Block())

        @block.sync
        def _(sp):
            sp.dma_start(wo[:, :, :], wout.rearrange("(k p) n -> p k n", p=P)).then_inc(w_in, 16)
            for s in range(TPC):
                sp.dma_start(bo[:, s, :], bout.rearrange("(a n) -> a n", a=1).broadcast_to([P, D])).then_inc(w_in, 16)
                sp.dma_start(rb[:, s, :], router_b.rearrange("(a n) -> a n", a=1).broadcast_to([P, E])).then_inc(w_in, 16)
            for k in range(2):
                sp.dma_start(rw[:, k, :], router_w[:, k * P:(k + 1) * P].rearrange("e p -> p e"),
                             allow_slow_non_contiguous=True).then_inc(w_in, 16)
            with sp.Fori(0, B) as b:
                for c in range(QG):
                    par = c % 2
                    n = b * QG + c
                    sp.wait_ge(y_mm, n * 2 + 2)
                    sp.dma_start(oc[par][:, :, :],
                                 heads_dram[bass.ds(b, 1), :, c * CH:(c + 1) * CH]
                                 .rearrange("b (k p) n -> p (b k) n", p=P)).then_inc(oc_in[par], 16)
                    sp.wait_ge(y_done, n * 2 + 2)
                    sp.dma_start(xc[par][:, :, :], x[bass.ds(n * TPC, TPC), :, :].rearrange("t p n -> p t n"))\
                      .then_inc(xc_in[par], 16)
            with sp.Fori(0, NCH // 2) as i:
                for par in range(2):
                    sp.wait_ge(acc_done, i * 2 + par + 1)
                    sp.dma_start(acc_dram[bass.ds((i * 2 + par) * TPC, TPC), :, :].rearrange("t p n -> p t n"),
                                 acc[par][:, :, :]).then_inc(acc_out[par], 16)
            for par in range(2):
                sp.wait_ge(acc_out[par], 16 * (NCH // 2) + 16)

        @block.tensor
        def _(pe):
            pe.sem_inc(y_mm, 4)
            pe.wait_ge(w_in, 16 * 11)
            with pe.Fori(0, NCH // 2) as i:
                for par in range(2):
                    n = i * 2 + par
                    pe.wait_ge(oc_in[par], i * 16 + 16)
                    for pair in range(2):
                        pe.wait_ge(y_done, n * 2 + pair + 3)
                        for s in range(2):
                            tok = (pair * 2 + s) * P
                            for k in range(2):
                                mm = pe.matmul(ps[:, pair, s * D:(s + 1) * D], oc[par][:, k, tok:tok + P],
                                               wo[:, k, :], start=(k == 0), stop=(k == 1))
                        mm.then_inc(y_mm, 1)
                    pe.wait_ge(ln_done, n * 4 + 8)
                    for k in range(2):
                        pe.wait_ge(x1_done, n * 2 + k + 1)
                        for s in range(TPC):
                            mm = pe.transpose(ps[:, 2 + k, s * P:(s + 1) * P], y[par][:, s, k * P:(k + 1) * P],
                                              t["ident"][:, :])
                        mm.then_inc(x1_mm, 1)
                    pe.wait_ge(x1_done, n * 2 + 4)
                    pe.wait_ge(lg_done, n + 1)
                    for s in range(TPC):
                        for k in range(2):
                            mm = pe.matmul(ps[:, 4, s * E:(s + 1) * E], x1T[par][:, k, s * P:(s + 1) * P],
                                           rw[:, k, :], start=(k == 0), stop=(k == 1))
                    mm.then_inc(lg_mm, 1)
            pe.wait_ge(step, 18)
            pe.wait_ge(c_step, 3)
            flat = mask[:, :, :].rearrange("p a b -> p (a b)")
            pe.matmul(ps[:, 5, 0:NT * E], upper[:, :], flat, start=True, stop=True).then_inc(cnt_mm, 1)
            pe.matmul(ps[:, 6, 0:NT * E], ones[:, :], flat, start=True, stop=True).then_inc(cnt_mm, 1)
            pe.sem_inc(met, 4)
            pe.wait_ge(lots_done, ST * LOT)
            with pe.Fori(0, EX) as e:
                pe.wait_ge(lot_step, e * 7 + 4)
                for n in range(NT):
                    pe.wait_ge(hit, e * NT + n + 1)
                    pe.matmul(ps[:, 7, 0:ST * LOT], hits[n % 4][:, :],
                              lots[:, n, bass.ds(e, 1), :].rearrange("p e l -> p (e l)"),
                              start=(n == 0), stop=(n == NT - 1)).then_inc(met, 1)

        @block.scalar
        def _(act):
            for par in range(2):
                act.sem_inc(x1_out[par], 16)
            act.sem_inc(x1_done, 2)
            act.wait_ge(eps_done, 1)
            with act.Fori(0, NCH // 2) as i:
                for par in range(2):
                    n = i * 2 + par
                    act.wait_ge(mv_done, n * 4 + 4)
                    act.wait_ge(rs_done, n + 1)
                    act.activation(sd[:, :], mv[:, :, 1], ACT.Sqrt, bias=eps[:, 0:1]).then_inc(sd_done, 1)
                    for k in range(2):
                        act.wait_ge(x1_mm, n * 2 + k + 1)
                        act.activation(x1T[par][:, k, :], ps[:, 2 + k, :], ACT.Copy).then_inc(x1_done, 1)
                    act.wait_ge(ln_done, n * 4 + 8)
                    act.dma_start(x1_dram[bass.ds(n * TPC, TPC), :, :].rearrange("t p n -> p t n"), y[par][:, :, :])\
                       .then_inc(x1_out[par], 16)
            for par in range(2):
                act.wait_ge(x1_out[par], 16 * (NCH // 2) + 16)
            act.wait_ge(step, 2)
            act.activation(ex[:, :, :], tmp[:, :, :], ACT.Exp).then_inc(exp_done, 1)

        @block.vector
        def _(dve):
            dve.sem_inc(y_done, 4)
            dve.sem_inc(rs_done, 1)
            dve.sem_inc(ln_done, 4)
            dve.sem_inc(lg_done, 1)
            for par in range(2):
                dve.sem_inc(acc_out[par], 16)
            dve.memset(eps[:, :], EPS).then_inc(eps_done, 1)
            dve.wait_ge(w_in, 16 * 11)
            with dve.Fori(0, NCH // 2) as i:
                for par in range(2):
                    n = i * 2 + par
                    dve.wait_ge(biased, n + 1)
                    dve.wait_ge(row_done, n + 1)
                    dve.wait_ge(x1_out[par], i * 16 + 16)
                    for pair in range(2):
                        dve.wait_ge(y_mm, n * 2 + pair + 5)
                        dve.tensor_tensor(y[par][:, 2 * pair:2 * pair + 2, :],
                                          ps[:, pair, :].rearrange("p (s n) -> p s n", s=2),
                                          xc[par][:, 2 * pair:2 * pair + 2, :], ALU.add).then_inc(y_done, 1)
                    dve.wait_ge(y_done, n * 2 + 6)
                    for s in range(TPC):
                        dve.bn_stats(stats[:, s, :], y[par][:, s, :]).then_inc(st_done, 1)
                    dve.wait_ge(st_done, n * 4 + 4)
                    dve.sem_inc(hold, 1)
                    for s in range(TPC):
                        dve.bn_aggr(mv[:, s, :], stats[:, s, :]).then_inc(mv_done, 1)
                    dve.wait_ge(sd_done, n + 1)
                    dve.reciprocal(rstd[:, :], sd[:, :]).then_inc(rs_done, 1)
                    dve.wait_ge(rs_done, n + 2)
                    for s in range(TPC):
                        dve.tensor_scalar(y[par][:, s, :], y[par][:, s, :], mv[:, s, 0:1], rstd[:, s:s + 1],
                                          ALU.subtract, ALU.mult).then_inc(ln_done, 1)
                    dve.wait_ge(ln_done, n * 4 + 8)
                    dve.wait_ge(lg_mm, n + 1)
                    dve.tensor_tensor(logits[:, bass.ds(n * TPC, TPC), :],
                                      ps[:, 4, 0:TPC * E].rearrange("p (s e) -> p s e", e=E), rb[:, :, :],
                                      ALU.add).then_inc(lg_done, 1)
            count = [0]

            def link(ins):
                ins.then_inc(step, 1)
                count[0] += 1
                dve.wait_ge(step, count[0])

            def wide(a):
                return a[:, :].rearrange("p (t o) -> p t o", o=1).broadcast_to([P, NT, E])

            dve.wait_ge(lg_done, NCH + 1)
            dve.wait_ge(c_step, 13)
            link(dve.tensor_reduce(top[:, :], logits[:, :, :], AX.X, ALU.max))
            link(dve.tensor_tensor(tmp[:, :, :], logits[:, :, :], wide(top), ALU.subtract))
            dve.wait_ge(exp_done, 1)
            link(dve.tensor_reduce(den[:, :], ex[:, :, :], AX.X, ALU.add))
            link(dve.reciprocal(keep[:, :], den[:, :]))
            link(dve.tensor_tensor(wgt[:, :, :], ex[:, :, :], wide(keep), ALU.mult))
            for k in range(2):
                src = (wgt, left)[k]
                link(dve.tensor_reduce(top[:, :], src[:, :, :], AX.X, ALU.max))
                link(dve.tensor_tensor(tmp[:, :, :], src[:, :, :], wide(top), ALU.is_lt))
                link(dve.scalar_tensor_tensor(out=tmp[:, :, :], in0=tmp[:, :, :], scalar=float(E),
                                              in1=expert_id[:, :, :], op0=ALU.mult, op1=ALU.add))
                link(dve.tensor_reduce(idx[k][:, :], tmp[:, :, :], AX.X, ALU.min))
                link(dve.tensor_tensor(pick[k][:, :, :], expert_id[:, :, :], wide(idx[k]), ALU.is_equal))
                if k == 0:
                    link(dve.scalar_tensor_tensor(out=left[:, :, :], in0=pick[0][:, :, :], scalar=-2.0,
                                                  in1=wgt[:, :, :], op0=ALU.mult, op1=ALU.add))
            link(dve.tensor_tensor(tmp[:, :, :], pick[0][:, :, :], pick[1][:, :, :], ALU.add))
            link(dve.scalar_tensor_tensor(out=mask[:, :, :], in0=wgt[:, :, :], scalar=0.0, in1=tmp[:, :, :],
                                          op0=ALU.is_gt, op1=ALU.mult))
            assert count[0] == 18
            dve.wait_ge(cnt_mm, 2)
            link(dve.tensor_copy(tot[:, :, :], ps[:, 6, 0:NT * E].rearrange("p (a b) -> p a b", b=E)))
            for e in range(E):
                dve.tensor_tensor_scan(scan[:, :, e], scan_ones(ones, NT), tot[:, :, e], 0.0, ALU.mult, ALU.add)\
                   .then_inc(step, 1)
            count[0] += E
            dve.wait_ge(step, count[0])
            link(dve.tensor_tensor(before[:, :, :], scan[:, :, :], tot[:, :, :], ALU.subtract))
            link(dve.tensor_tensor(before[:, :, :], ps[:, 5, 0:NT * E].rearrange("p (a b) -> p a b", b=E),
                                   before[:, :, :], ALU.add))
            link(dve.scalar_tensor_tensor(out=valid[:, :, :], in0=before[:, :, :], scalar=float(CAP),
                                          in1=mask[:, :, :], op0=ALU.is_lt, op1=ALU.mult))
            link(dve.tensor_scalar(of_tile[:, :, :], before[:, :, :], float(P), None, ALU.is_ge))
            for n in range(2, ST):
                link(dve.scalar_tensor_tensor(out=of_tile[:, :, :], in0=before[:, :, :], scalar=float(n * P),
                                              in1=of_tile[:, :, :], op0=ALU.is_ge, op1=ALU.add))
            link(dve.scalar_tensor_tensor(out=in_tile[:, :, :], in0=of_tile[:, :, :], scalar=-float(P),
                                          in1=before[:, :, :], op0=ALU.mult, op1=ALU.add))
            link(dve.tensor_tensor(left[:, :, :], wgt[:, :, :], mask[:, :, :], ALU.mult))
            for n in range(3):
                link(dve.tensor_copy(lot_w[n][:, :, :], left[:, :, :]))
                if n < 2:
                    link(dve.tensor_tensor(left[:, :, :], left[:, :, :], lot_w[n][:, :, :], ALU.subtract))
            for a in range(ST):
                link(dve.scalar_tensor_tensor(out=tmp[:, :, :], in0=of_tile[:, :, :], scalar=float(a),
                                              in1=valid[:, :, :], op0=ALU.is_equal, op1=ALU.mult))
                c = a * LOT
                for what, value in ((LOT_PLACE, wide(place)), (LOT_TILE, wide(tile_id)), (LOT_W, lot_w[0][:, :, :]),
                                    (LOT_W + 1, lot_w[1][:, :, :]), (LOT_W + 2, lot_w[2][:, :, :])):
                    dve.tensor_tensor(lots[:, :, :, c + what], tmp[:, :, :], value, ALU.mult).then_inc(lots_done, 1)
                dve.tensor_copy(lots[:, :, :, c + LOT_TAKEN], tmp[:, :, :]).then_inc(lots_done, 1)
                dve.wait_ge(lots_done, (a + 1) * LOT)
            link(dve.tensor_tensor(keep[:, :], wgt[:, :, EX], mask[:, :, EX], ALU.mult))
            dve.tensor_scalar(keep[:, :], keep[:, :], 1.0, None, ALU.add).then_inc(kept, 1)
            dve.sem_inc(lot_step, 4)
            with dve.Fori(0, EX) as e:
                for n in range(NT):
                    dve.wait_ge(met, e * NT + n + 1)
                    dve.tensor_scalar(hits[n % 4][:, :], columns[:, :],
                                      in_tile[:, n, bass.ds(e, 1)], None, ALU.is_equal).then_inc(hit, 1)
                dve.wait_ge(met, e * NT + NT + 4)
                dve.tensor_copy(lot[:, :, :], ps[:, 7, 0:ST * LOT].rearrange("p (a l) -> p a l", l=LOT))\
                   .then_inc(lot_step, 1)
                dve.wait_ge(lot_step, e * 7 + 5)
                w_row = t["slot_weight"][:, bass.ds(e, 1), :].rearrange("p e a -> p (e a)")
                tok = t["slot_token"][:, bass.ds(e, 1), :].rearrange("p e a -> p (e a)")
                dve.tensor_tensor(lot[:, :, LOT_W], lot[:, :, LOT_W], lot[:, :, LOT_W + 1], ALU.add)\
                   .then_inc(lot_step, 1)
                dve.scalar_tensor_tensor(out=lot[:, :, LOT_PLACE], in0=lot[:, :, LOT_TILE], scalar=float(P),
                                         in1=lot[:, :, LOT_PLACE], op0=ALU.mult, op1=ALU.add).then_inc(lot_step, 1)
                dve.scalar_tensor_tensor(out=free[:, :], in0=lot[:, :, LOT_TAKEN], scalar=-1.0,
                                         in1=t["beyond"][:, :], op0=ALU.add, op1=ALU.mult).then_inc(lot_step, 1)
                dve.wait_ge(lot_step, e * 7 + 8)
                dve.tensor_tensor(w_row, lot[:, :, LOT_W], lot[:, :, LOT_W + 2], ALU.add).then_inc(lot_step, 1)
                dve.tensor_tensor(lot[:, :, LOT_TILE], lot[:, :, LOT_PLACE], free[:, :], ALU.subtract)\
                   .then_inc(lot_step, 1)
                dve.wait_ge(lot_step, e * 7 + 10)
                dve.tensor_copy(tok, lot[:, :, LOT_TILE]).then_inc(lot_step, 1)
                dve.wait_ge(lot_step, e * 7 + 11)
            dve.wait_ge(kept, 1)
            dve.wait_ge(row_done, NCH + 2)
            with dve.Fori(0, NCH // 2) as i:
                for par in range(2):
                    n = i * 2 + par
                    dve.wait_ge(acc_out[par], i * 16 + 16)
                    for s in range(TPC):
                        ins = dve.tensor_scalar(acc[par][:, s, :],
                                                x1[:, bass.ds(n * TPC + s, 1), :].rearrange("p a n -> p (a n)"),
                                                keep[:, bass.ds(n * TPC + s, 1)], None, ALU.mult)
                    ins.then_inc(acc_done, 1)

        @block.gpsimd
        def _(pool):
            pool.sem_inc(row_done, 2)
            prefix_ones(pool, upper, ones, c_step)
            flat = iota_i[:, :, :]
            pool.iota(flat, [[0, NT], [1, E]], base=0, channel_multiplier=0).then_inc(c_step, 1)
            pool.wait_ge(c_step, 4)
            pool.tensor_copy(expert_id[:, :, :], flat).then_inc(c_step, 1)
            def numbers(dst, src, pattern, base, mult, at):
                pool.wait_ge(c_step, at)
                pool.iota(src, pattern, base=base, channel_multiplier=mult).then_inc(c_step, 1)
                pool.wait_ge(c_step, at + 1)
                pool.tensor_copy(dst, src).then_inc(c_step, 1)

            ids = t["token_ids"]
            numbers(tile_id[:, :], ids[:, 0:NT], [[1, NT]], 0, 0, 5)
            numbers(place[:, :], ids[:, 0:NT], [[0, NT]], 0, 1, 7)
            numbers(columns[:, :], ids[:, :], [[1, P]], 0, 0, 9)
            numbers(t["beyond"][:, :], ids[:, 0:ST], [[P, ST]], T, 1, 11)
            pool.wait_ge(w_in, 16 * 11)
            with pool.Fori(0, NCH // 2) as i:
                for par in range(2):
                    n = i * 2 + par
                    pool.wait_ge(xc_in[par], i * 16 + 16)
                    pool.tensor_tensor(xc[par][:, :, :], xc[par][:, :, :], bo[:, :, :], ALU.add).then_inc(biased, 1)
                    pool.wait_ge(ln_done, n * 4 + 8)
                    pool.tensor_copy(x1[:, bass.ds(n * TPC, TPC), :], y[par][:, :, :]).then_inc(row_done, 1)


def scan_ones(ones, n):
    return ones[:, 0:n]


def expert_phase(nc, t, w1_dram, w2_dram, x1_rows, acc_dram, acc_rows, out, ps):
    with ExitStack() as ctx:
        def sb(name, shape, dt):
            return ctx.enter_context(nc.sbuf_tensor(name, shape, dt))

        def sem(name):
            return ctx.enter_context(nc.semaphore(name))

        w1 = [sb(f"w1_{p}", [P, 2, F], F32) for p in range(2)]
        w2 = [sb(f"w2_{p}", [P, F // P, D], F32) for p in range(2)]
        xe = [sb(f"xe{p}", [P, ST, D], F32) for p in range(2)]
        tok = [sb(f"tok{p}", [P, ST], I32) for p in range(2)]
        xeT = sb("xeT", [P, 2, CAP], F32)
        hT = sb("hT", [P, F // P, CAP], F32)
        ye = [sb(f"ye{p}", [P, ST, D], F32) for p in range(2)]
        w_in = [sem(f"ew_in{p}") for p in range(2)]
        xe_in = [sem(f"xe_in{p}") for p in range(2)]
        xT_mm = sem("xeT_mm")
        xT_a = sem("xeT_done")
        up_mm = sem("up_mm")
        h_a = sem("relu_by_act")
        h_v = sem("relu_by_dve")
        dn_mm = sem("down_mm")
        ye_done = sem("ye_done")
        tok_done = sem("tok_done")
        added = sem("added")
        folded = sem("folded")
        hold = sem("expert_hold")
        FT = F // P

        def for_experts(eng, body):
            with eng.Fori(0, EX - 2, 2) as e:
                body(e, 0)
                body(e + 1, 1)
            body(EX - 1, 0)

        with nc.Block() as block:
            @block.sync
            def _(sp):
                def load(e, par):
                    sp.wait_ge(dn_mm, e * ST + ST)
                    one = slice(e, e + 1) if isinstance(e, int) else bass.ds(e, 1)
                    sp.dma_start(w1[par][:, :, :], w1_dram[one, :, :].rearrange("e (k p) n -> p (e k) n", p=P))\
                      .then_inc(w_in[par], 16)
                    sp.dma_start(w2[par][:, :, :], w2_dram[one, :, :].rearrange("e (k p) n -> p (e k) n", p=P))\
                      .then_inc(w_in[par], 16)

                for_experts(sp, load)

            @block.tensor
            def _(pe):
                pe.sem_inc(dn_mm, 2 * ST)

                def expert(e, par):
                    half = (e - par) * 8 + 16
                    pe.wait_ge(xe_in[par], half * ST)
                    for k in range(2):
                        pe.wait_ge(xT_a, e * 2 + k + 1)
                        for s in range(ST):
                            mm = pe.transpose(ps[:, k, s * P:(s + 1) * P], xe[par][:, s, k * P:(k + 1) * P],
                                              t["ident"][:, :])
                        mm.then_inc(xT_mm, 1)
                    pe.wait_ge(xT_a, e * 2 + 4)
                    pe.wait_ge(w_in[par], half * 2)
                    for j in range(FT):
                        pe.wait_ge((h_a, h_v)[j % 2], e * (FT // 2) + j // 2 + 1)
                        for k in range(2):
                            mm = pe.matmul(ps[:, 2 + j % 2, :], w1[par][:, k, j * P:(j + 1) * P], xeT[:, k, :],
                                           start=(k == 0), stop=(k == 1))
                        mm.then_inc(up_mm, 1)
                    pe.wait_ge(h_a, e * (FT // 2) + FT // 2 + 1)
                    pe.wait_ge(h_v, e * (FT // 2) + FT // 2 + 1)
                    for s in range(ST):
                        pe.wait_ge(ye_done, e * ST + s + 5)
                        for j in range(FT):
                            mm = pe.matmul(ps[:, 4 + s, 0:D], hT[:, j, s * P:(s + 1) * P], w2[par][:, j, :],
                                           start=(j == 0), stop=(j == FT - 1))
                        mm.then_inc(dn_mm, 1)

                for_experts(pe, expert)

            @block.scalar
            def _(act):
                act.sem_inc(xT_a, 2)
                act.sem_inc(h_a, 1)

                def expert(e, par):
                    for k in range(2):
                        act.wait_ge(xT_mm, e * 2 + k + 5)
                        act.activation(xeT[:, k, :], ps[:, k, :], ACT.Copy).then_inc(xT_a, 1)
                    act.wait_ge(dn_mm, e * ST + 2 * ST)
                    for j in range(0, FT, 2):
                        act.wait_ge(up_mm, e * FT + j + 1)
                        act.activation(hT[:, j, :], ps[:, 2, :], ACT.Relu).then_inc(h_a, 1)

                for_experts(act, expert)

            @block.vector
            def _(dve):
                dve.sem_inc(h_v, 1)
                dve.sem_inc(ye_done, 2 * ST)
                dve.sem_inc(folded, 2 * ST)

                def expert(e, par):
                    one = slice(e, e + 1) if isinstance(e, int) else bass.ds(e, 1)
                    dve.wait_ge(folded, e * ST + ST)
                    dve.wait_ge(dn_mm, e * ST + 2 * ST)
                    for j in range(1, FT, 2):
                        dve.wait_ge(up_mm, e * FT + j + 1)
                        dve.tensor_scalar(hT[:, j, :], ps[:, 3, :], 0.0, None, ALU.max).then_inc(h_v, 1)
                    for s in range(ST):
                        dve.wait_ge(dn_mm, e * ST + 2 * ST + s + 1)
                        dve.tensor_scalar(ye[par][:, s, :], ps[:, 4 + s, 0:D],
                                          t["slot_weight"][:, one, s:s + 1].rearrange("p e a -> p (e a)"), None,
                                          ALU.mult).then_inc(ye_done, 1)

                for_experts(dve, expert)

            @block.gpsimd
            def _(pool):
                def gather(e, par):
                    one = slice(e, e + 1) if isinstance(e, int) else bass.ds(e, 1)
                    pool.wait_ge(xT_mm, e * 2 + 2)
                    pool.sem_inc(hold, 1)
                    pool.tensor_copy(tok[par][:, :], t["slot_token"][:, one, :].rearrange("p e a -> p (e a)"))\
                        .then_inc(tok_done, 1)
                    pool.wait_ge(tok_done, e + 1)
                    pool.sem_inc(hold, 1)
                    for s in range(ST):
                        pool.indirect_dma_start(out=xe[par][:, s, :], out_offset=None, in_=x1_rows,
                                                in_offset=bass.IndirectOffsetOnAxis(ap=tok[par][:, s:s + 1], axis=0),
                                                bounds_check=T + CAP - 1, oob_is_err=False).then_inc(xe_in[par], 16)

                def add(e, par):
                    for s in range(ST):
                        pool.wait_ge(ye_done, e * ST + 2 * ST + s + 1)
                        pool.sem_inc(hold, 1)
                        pool.indirect_dma_start(out=acc_rows, out_offset=bass.IndirectOffsetOnAxis(
                            ap=tok[par][:, s:s + 1], axis=0), in_=ye[par][:, s, :], in_offset=None,
                            bounds_check=T + CAP - 1, oob_is_err=False, compute_op=ALU.add).then_inc(added, 16)
                        pool.wait_ge(added, e * (16 * ST) + 16 * (s + 1))
                        pool.sem_inc(folded, 1)

                pool.sem_inc(xT_mm, 4)
                gather(0, 0)
                with pool.Fori(0, EX - 2, 2) as e:
                    gather(e + 1, 1)
                    add(e, 0)
                    gather(e + 2, 0)
                    add(e + 1, 1)
                add(EX - 1, 0)
                pool.wait_ge(added, 16 * ST * EX)

        a_in = [sem(f"a_in{p}") for p in range(4)]
        ai = [sb(f"sum{p}", [P, TPC, D], F32) for p in range(4)]
        stats = sb("stats2", [P, TPC, 6], F32)
        mv = sb("mean_var2", [P, TPC, 2], F32)
        sd = sb("std2", [P, TPC], F32)
        rstd = sb("rstd2", [P, TPC], F32)
        eps = sb("eps2", [P, 1], F32)
        eps_done = sem("eps_done2")
        st_done = sem("stats_done2")
        mv_done = sem("mean_var_done2")
        sd_done = sem("std_done2")
        rs_done = sem("rstd_done2")
        ln_done = sem("ln_done2")
        stored = [sem(f"stored{p}") for p in range(4)]
        with nc.Block() as block:
            @block.sync
            def _(sp):
                with sp.Fori(0, NCH // 4) as i:
                    for q in range(4):
                        n = i * 4 + q
                        sp.wait_ge(stored[q], i * 16 + 16)
                        sp.dma_start(ai[q][:, :, :], acc_dram[bass.ds(n * TPC, TPC), :, :].rearrange("t p n -> p t n"))\
                          .then_inc(a_in[q], 16)

            @block.scalar
            def _(act):
                for q in range(4):
                    act.sem_inc(stored[q], 16)
                act.wait_ge(eps_done, 1)
                with act.Fori(0, NCH // 4) as i:
                    for q in range(4):
                        n = i * 4 + q
                        act.wait_ge(mv_done, n * 4 + 4)
                        act.wait_ge(rs_done, n + 1)
                        act.activation(sd[:, :], mv[:, :, 1], ACT.Sqrt, bias=eps[:, 0:1]).then_inc(sd_done, 1)
                        act.wait_ge(ln_done, n * 4 + 4)
                        act.dma_start(out[bass.ds(n * TPC, TPC), :, :].rearrange("t p n -> p t n"), ai[q][:, :, :])\
                           .then_inc(stored[q], 16)
                for q in range(4):
                    act.wait_ge(stored[q], 16 * (NCH // 4) + 16)

            @block.vector
            def _(dve):
                dve.sem_inc(rs_done, 1)
                dve.memset(eps[:, :], EPS).then_inc(eps_done, 1)
                with dve.Fori(0, NCH // 4) as i:
                    for q in range(4):
                        n = i * 4 + q
                        dve.wait_ge(a_in[q], i * 16 + 16)
                        for s in range(TPC):
                            dve.bn_stats(stats[:, s, :], ai[q][:, s, :]).then_inc(st_done, 1)
                        dve.wait_ge(st_done, n * 4 + 4)
                        dve.sem_inc(hold, 1)
                        for s in range(TPC):
                            dve.bn_aggr(mv[:, s, :], stats[:, s, :]).then_inc(mv_done, 1)
                        dve.wait_ge(sd_done, n + 1)
                        dve.reciprocal(rstd[:, :], sd[:, :]).then_inc(rs_done, 1)
                        dve.wait_ge(rs_done, n + 2)
                        for s in range(TPC):
                            dve.tensor_scalar(ai[q][:, s, :], ai[q][:, s, :], mv[:, s, 0:1], rstd[:, s:s + 1],
                                              ALU.subtract, ALU.mult).then_inc(ln_done, 1)


def rows_beyond(nc, t, x1_dram, acc_dram):
    with ExitStack() as ctx:
        blank = ctx.enter_context(nc.sbuf_tensor("blank", [P, ST, D], F32))
        zero = ctx.enter_context(nc.semaphore("blank_zero"))
        stored = ctx.enter_context(nc.semaphore("blank_stored"))
        block = ctx.enter_context(nc.Block())

        @block.vector
        def _(dve):
            dve.memset(blank[:, :, :], 0.0).then_inc(zero, 1)

        @block.sync
        def _(sp):
            sp.wait_ge(zero, 1)
            for rows in (x1_dram, acc_dram):
                sp.dma_start(rows[NT:NT + ST, :, :].rearrange("t p n -> p t n"), blank[:, :, :]).then_inc(stored, 16)
            sp.wait_ge(stored, 32)


def build(nc, x, wqkv, bqkv, wout, bout, router_w, router_b, w1, w2, q_pos, k_pos, slopes, out):
    def dram(name, shape, dt):
        return nc.dram_tensor(name, shape, dt, kind="Internal").ap()

    q_pos, k_pos = q_pos.bitcast(BF16), k_pos.bitcast(BF16)

    parts_dram = dram("qk_parts", (2, H, 3, HD, T), BF16)
    shift_dram = dram("shift_rows", (B, H, 3, CH), BF16)
    heads_dram = dram("head_outputs", (B, D, L), F32)
    x1 = dram("x1_rows", (T + CAP, D), F32)
    x1_dram = x1.rearrange("(t p) n -> t p n", p=P)
    acc = dram("token_sums", (T + CAP, D), F32)
    acc_dram = acc.rearrange("(t p) n -> t p n", p=P)
    x_t = x.rearrange("b (t p) n -> (b t) p n", p=P)
    out_t = out.rearrange("b (t p) n -> (b t) p n", p=P)
    with ExitStack() as ctx:
        t = {
            "bounded": ctx.enter_context(nc.sbuf_tensor("bounded", [1, 1], I32)),
            "ident": ctx.enter_context(nc.sbuf_tensor("ident", [P, P], F32)),
            "token_ids": ctx.enter_context(nc.sbuf_tensor("token_ids", [P, P], I32)),
            "beyond": ctx.enter_context(nc.sbuf_tensor("beyond", [P, ST], F32)),
            "slot_weight": ctx.enter_context(nc.sbuf_tensor("slot_weight", [P, EX, ST], F32)),
            "slot_token": ctx.enter_context(nc.sbuf_tensor("slot_token", [P, EX, ST], I32)),
            "ident_done": ctx.enter_context(nc.semaphore("ident_done")),
        }
        ps = ctx.enter_context(nc.psum_tensor("ps", [P, 8, 512], F32))
        rows_beyond(nc, t, x1_dram, acc_dram)
        with ExitStack() as v_life:
            t["v"] = v_life.enter_context(nc.sbuf_tensor("v", [P, NT, D], F32))
            project_phase(nc, t, x_t, wqkv, bqkv, parts_dram, shift_dram, ps)
            attention_phase(nc, t, parts_dram, shift_dram, heads_dram, q_pos, k_pos, slopes, ps)
        route_phase(nc, t, x_t, heads_dram, wout, bout, router_w, router_b, x1_dram, acc_dram, ps)
        expert_phase(nc, t, w1, w2, x1, acc_dram, acc, out_t, ps)


_INS = ["L0_attn_x", "L0_attn_Wqkv", "L0_attn_bqkv", "L0_attn_Wout", "L0_attn_bout",
        "L0_ffn_router_w", "L0_ffn_router_b", "L0_ffn_experts_inter", "L0_ffn_experts_out"]


def bf16_bits(a):
    import numpy as np
    u = np.ascontiguousarray(a, np.float32).view(np.uint32)
    return ((u + 0x7FFF + ((u >> 16) & 1)) >> 16).astype(np.uint16)


def bf16_value(bits):
    import numpy as np
    return (bits.astype(np.uint32) << 16).view(np.float32)


def shape_constants():
    import numpy as np
    start = 2 ** (-2 ** (-(np.log2(H) - 3)))
    slopes = np.asarray([start ** i for i in range(H)], np.float32)
    parts, rest = [], slopes.copy()
    for _ in range(3):
        parts.append(bf16_value(bf16_bits(rest)))
        rest = rest - parts[-1]
    pos = np.arange(L)
    hi, lo = (pos // P) * P, pos % P
    q_pos = np.zeros((H, 3 + POS, L), np.float32)
    k_pos = np.zeros((H, 2, 3 + POS, L), np.float32)
    for p in range(3):
        for r, (part, of_query) in enumerate([(hi, True), (hi, False), (lo, True), (lo, False)]):
            row = 3 + 4 * p + r
            for h in range(H):
                s = float(parts[p][h])
                q_pos[h, row] = part if of_query else s
                for ver, sign in ((RIGHT, -1.0), (LEFT, 1.0)):
                    k_pos[h, ver, row] = sign * s if of_query else -sign * part
    k_pos[:, :, 0:3, :] = 1
    minus = np.ascontiguousarray(np.broadcast_to(-slopes[None, :], (P, H)), dtype=np.float32)
    return {"q_pos": bf16_bits(q_pos), "k_pos": bf16_bits(k_pos), "minus_slopes": minus}


def kernel(**inputs):
    import numpy as _np
    import concourse.bacc as _bacc
    from concourse import mybir as _mybir
    from concourse.bass_utils import run_bass_kernel_spmd as _run

    nc = _bacc.Bacc("TRN2", target_bir_lowering=False, num_devices=1)
    arrays, args = {}, []
    given = {n: _np.ascontiguousarray(inputs[n]) for n in _INS}
    given.update(shape_constants())
    for name, a in given.items():
        arrays[f"in_{name}_dram"] = a
        args.append(nc.dram_tensor(f"in_{name}_dram", a.shape, _mybir.dt.from_np(a.dtype), kind="ExternalInput").ap())
    args.append(nc.dram_tensor("out_0_dram", (B, L, D), _mybir.dt.float32, kind="ExternalOutput").ap())
    build(nc, *args)
    r = _run(nc, [arrays], core_ids=[0])
    return r.results[0]["out_0_dram"]
```

```python
import concourse.bass as bass
from concourse import mybir
from contextlib import ExitStack
import math

F32 = mybir.dt.float32
BF16 = mybir.dt.bfloat16
I32 = mybir.dt.int32
ALU = mybir.AluOpType
ACT = mybir.ActivationFunctionType
AX = mybir.AxisListType

B, L, D, H = 2, 2048, 256, 16
HD = D // H
T = B * L
E, EX, F = 8, 7, 1024
CAP = T // E
EPS = 1e-5
P = 128
CH = 512
NCH = T // CH
TPC = CH // P
NT = T // P
KB = L // P
QG = L // CH

PAIRS = 6
Q_PARTS = ((0, 3), (1, 2), (2, 1))
K_PARTS = (3, 2, 1)
ROW_M = PAIRS * HD
ROW_POS = ROW_M + 3
POS = 12
ROWS = ROW_POS + POS
RIGHT, LEFT, DIAG = range(3)

SLOT_BANKS = 3
TILES = KB * QG
CHUNKS = -(-TILES // SLOT_BANKS)
RING = 11
PV_LAG = 5

ST = CAP // P
LOT_PLACE, LOT_TILE, LOT_TAKEN, LOT_W = 0, 1, 2, 3
LOT = 6
HIT_TILES = 8
HIT_SLOTS = 4
POOL_TILES = 1

LIMIT = 32.0
GONE = 104.0


def slope(h):
    return 2.0 ** (-h / 2)


def reach(h):
    return math.ceil((LIMIT + GONE) / slope(h) / 16) * 16


FULL_FROM = next(h for h in range(H) if reach(h) >= L - P)
LOOPED = FULL_FROM + 1


ORDER = [g * (KB // QG) + n for n in range(KB // QG) for g in range(QG)]


def band_plan(h):
    chunks, at, width = [[]], 0, SLOT_BANKS * CH
    for kb in ORDER:
        k0 = kb * P
        a, end = max(0, k0 - reach(h)), min(L, k0 + P + reach(h))
        while a < end:
            z = min(end, (a // CH + 1) * CH, a + width - at)
            if k0 < z < k0 + P:
                z = k0
            if z > a:
                chunks[-1].append((kb, a // CH, a, z, at))
            at += z - a
            if z == k0 and a + width - (at - (z - a)) < k0 + P or at == width:
                chunks.append([])
                at = 0
            a = z
    return [c for c in chunks if c]


def by_turns(chunk):
    turn = lambda n: sum(p[1] == chunk[n][1] for p in chunk[:n])
    return [chunk[n] for n in sorted(range(len(chunk)), key=lambda n: (turn(n), chunk[n][1]))]


def own_column(piece):
    kb, g, a, z, at = piece
    return at + kb * P - a if a <= kb * P < z else None


PLANS = [band_plan(h) for h in range(LOOPED + 1)]
BEGIN = [[sum(B * len(p) for p in PLANS[:h]) + b * len(PLANS[h]) for b in range(B)] for h in range(LOOPED + 1)]


def chunk_number(h, like, b):
    return h * (B * CHUNKS) + (BEGIN[like][b] - like * B * CHUNKS)


def item_before(h, like, b):
    return (h, like, 0) if b == 1 else (h - 1, like - 1, 1)


def score_cuts(piece):
    kb, g, a, z, at = piece
    k0 = kb * P
    ends = {a, z} | {c for c in (k0, k0 + P) if a < c < z}
    ends |= {a - at + n * CH for n in range(1, SLOT_BANKS) if a < a - at + n * CH < z}
    ends = sorted(ends)
    return [(LEFT if e <= k0 else RIGHT if s >= k0 + P else DIAG, s, e, at + s - a) for s, e in zip(ends, ends[1:])]


def stack_rows(ver):
    return (RIGHT, ROW_POS) if ver == DIAG else (ver, ROWS)


def chunk_tiles(ch):
    return [(n // QG, n % QG) for n in range(ch * SLOT_BANKS, min((ch + 1) * SLOT_BANKS, TILES))]


def blocks_done(ch):
    return min((ch + 1) * SLOT_BANKS, TILES) // QG if ch >= 0 else 0


def ring_user_before(b, ch):
    if ch >= RING:
        return b, ch - RING
    last = max(c for c in range(CHUNKS) if c % RING == ch % RING)
    return b - 1, last


def load_route_weights(sp, t, wout, bout, router_w, router_b):
    def load(dst, src, **kind):
        sp.dma_start(dst, src, **kind).then_inc(t["route_w_in"], 16)

    load(t["w_out"][:, :, :], wout.rearrange("(k p) n -> p k n", p=P))
    for s in range(TPC):
        load(t["b_out"][:, s, :], bout.rearrange("(a n) -> a n", a=1).broadcast_to([P, D]))
        load(t["router_bias"][:, s, :], router_b.rearrange("(a n) -> a n", a=1).broadcast_to([P, E]))
    for k in range(2):
        load(t["router_wT"][:, k, :], router_w[:, k * P:(k + 1) * P].rearrange("e p -> p e"),
             allow_slow_non_contiguous=True)


def load_expert(sp, t, w1_dram, w2_dram, e, par):
    one = slice(e, e + 1) if isinstance(e, int) else bass.ds(e, 1)
    sp.dma_start(t["w1"][par][:, :, :], w1_dram[one, :, :].rearrange("e (k p) n -> p (e k) n", p=P))\
      .then_inc(t["expert_w_in"][par], 16)
    sp.dma_start(t["w2"][par][:, :, :], w2_dram[one, :, :].rearrange("e (k p) n -> p (e k) n", p=P))\
      .then_inc(t["expert_w_in"][par], 16)


def project_phase(nc, t, x, wqkv, bqkv, wout, bout, router_w, router_b, slopes, parts_dram, shift_dram,
                  x1_dram, acc_dram, ps):
    with ExitStack() as ctx:
        def sb(name, shape, dt):
            return ctx.enter_context(nc.sbuf_tensor(name, shape, dt))

        def sem(name):
            return ctx.enter_context(nc.semaphore(name))

        xin = [sb(f"xin{p}", [P, TPC, D], F32) for p in range(2)]
        xT = [sb(f"xT{p}", [P, 2, CH], F32) for p in range(2)]
        w = sb("w_qkv", [P, 2, 3 * D], F32)
        bcol = sb("bias_qk_columns", [P, 4], F32)
        bv = sb("bias_v_rows", [P, 2, D], F32)
        split = [sb(f"split{m}", [P, 3, CH], BF16) for m in range(4)]
        rest = [sb(f"rest{m}", [P, CH], F32) for m in range(4)]

        w_in = sem("w_in")
        x_in = [sem(f"x_in{p}") for p in range(2)]
        scaled = sem("scaled")
        xT_mm = sem("xT_mm")
        xT_a = sem("xT_evacuated_by_act")
        xT_v = sem("xT_evacuated_by_dve")
        qk_mm = sem("qk_mm")
        hi_done = sem("hi_part_done")
        rest_done = sem("rest_done")
        mid_done = sem("mid_part_done")
        lo_done = sem("lo_part_done")
        parts_out = [sem(f"parts_out{m}") for m in range(4)]
        v_mm = sem("v_mm")
        v_done = sem("v_done")
        square = [sb(f"square{m}", [P, CH], BF16) for m in range(4)]
        heads_of = sb("heads_of_rows", [P, 2, H], BF16)
        norm_max = sb("norm_max", [H, 2, NCH], F32)
        top_norm = sb("top_norm", [H, 2, B], F32)
        bound = sb("bound", [H, B], F32)
        worst = sb("worst", [H, 1], F32)
        okay = sb("okay", [1, 1], F32)
        shift = sb("shift", [H, B], F32)
        shift_rest = sb("shift_rest", [H, B], F32)
        shift_p = sb("shift_parts", [H, 3, B], BF16)
        shift_w = sb("shift_wide", [H, B, 3, CH], BF16)
        zeros = sb("zeros", [H, CH], BF16)
        of_done = sem("heads_of_done")
        sq_done = sem("square_done")
        n_mm = sem("norm_mm")
        n_done = sem("norm_done")
        b_step = sem("bound_step")
        b_sqrt = sem("bound_sqrt")
        b_T = sem("bound_T")
        shift_done = sem("shift_done")
        shift_out = sem("shift_out")
        hold = sem("project_hold")
        dist, nslope, near = t["distance"], t["minus_slopes"], t["near_bias"]
        slopes_in = sem("slopes_in")
        blank = sb("blank", [P, ST, D], F32)
        blank_done = sem("blank_done")
        blank_out = sem("blank_out")
        dist_done = sem("dist_done")
        block = ctx.enter_context(nc.Block())


        @block.sync
        def _(sp):
            sp.dma_start(nslope[:, :], slopes).then_inc(slopes_in, 16)
            sp.dma_start(w[:, :, :], wqkv.rearrange("(k p) n -> p k n", p=P)).then_inc(w_in, 16)
            sp.dma_start(bcol[:, :], bqkv[0:2 * D].rearrange("(m p) -> p m", p=P),
                         allow_slow_non_contiguous=True).then_inc(w_in, 16)
            for r in range(2):
                sp.dma_start(bv[:, r, :], bqkv[2 * D:3 * D].rearrange("(a n) -> a n", a=1).broadcast_to([P, D]))\
                  .then_inc(w_in, 16)
            sp.wait_ge(blank_done, 1)
            for rows in (x1_dram, acc_dram):
                sp.dma_start(rows[NT:NT + ST, :, :].rearrange("t p n -> p t n"), blank[:, :, :]).then_inc(blank_out, 16)
            load_route_weights(sp, t, wout, bout, router_w, router_b)
            with sp.Fori(0, NCH // 2) as i:
                for par in range(2):
                    for m in range(4):
                        sp.wait_ge(lo_done, i * 8 + par * 4 + m + 5)
                        for part in range(3):
                            sp.dma_start(parts_dram[m // 2, (m % 2) * 8:(m % 2) * 8 + 8, part, :,
                                                    bass.ds((i * 2 + par) * CH, CH)],
                                         split[m][:, part, :]).then_inc(parts_out[m], 16)
            for m in range(4):
                sp.wait_ge(parts_out[m], 48 * (NCH + 1))
            sp.wait_ge(shift_done, 1)
            sp.dma_start(shift_dram.rearrange("b h r n -> h b r n"), shift_w[:, :, :, :]).then_inc(shift_out, 16)
            sp.wait_ge(shift_out, 16)
            sp.wait_ge(blank_out, 32)

        @block.tensor
        def _(pe):
            pe.sem_inc(xT_mm, 4)
            pe.sem_inc(v_mm, 4)
            pe.sem_inc(n_mm, 2)
            pe.wait_ge(t["ident_done"], 2)
            pe.wait_ge(of_done, 4)
            pe.wait_ge(scaled, 2)
            def transposes(i, par):
                pe.wait_ge(x_in[par], i * 16 + 16)
                for k in range(2):
                    for s in range(TPC):
                        mm = pe.transpose(ps[:, k, s * P:(s + 1) * P], xin[par][:, s, k * P:(k + 1) * P],
                                          t["ident"][:, :])
                    mm.then_inc(xT_mm, 1)

            def qk(i, par):
                pe.wait_ge(xT_a, i * 2 + par + 2)
                pe.wait_ge(xT_v, i * 2 + par + 2)
                for m in range(4):
                    pe.wait_ge(rest_done, i * 8 + par * 4 + m + 1)
                    if m >= 2:
                        pe.wait_ge(n_done, i * 4 + par * 2 + m - 1)
                    for k in range(2):
                        mm = pe.matmul(ps[:, 2 + m, :], w[:, k, m * P:(m + 1) * P], xT[par][:, k, :],
                                       start=(k == 0), stop=(k == 1))
                    mm.then_inc(qk_mm, 1)

            def v_product(i, par):
                for pair in range(2):
                    pe.wait_ge(v_done, i * 4 + par * 2 + pair + 1)
                    for s in range(2):
                        tok = (pair * 2 + s) * P
                        for k in range(2):
                            mm = pe.matmul(ps[:, 6 + pair, s * D:(s + 1) * D], xT[par][:, k, tok:tok + P],
                                           w[:, k, 2 * D:3 * D], start=(k == 0), stop=(k == 1))
                    mm.then_inc(v_mm, 1)

            def norms(i, par):
                for side in range(2):
                    pe.wait_ge(rest_done, i * 8 + par * 4 + side + 7)
                    for m in range(2):
                        pe.wait_ge(sq_done, i * 8 + par * 4 + side * 2 + m + 5)
                        mm = pe.matmul(ps[0:H, 4 + side, :], heads_of[:, m, :], square[side * 2 + m][:, :],
                                       start=(m == 0), stop=(m == 1))
                    mm.then_inc(n_mm, 1)

            transposes(0, 0)
            with pe.Fori(0, NCH // 2 - 1) as i:
                for par in range(2):
                    qk(i, par)
                    v_product(i, par)
                    transposes(i + par, 1 - par)
                    norms(i, par)
            last = NCH // 2 - 1
            qk(last, 0)
            v_product(last, 0)
            transposes(last, 1)
            norms(last, 0)
            qk(last, 1)
            v_product(last, 1)
            norms(last, 1)
            pe.wait_ge(b_step, 4)
            pe.transpose(ps[0:1, 0, 0:H], worst[:, :], t["ident"][0:H, 0:H]).then_inc(b_T, 1)

        @block.scalar
        def _(act):
            act.sem_inc(xT_a, 1)
            act.sem_inc(sq_done, 4)

            def hi(i, par, m):
                act.wait_ge(qk_mm, i * 8 + par * 4 + m + 1)
                act.wait_ge(parts_out[m], (i * 2 + par) * 48 + 48)
                act.wait_ge(sq_done, i * 8 + par * 4 + m + 1)
                act.activation(split[m][:, 0, :], ps[:, 2 + m, :], ACT.Identity, bias=bcol[:, m:m + 1])\
                   .then_inc(hi_done, 1)

            def mid(i, par, m):
                act.wait_ge(rest_done, i * 8 + par * 4 + m + 5)
                act.activation(split[m][:, 1, :], rest[m][:, :], ACT.Copy).then_inc(mid_done, 1)

            def load_x(c, par):
                act.dma_start(xin[par][:, :, :], x[bass.ds(c * TPC, TPC), :, :].rearrange("t p n -> p t n"))\
                   .then_inc(x_in[par], 16)

            def chunk(i, par, more):
                act.wait_ge(xT_mm, i * 4 + par * 2 + 5)
                act.wait_ge(v_mm, i * 4 + par * 2 + 2)
                act.activation(xT[par][:, 0, :], ps[:, 0, :], ACT.Copy).then_inc(xT_a, 1)
                hi(i, par, 0)
                if more:
                    act.wait_ge(xT_mm, i * 4 + par * 2 + 6)
                    load_x(i * 2 + (par + 2), par)
                for m in range(1, 4):
                    hi(i, par, m)
                    mid(i, par, m - 1)
                mid(i, par, 3)

            for par in range(2):
                load_x(par, par)
            act.wait_ge(slopes_in, 16)
            act.wait_ge(dist_done, 3)
            for h in range(H):
                act.activation(near[:, h, :], dist[:, :], ACT.Exp, scale=nslope[:, h:h + 1])
            act.wait_ge(scaled, 2)
            with act.Fori(0, NCH // 2 - 1) as i:
                for par in range(2):
                    chunk(i, par, True)
            for par in range(2):
                chunk(NCH // 2 - 1, par, False)
            act.wait_ge(b_step, 2)
            act.activation(bound[:, :], shift_rest[:, :], ACT.Sqrt).then_inc(b_sqrt, 1)

        @block.vector
        def _(dve):
            dve.sem_inc(xT_v, 1)
            dve.sem_inc(rest_done, 4)
            dve.sem_inc(lo_done, 4)
            dve.sem_inc(v_done, 2)
            dve.sem_inc(n_done, 2)
            for m in range(4):
                dve.sem_inc(parts_out[m], 48)
            for b in range(B):
                dve.memset(t["v_heads"][b][:, :, HD:32], 1.0)
            dve.memset(blank[:, :, :], 0.0).then_inc(blank_done, 1)
            dve.wait_ge(dist_done, 2)
            dve.scalar_tensor_tensor(out=dist[:, :], in0=near[:, 0, :], scalar=-1.0, in1=near[:, 0, :],
                                     op0=ALU.mult, op1=ALU.max).then_inc(dist_done, 1)
            dve.wait_ge(w_in, 64)
            dve.tensor_scalar(w[:, :, 0:D], w[:, :, 0:D], HD ** -0.5, None, ALU.mult).then_inc(scaled, 1)
            dve.tensor_scalar(bcol[:, 0:2], bcol[:, 0:2], HD ** -0.5, None, ALU.mult).then_inc(scaled, 1)
            dve.wait_ge(scaled, 2)

            def take_rest(i, par, m):
                dve.wait_ge(hi_done, i * 8 + par * 4 + m + 1)
                dve.wait_ge(lo_done, i * 8 + par * 4 + m + 1)
                dve.scalar_tensor_tensor(out=rest[m][:, :], in0=ps[:, 2 + m, :], scalar=bcol[:, m:m + 1],
                                         in1=split[m][:, 0, :], op0=ALU.add, op1=ALU.subtract)\
                   .then_inc(rest_done, 1)

            def lo(i, par, m):
                dve.wait_ge(mid_done, i * 8 + par * 4 + m + 1)
                dve.tensor_tensor(split[m][:, 2, :], rest[m][:, :], split[m][:, 1, :], ALU.subtract)\
                   .then_inc(lo_done, 1)

            def evacuate(i, par):
                dve.wait_ge(xT_mm, i * 4 + par * 2 + 6)
                dve.wait_ge(v_mm, i * 4 + par * 2 + 2)
                dve.tensor_copy(xT[par][:, 1, :], ps[:, 1, :]).then_inc(xT_v, 1)

            def parts_and_v(i, par):
                take_rest(i, par, 0)
                for m in range(1, 4):
                    take_rest(i, par, m)
                    lo(i, par, m - 1)
                lo(i, par, 3)
                for pair in range(2):
                    dve.wait_ge(v_mm, i * 4 + par * 2 + pair + 5)
                    dve.tensor_tensor(t["v"][:, bass.ds((i * 2 + par) * TPC + pair * 2, 2), :],
                                      ps[:, 6 + pair, :].rearrange("p (s n) -> p s n", s=2), bv[:, :, :],
                                      ALU.add).then_inc(v_done, 1)

            def top_norms(n):
                for side in range(2):
                    dve.wait_ge(n_mm, n * 2 + side + 3)
                    dve.tensor_reduce(norm_max[:, side, bass.ds(n, 1)], ps[0:H, 4 + side, :], AX.X,
                                      ALU.max).then_inc(n_done, 1)

            evacuate(0, 0)
            parts_and_v(0, 0)
            evacuate(0, 1)
            top_norms(0)
            parts_and_v(0, 1)
            with dve.Fori(1, NCH // 2) as i:
                for par in range(2):
                    evacuate(i, par)
                    top_norms(i * 2 + (par - 1))
                    parts_and_v(i, par)
            top_norms(NCH - 1)
            dve.wait_ge(n_done, 2 * NCH + 2)
            dve.tensor_reduce(top_norm[:, :, :], norm_max[:, :, :].rearrange("h s (b c) -> h s b c", b=B), AX.X,
                              ALU.max).then_inc(b_step, 1)
            dve.wait_ge(b_step, 1)
            dve.tensor_tensor(shift_rest[:, :], top_norm[:, 0, :], top_norm[:, 1, :], ALU.mult).then_inc(b_step, 1)
            dve.wait_ge(b_sqrt, 1)
            dve.tensor_scalar(shift[:, :], bound[:, :], -1.02, None, ALU.mult).then_inc(b_step, 1)
            dve.wait_ge(b_step, 3)
            dve.tensor_reduce(worst[:, :], shift[:, :], AX.X, ALU.min).then_inc(b_step, 1)
            dve.wait_ge(b_T, 1)
            dve.tensor_reduce(okay[:, :], ps[0:1, 0, 0:H], AX.X, ALU.min).then_inc(b_step, 1)
            dve.wait_ge(b_step, 5)
            dve.tensor_scalar(t["bounded"][:, :], okay[:, :], -LIMIT / 2, None, ALU.is_ge).then_inc(b_step, 1)
            dve.tensor_copy(shift_p[:, 0, :], shift[:, :]).then_inc(b_step, 1)
            dve.wait_ge(b_step, 7)
            dve.tensor_tensor(shift_rest[:, :], shift[:, :], shift_p[:, 0, :], ALU.subtract).then_inc(b_step, 1)
            dve.wait_ge(b_step, 8)
            dve.tensor_copy(shift_p[:, 1, :], shift_rest[:, :]).then_inc(b_step, 1)
            dve.wait_ge(b_step, 9)
            dve.tensor_tensor(shift_p[:, 2, :], shift_rest[:, :], shift_p[:, 1, :], ALU.subtract).then_inc(b_step, 1)
            dve.wait_ge(b_step, 10)
            for b in range(B):
                for part in range(3):
                    ins = dve.tensor_tensor(shift_w[:, b, part, :], zeros[:, :],
                                            shift_p[:, part, b:b + 1].broadcast_to([H, CH]), ALU.add)
            ins.then_inc(shift_done, 1)

        @block.gpsimd
        def _(pool):
            ident, step = t["ident"], t["ident_done"]
            pool.memset(ident[:, :], 0.0).then_inc(step, 1)
            pool.wait_ge(step, 1)
            pool.affine_select(out=ident[:, :], in_=ident[:, :], compare_op=ALU.not_equal, fill=1.0, base=0,
                               pattern=[[-1, P]], channel_multiplier=1).then_inc(step, 1)
            pool.iota(t["token_ids"][:, 0:P], [[1, P]], base=0, channel_multiplier=-1).then_inc(dist_done, 1)
            pool.wait_ge(dist_done, 1)
            pool.tensor_copy(near[:, 0, :], t["token_ids"][:, 0:P]).then_inc(dist_done, 1)
            pool.memset(zeros[:, :], 0.0).then_inc(of_done, 1)
            pool.memset(heads_of[:, :, :], 1.0).then_inc(of_done, 1)
            pool.wait_ge(of_done, 2)
            pool.affine_select(out=heads_of[:, :, :], in_=heads_of[:, :, :], compare_op=ALU.is_ge, fill=0.0, base=0,
                               pattern=[[P, 2], [-HD, H]], channel_multiplier=1).then_inc(of_done, 1)
            pool.wait_ge(of_done, 3)
            pool.affine_select(out=heads_of[:, :, :], in_=heads_of[:, :, :], compare_op=ALU.is_ge, fill=0.0,
                               base=HD - 1, pattern=[[-P, 2], [HD, H]], channel_multiplier=-1).then_inc(of_done, 1)
            pool.wait_ge(of_done, 4)
            with pool.Fori(0, NCH // 2) as i:
                for par in range(2):
                    for m in range(4):
                        pool.wait_ge(hi_done, i * 8 + par * 4 + m + 1)
                        pool.sem_inc(hold, 1)
                        pool.wait_ge(n_mm, i * 4 + par * 2 + m // 2 + 1)
                        pool.sem_inc(hold, 1)
                        pool.tensor_tensor(square[m][:, :], split[m][:, 0, :], split[m][:, 0, :], ALU.mult)\
                            .then_inc(sq_done, 1)


def attention_phase(nc, t, parts_dram, shift_dram, heads_dram, q_pos, k_pos, ps):
    with ExitStack() as ctx:
        def sb(name, shape, dt):
            return ctx.enter_context(nc.sbuf_tensor(name, shape, dt))

        def sem(name):
            return ctx.enter_context(nc.semaphore(name))

        q_st = [sb(f"q_stack{b}", [ROWS, L], BF16) for b in range(B)]
        k_st = [sb(f"k_stack{b}", [ROWS, 2, L], BF16) for b in range(B)]
        prob = sb("prob", [P, RING, SLOT_BANKS * CH], F32)
        vh, dist, nslope, near = (t[name] for name in ("v_heads", "distance", "minus_slopes", "near_bias"))
        unit_max = sb("unit_max", [P, KB, 2], F32)
        row_max = sb("row_max", [P, KB], F32)
        neg_max = sb("neg_max", [KB, P], F32)
        max_rest = sb("max_rest", [KB, P], F32)
        max_parts = sb("max_parts", [KB, 3, P], BF16)
        o_sb = sb("o_sum", [P, CH], F32)
        o_den = sb("o_den", [P, CH], F32)
        o_rec = sb("o_rec", [P, CH], F32)
        o_out = [sb(f"o_out{b}", [P, CH], F32) for b in range(B)]

        stack_in = [sem(f"stack_in{b}") for b in range(B)]
        unit_mm = sem("unit_mm")
        unit_bias = sem("unit_bias")
        unit_done = sem("unit_done")
        max_step = sem("max_step")
        max_T = sem("max_T")
        max_ready = sem("max_ready")
        max_in = [sem(f"max_in{b}") for b in range(B)]
        vh_done = sem("vh_done")
        scored = sem("scored")
        expd = sem("expd")
        diag_done = sem("diag_done")
        diag_even = sem("diag_even_done")
        diag_odd = sem("diag_odd_done")
        pv_done = sem("pv_done")
        o_read = sem("o_read")
        o_step = sem("o_step")
        o_ready = sem("o_ready")
        hold = sem("attn_hold")
        o_stored = [sem(f"o_stored{b}") for b in range(B)]

        LOADS = (1 + 3) + (1 + 3)

        def load_stacks(sp, h, b, q_row):
            head, cols = bass.ds(h, 1), slice(b * L, (b + 1) * L)
            row = 0
            for part, times in Q_PARTS:
                sp.dma_start(q_st[b][row:row + times * HD, :],
                             parts_dram[0, head, part, :, cols].broadcast_to([times, HD, L])).then_inc(stack_in[b], 16)
                row += times * HD
            sp.dma_start(q_st[b][q_row:ROWS, :], q_pos[head, q_row - ROW_M:, :].rearrange("h r n -> (h r) n"))\
              .then_inc(stack_in[b], 16)
            row = 0
            for parts in K_PARTS:
                rows = parts * HD
                sp.dma_start(k_st[b][row:row + rows, :, :],
                             parts_dram[1, head, 0:parts, :, cols].rearrange("h p d n -> (p d) h n")
                             .broadcast_to([rows, 2, L])).then_inc(stack_in[b], 16)
                row += rows
            sp.dma_start(k_st[b][ROW_M:ROWS, :, :], k_pos[head, :, :, :].rearrange("h v r n -> (h r) v n"))\
              .then_inc(stack_in[b], 16)

        def store_heads(sp, h, b):
            for g in range(QG):
                sp.dma_start(heads_dram[b, bass.ds(h * HD, HD), g * CH:(g + 1) * CH],
                             o_out[b][32 * g:32 * g + HD, :]).then_inc(o_stored[b], 16)

        def divide(dve, item):
            dve.stream_shuffle(o_den[:, :], o_sb[:, :], [HD] * 32).then_inc(o_step, 1)
            dve.wait_ge(o_step, item * 2 + 1)
            dve.reciprocal(o_rec[:, :], o_den[:, :]).then_inc(o_step, 1)
            dve.wait_ge(o_step, item * 2 + 2)


        def banded_sync(sp):
            def item(h, like, b):
                if like > 0:
                    before = item_before(h, like, b)
                    sp.wait_ge(scored, chunk_number(*before))
                load_stacks(sp, h, b, ROW_POS)
                sp.dma_start(q_st[b][ROW_M:ROW_POS, :].rearrange("r (g n) -> r g n", g=QG),
                             shift_dram[b, bass.ds(h, 1), :, :].rearrange("h r n -> r h n")
                             .broadcast_to([3, QG, CH])).then_inc(stack_in[b], 16)
                if like > 0:
                    sp.wait_ge(o_ready, h * 2 + b - 1)
                    store_heads(sp, h - 1, b)

            for h in range(LOOPED):
                for b in range(B):
                    item(h, h, b)
            with sp.Fori(LOOPED, H) as h:
                for b in range(B):
                    item(h, LOOPED, b)
            for b in range(B):
                sp.wait_ge(o_ready, H * 2 + b - 1)
                store_heads(sp, H - 1, b)
            for b in range(B):
                sp.wait_ge(o_stored[b], 64 * H)

        def banded_tensor(pe):
            def score(h, like, b, r):
                number, c = chunk_number(h, like, b) + r, BEGIN[like][b] + r
                if r == 0:
                    pe.wait_ge(stack_in[b], h * (16 * LOADS + 16) + (16 * LOADS + 16))
                if c >= 2:
                    pe.wait_ge(expd, number - 1)
                for piece in PLANS[like][r]:
                    kb = piece[0]
                    for ver, a, z, at in score_cuts(piece):
                        ver, rows = stack_rows(ver)
                        bank, col = divmod(at, CH)
                        mm = pe.matmul(ps[:, SLOT_BANKS * (c % 2) + bank, col:col + z - a],
                                       k_st[b][0:rows, ver, kb * P:(kb + 1) * P], q_st[b][0:rows, a:z],
                                       start=True, stop=True)
                mm.then_inc(scored, 1)

            def pv(h, like, b, r):
                plan = PLANS[like]
                number, c = chunk_number(h, like, b) + r, BEGIN[like][b] + r
                pe.wait_ge(expd, number + 1)
                blocks = sum(own_column(piece) is not None for chunk in plan[:r + 1] for piece in chunk)
                pe.wait_ge(diag_even, h * KB + (b * KB // 2 + (blocks + 1) // 2))
                if like > 0 or b > 0 or blocks > 1:
                    pe.wait_ge(diag_odd, h * KB + (b * KB // 2 + blocks // 2))
                if r == 0:
                    pe.wait_ge(vh_done, h * 2 + b + 1)
                    if like > 0:
                        pe.wait_ge(o_read, h * 2 + b - 1)
                pieces = [(n, piece) for n, chunk in enumerate(plan) for piece in by_turns(chunk)]
                for n, piece in pieces:
                    if n != r:
                        continue
                    kb, g, a, z, at = piece
                    of_group = [p for _, p in pieces if p[1] == g]
                    mm = pe.matmul(ps[32 * g:32 * g + 32, 6 + b, a - g * CH:z - g * CH], vh[b][:, kb, :],
                                   prob[:, c % RING, at:at + z - a], start=(piece is of_group[0]),
                                   stop=(piece is of_group[-1]), skip_group_check=True)
                mm.then_inc(pv_done, 1)

            def item(h, like, b):
                for r in range(len(PLANS[like])):
                    score(h, like, b, r)
                    if r >= PV_LAG:
                        pv(h, like, b, r - PV_LAG)
                    elif like > 0 or b > 0:
                        before = item_before(h, like, b)
                        pv(*before, len(PLANS[before[1]]) + r - PV_LAG)

            for h in range(LOOPED):
                for b in range(B):
                    item(h, h, b)
            with pe.Fori(LOOPED, H) as h:
                for b in range(B):
                    item(h, LOOPED, b)
            for r in range(CHUNKS - PV_LAG, CHUNKS):
                pv(H - 1, LOOPED, 1, r)

        def banded_scalar(act):
            def item(h, like, b):
                for r, chunk in enumerate(PLANS[like]):
                    number, c = chunk_number(h, like, b) + r, BEGIN[like][b] + r
                    act.wait_ge(scored, number + 1)
                    if c >= RING:
                        act.wait_ge(pv_done, number - (RING - 1))
                    width = chunk[-1][4] + chunk[-1][3] - chunk[-1][2]
                    bank = SLOT_BANKS * (c % 2)
                    act.activation(prob[:, c % RING, 0:width],
                                   ps[:, bank:bank + SLOT_BANKS, :].rearrange("p c n -> p (c n)")[:, 0:width],
                                   ACT.Exp).then_inc(expd, 1)

            for h in range(LOOPED):
                for b in range(B):
                    item(h, h, b)
            with act.Fori(LOOPED, H) as h:
                for b in range(B):
                    item(h, LOOPED, b)

        def near_blocks(eng, h, like, b, r, odd, done):
            own = [own_column(piece) for piece in PLANS[like][r]
                   if own_column(piece) is not None and ORDER.index(piece[0]) % 2 == odd]
            if own:
                eng.wait_ge(expd, chunk_number(h, like, b) + r + 1)
                if odd:
                    eng.sem_inc(hold, 1)
            for at in own:
                here = prob[:, (BEGIN[like][b] + r) % RING, at:at + P]
                eng.tensor_tensor(here, here, near[:, bass.ds(h, 1), :].rearrange("p a n -> p (a n)"), ALU.mult)\
                   .then_inc(done, 1)

        def banded_vector(dve):
            def normalise(h, like, b, end):
                dve.wait_ge(pv_done, end)
                dve.tensor_copy(o_sb[:, :], ps[:, 6 + b, :]).then_inc(o_read, 1)
                dve.wait_ge(o_read, h * 2 + b + 1)
                dve.sem_inc(hold, 1)
                divide(dve, h * 2 + b)
                if like > 0:
                    dve.wait_ge(o_stored[b], h * 64)
                dve.tensor_tensor(o_out[b][:, :], o_sb[:, :], o_rec[:, :], ALU.mult).then_inc(o_ready, 1)
                dve.wait_ge(o_ready, h * 2 + b + 1)

            def item(h, like, b):
                for r in range(len(PLANS[like])):
                    near_blocks(dve, h, like, b, r, 0, diag_even)
                    if r == PV_LAG - 1 and (like > 0 or b > 0):
                        normalise(*item_before(h, like, b), chunk_number(h, like, b))

            for h in range(LOOPED):
                for b in range(B):
                    item(h, h, b)
            with dve.Fori(LOOPED, H) as h:
                for b in range(B):
                    item(h, LOOPED, b)
            normalise(H - 1, LOOPED, 1, chunk_number(H, LOOPED, 0))

        def banded_gpsimd(pool):
            def item(h, like, b):
                if like > 0:
                    before = item_before(h, like, b)
                    pool.wait_ge(pv_done, chunk_number(*before))
                pool.tensor_copy(vh[b][:, :, 0:HD], t["v"][:, b * KB:(b + 1) * KB, bass.ds(h * HD, HD)])\
                    .then_inc(vh_done, 1)
                for r in range(len(PLANS[like])):
                    near_blocks(pool, h, like, b, r, 1, diag_odd)

            for h in range(LOOPED):
                for b in range(B):
                    item(h, h, b)
            with pool.Fori(LOOPED, H) as h:
                for b in range(B):
                    item(h, LOOPED, b)


        def general_sync(sp):
            with sp.Fori(0, H) as h:
                for b in range(B):
                    sp.wait_ge(scored, h * (2 * CHUNKS) + (b + 1) * CHUNKS)
                    load_stacks(sp, h, b, ROW_M)
                    sp.wait_ge(max_ready, h * 2 + b + 1)
                    for part in range(3):
                        sp.dma_start(q_st[b][ROW_M + part:ROW_M + part + 1, :].rearrange("r (t n) -> r t n", t=KB),
                                     max_parts[:, part, :]).then_inc(max_in[b], 16)
                    sp.wait_ge(o_ready, h * 2 + b + 1)
                    store_heads(sp, h, b)
            for b in range(B):
                sp.wait_ge(o_stored[b], 64 * (H + 1))

        def general_tensor(pe):
            pe.sem_inc(scored, 2 * CHUNKS)
            pe.sem_inc(pv_done, 2 * KB)
            with pe.Fori(0, H) as h:
                for b in range(B):
                    pe.wait_ge(stack_in[b], h * (16 * LOADS) + 16 * LOADS)
                    pe.wait_ge(expd, h * (2 * CHUNKS) + (b + 2) * CHUNKS)
                    for u in range(2 * KB):
                        i, half = divmod(u, 2)
                        if u >= 3:
                            pe.wait_ge(unit_done, h * (4 * KB) + b * 2 * KB + u - 2)
                        for bank in range(2):
                            k0 = half * 1024 + bank * CH
                            cuts = sorted({k0, k0 + CH, *(c for c in (i * P, i * P + P) if k0 < c < k0 + CH)})
                            for a, z in zip(cuts, cuts[1:]):
                                ver = RIGHT if z <= i * P else LEFT if a >= i * P + P else DIAG
                                ver, rows = stack_rows(ver)
                                mm = pe.matmul(ps[:, 2 * (u % 3) + bank, a - k0:z - k0],
                                               q_st[b][0:rows, i * P:(i + 1) * P], k_st[b][0:rows, ver, a:z],
                                               start=True, stop=True)
                        mm.then_inc(unit_mm, 1)
                    pe.wait_ge(max_step, h * 10 + b * 5 + 1)
                    pe.transpose(ps[0:KB, 0, 0:P], row_max[:, :], t["ident"][:, :]).then_inc(max_T, 1)
                    pe.wait_ge(max_in[b], h * 48 + 48)
                    pe.wait_ge(vh_done, h * 2 + b + 3)

                    def score(ch):
                        if ch >= 2:
                            pe.wait_ge(expd, h * (2 * CHUNKS) + (b + 2) * CHUNKS + ch - 1)
                        for n, (kb, g) in enumerate(chunk_tiles(ch)):
                            bank = SLOT_BANKS * (ch % 2) + n
                            q0, k0 = g * CH, kb * P
                            cuts = sorted({q0, q0 + CH, *(c for c in (k0, k0 + P) if q0 < c < q0 + CH)})
                            for a, z in zip(cuts, cuts[1:]):
                                ver = LEFT if z <= k0 else RIGHT if a >= k0 + P else DIAG
                                ver, rows = stack_rows(ver)
                                mm = pe.matmul(ps[:, bank, a - q0:z - q0], k_st[b][0:rows, ver, k0:k0 + P],
                                               q_st[b][0:rows, a:z], start=True, stop=True)
                        mm.then_inc(scored, 1)

                    def pv(kb):
                        if kb == 0:
                            pe.wait_ge(o_read, h * 2 + b + 1)
                        last = (QG * kb + QG - 1) // SLOT_BANKS
                        pe.wait_ge(expd, h * (2 * CHUNKS) + (b + 2) * CHUNKS + last + 1)
                        pe.wait_ge(diag_done, h * (2 * KB) + b * KB + kb + 1)
                        for g in range(QG):
                            n = QG * kb + g
                            ch, c = divmod(n, SLOT_BANKS)
                            mm = pe.matmul(ps[32 * g:32 * g + 32, 6 + b, :], vh[b][:, kb, :],
                                           prob[:, ch % RING, c * CH:(c + 1) * CH],
                                           start=(kb == 0), stop=(kb == KB - 1))
                        mm.then_inc(pv_done, 1)

                    for ch in range(CHUNKS):
                        score(ch)
                        for kb in range(blocks_done(ch - PV_LAG - 1), blocks_done(ch - PV_LAG)):
                            pv(kb)
                    for kb in range(blocks_done(CHUNKS - 1 - PV_LAG), KB):
                        pv(kb)

        def general_scalar(act):
            act.sem_inc(expd, 2 * CHUNKS)
            with act.Fori(0, H) as h:
                for b in range(B):
                    for ch in range(CHUNKS):
                        act.wait_ge(scored, h * (2 * CHUNKS) + (b + 2) * CHUNKS + ch + 1)
                        pb, pch = ring_user_before(b, ch)
                        act.wait_ge(pv_done, h * (2 * KB) + (pb + 2) * KB
                                    + (min(pch * SLOT_BANKS + SLOT_BANKS, TILES) - 1) // QG + 1)
                        n = len(chunk_tiles(ch))
                        bank = SLOT_BANKS * (ch % 2)
                        act.activation(prob[:, ch % RING, 0:n * CH],
                                       ps[:, bank:bank + n, :].rearrange("p c n -> p (c n)"),
                                       ACT.Exp).then_inc(expd, 1)

        def general_vector(dve):
            dve.sem_inc(o_read, 2)
            for b in range(B):
                dve.sem_inc(o_stored[b], 64)
            with dve.Fori(0, H) as h:
                for b in range(B):
                    for u in range(2 * KB):
                        i, half = divmod(u, 2)
                        dve.wait_ge(unit_mm, h * (4 * KB) + b * 2 * KB + u + 1)
                        if i * P // 1024 == half:
                            bank, a = divmod(i * P - half * 1024, CH)
                            here = ps[:, 2 * (u % 3) + bank, a:a + P]
                            dve.scalar_tensor_tensor(out=here, in0=dist[:, :], scalar=nslope[:, bass.ds(h, 1)],
                                                     in1=here, op0=ALU.mult, op1=ALU.add).then_inc(unit_bias, 1)
                            dve.wait_ge(unit_bias, h * (2 * KB) + b * KB + i + 1)
                        dve.tensor_reduce(unit_max[:, i, half:half + 1],
                                          ps[:, 2 * (u % 3):2 * (u % 3) + 2, :].rearrange("p c n -> p (c n)"),
                                          AX.X, ALU.max).then_inc(unit_done, 1)
                    dve.wait_ge(unit_done, h * (4 * KB) + (b + 1) * 2 * KB)
                    step = h * 10 + b * 5
                    dve.tensor_tensor(row_max[:, :], unit_max[:, :, 0], unit_max[:, :, 1], ALU.max)\
                       .then_inc(max_step, 1)
                    dve.wait_ge(max_T, h * 2 + b + 1)
                    dve.tensor_scalar(neg_max[:, :], ps[0:KB, 0, 0:P], -1.0, None, ALU.mult).then_inc(max_step, 1)
                    dve.wait_ge(max_step, step + 2)
                    dve.tensor_copy(max_parts[:, 0, :], neg_max[:, :]).then_inc(max_step, 1)
                    dve.wait_ge(max_step, step + 3)
                    dve.tensor_tensor(max_rest[:, :], neg_max[:, :], max_parts[:, 0, :], ALU.subtract)\
                       .then_inc(max_step, 1)
                    dve.wait_ge(max_step, step + 4)
                    dve.tensor_copy(max_parts[:, 1, :], max_rest[:, :]).then_inc(max_step, 1)
                    dve.wait_ge(max_step, step + 5)
                    dve.tensor_tensor(max_parts[:, 2, :], max_rest[:, :], max_parts[:, 1, :], ALU.subtract)\
                       .then_inc(max_ready, 1)
                    for kb in range(KB):
                        g, off = divmod(kb * P, CH)
                        n = QG * kb + g
                        ch, c = divmod(n, SLOT_BANKS)
                        dve.wait_ge(expd, h * (2 * CHUNKS) + (b + 2) * CHUNKS + ch + 1)
                        here = prob[:, ch % RING, c * CH + off:c * CH + off + P]
                        dve.tensor_tensor(here, here, near[:, bass.ds(h, 1), :].rearrange("p a n -> p (a n)"),
                                          ALU.mult).then_inc(diag_done, 1)
                    dve.wait_ge(pv_done, h * (2 * KB) + (b + 3) * KB)
                    dve.tensor_copy(o_sb[:, :], ps[:, 6 + b, :]).then_inc(o_read, 1)
                    dve.wait_ge(o_read, h * 2 + b + 3)
                    dve.sem_inc(hold, 1)
                    divide(dve, h * 2 + b)
                    dve.wait_ge(o_stored[b], h * 64 + 64)
                    dve.tensor_tensor(o_out[b][:, :], o_sb[:, :], o_rec[:, :], ALU.mult).then_inc(o_ready, 1)
                    dve.wait_ge(o_ready, h * 2 + b + 1)

        def general_gpsimd(pool):
            pool.sem_inc(vh_done, 2)
            with pool.Fori(0, H) as h:
                for b in range(B):
                    pool.wait_ge(pv_done, h * (2 * KB) + (b + 1) * KB)
                    pool.tensor_copy(vh[b][:, :, 0:HD], t["v"][:, b * KB:(b + 1) * KB, bass.ds(h * HD, HD)])\
                        .then_inc(vh_done, 1)

        with nc.Block() as block:
            @block.sync
            def _(sp):
                bounded = sp.value_load(t["bounded"][0:1, 0:1], min_val=0, max_val=1)
                with sp.If(bounded == 1):
                    banded_sync(sp)
                with sp.Else():
                    general_sync(sp)

            @block.tensor
            def _(pe):
                bounded = pe.value_load(t["bounded"][0:1, 0:1], min_val=0, max_val=1)
                with pe.If(bounded == 1):
                    banded_tensor(pe)
                with pe.Else():
                    general_tensor(pe)

            @block.scalar
            def _(act):
                bounded = act.value_load(t["bounded"][0:1, 0:1], min_val=0, max_val=1)
                with act.If(bounded == 1):
                    banded_scalar(act)
                with act.Else():
                    general_scalar(act)

            @block.vector
            def _(dve):
                bounded = dve.value_load(t["bounded"][0:1, 0:1], min_val=0, max_val=1)
                with dve.If(bounded == 1):
                    banded_vector(dve)
                with dve.Else():
                    general_vector(dve)

            @block.gpsimd
            def _(pool):
                bounded = pool.value_load(t["bounded"][0:1, 0:1], min_val=0, max_val=1)
                with pool.If(bounded == 1):
                    banded_gpsimd(pool)
                with pool.Else():
                    general_gpsimd(pool)


def prefix_ones(pool, upper, ones, step):
    pool.memset(ones[:, :], 1.0).then_inc(step, 1)
    pool.memset(upper[:, :], 1.0).then_inc(step, 1)
    pool.wait_ge(step, 2)
    pool.affine_select(out=upper[:, :], in_=upper[:, :], compare_op=ALU.is_gt, fill=0.0, base=0,
                       pattern=[[1, P]], channel_multiplier=-1).then_inc(step, 1)


def route_phase(nc, t, x, heads_dram, w1_dram, w2_dram, x1_dram, acc_dram, ps):
    with ExitStack() as ctx:
        def sb(name, shape, dt):
            return ctx.enter_context(nc.sbuf_tensor(name, shape, dt))

        def sem(name):
            return ctx.enter_context(nc.semaphore(name))

        wo, bo, rw, rb, w_in = (t[name] for name in ("w_out", "b_out", "router_wT", "router_bias", "route_w_in"))
        oc = [sb(f"heads_chunk{p}", [P, 2, CH], F32) for p in range(2)]
        xc = [sb(f"x_chunk{p}", [P, TPC, D], F32) for p in range(2)]
        y = [sb(f"y{p}", [P, TPC, D], F32) for p in range(2)]
        x1T = [sb(f"x1T{p}", [P, 2, CH], F32) for p in range(2)]
        stats = sb("stats", [P, TPC, 6], F32)
        mv = sb("mean_var", [P, TPC, 2], F32)
        sd = sb("std", [P, TPC], F32)
        rstd = sb("rstd", [P, TPC], F32)
        eps = sb("eps", [P, 1], F32)
        x1 = sb("x1", [P, NT, D], F32)
        logits = sb("logits", [P, NT, E], F32)
        shape = [P, NT, E]
        ex = sb("ex", shape, F32)
        wgt = sb("weights", shape, F32)
        left = sb("weights_left", shape, F32)
        tmp = sb("tmp", shape, F32)
        pick = [sb(f"pick{k}", shape, F32) for k in range(2)]
        mask = sb("mask", shape, F32)
        before = sb("before", shape, F32)
        valid = sb("valid", shape, F32)
        tot = sb("totals", shape, F32)
        scan = sb("scan", shape, F32)
        expert_id = sb("expert_id", shape, F32)
        top = sb("top", [P, NT], F32)
        den = sb("den", [P, NT], F32)
        idx = [sb(f"choice{k}", [P, NT], F32) for k in range(2)]
        upper = sb("upper", [P, P], F32)
        ones = sb("ones", [P, P], F32)
        iota_i = sb("iota_i", shape, I32)
        column_ids = sb("column_ids", [P, P, HIT_TILES], I32)
        tile_id = sb("tile_id", [P, NT], F32)
        place = sb("place", [P, NT], F32)
        in_tile = sb("slot_in_tile", [P, E, NT], BF16)
        of_tile = sb("slot_tile", shape, F32)
        lot_w = [sb(f"lot_w{n}", shape, BF16) for n in range(3)]
        sel = [sb(f"in_slot_tile{a}", shape, F32) for a in range(ST)]
        lots = sb("lots", [P, NT, E, ST * LOT], BF16)
        columns = sb("columns", [P, P, HIT_TILES], BF16)
        hits = [sb(f"hits{n}", [P, P, HIT_TILES], BF16) for n in range(HIT_SLOTS)]
        lot = sb("lot", [P, EX, ST, LOT], F32)
        free = sb("free", [P, EX, ST], F32)
        acc = [sb(f"acc{p}", [P, TPC, D], F32) for p in range(2)]
        keep = sb("keep", [P, NT], F32)

        hold = sem("route_hold")
        oc_in = [sem(f"oc_in{p}") for p in range(2)]
        xc_in = [sem(f"xc_in{p}") for p in range(2)]
        biased = sem("x_biased")
        y_mm = sem("y_mm")
        y_done = sem("y_done")
        st_done = sem("stats_done")
        mv_done = sem("mean_var_done")
        sd_done = sem("std_done")
        rs_done = sem("rstd_done")
        ln_done = sem("ln_done")
        row_done = sem("row_done")
        x1_mm = sem("x1T_mm")
        x1_done = sem("x1T_done")
        lg_mm = sem("logits_mm")
        lg_done = sem("logits_done")
        step = sem("route_step")
        c_step = sem("route_const_step")
        cnt_mm = sem("counts_mm")
        exp_done = sem("router_exp_done")
        eps_done = sem("eps_done")
        kept = sem("kept")
        sel_done = sem("in_slot_tile_done")
        lots_done = sem("lots_done")
        lots_pool = sem("lots_by_pool_done")
        hit = sem("hit")
        met = sem("met")
        lot_step = sem("lot_step")
        x1_out = [sem(f"x1_out{p}") for p in range(2)]
        acc_done = sem("acc_done")
        acc_out = [sem(f"acc_out{p}") for p in range(2)]
        block = ctx.enter_context(nc.Block())

        def wide(a):
            return a[:, :].rearrange("p (t o) -> p t o", o=1).broadcast_to([P, NT, E])

        def lot_values(a):
            return ((LOT_PLACE, wide(place)), (LOT_TILE, wide(tile_id)), (LOT_W, lot_w[0][:, :, :]),
                    (LOT_W + 1, lot_w[1][:, :, :]), (LOT_W + 2, lot_w[2][:, :, :]))

        @block.sync
        def _(sp):
            with sp.Fori(0, B) as b:
                for c in range(QG):
                    par = c % 2
                    n = b * QG + c
                    sp.wait_ge(y_mm, n * 2 + 2)
                    sp.dma_start(oc[par][:, :, :],
                                 heads_dram[bass.ds(b, 1), :, c * CH:(c + 1) * CH]
                                 .rearrange("b (k p) n -> p (b k) n", p=P)).then_inc(oc_in[par], 16)
                    sp.wait_ge(y_done, n * 2 + 2)
                    sp.dma_start(xc[par][:, :, :], x[bass.ds(n * TPC, TPC), :, :].rearrange("t p n -> p t n"))\
                      .then_inc(xc_in[par], 16)
            sp.wait_ge(ln_done, 4 * NCH + 4)
            for par in range(2):
                load_expert(sp, t, w1_dram, w2_dram, par, par)
            with sp.Fori(0, NCH // 2) as i:
                for par in range(2):
                    sp.wait_ge(acc_done, i * 2 + par + 1)
                    sp.dma_start(acc_dram[bass.ds((i * 2 + par) * TPC, TPC), :, :].rearrange("t p n -> p t n"),
                                 acc[par][:, :, :]).then_inc(acc_out[par], 16)
            for par in range(2):
                sp.wait_ge(acc_out[par], 16 * (NCH // 2) + 16)

        @block.tensor
        def _(pe):
            pe.sem_inc(y_mm, 4)
            pe.wait_ge(w_in, 16 * 11)
            def project(i, par):
                n = i * 2 + par
                pe.wait_ge(oc_in[par], i * 16 + 16)
                for pair in range(2):
                    pe.wait_ge(y_done, n * 2 + pair + 3)
                    for s in range(2):
                        tok = (pair * 2 + s) * P
                        for k in range(2):
                            mm = pe.matmul(ps[:, pair, s * D:(s + 1) * D], oc[par][:, k, tok:tok + P],
                                           wo[:, k, :], start=(k == 0), stop=(k == 1))
                    mm.then_inc(y_mm, 1)

            def route(i, par):
                n = i * 2 + par
                pe.wait_ge(ln_done, n * 4 + 8)
                for k in range(2):
                    pe.wait_ge(x1_done, n * 2 + k + 1)
                    for s in range(TPC):
                        mm = pe.transpose(ps[:, 2 + k, s * P:(s + 1) * P], y[par][:, s, k * P:(k + 1) * P],
                                          t["ident"][:, :])
                    mm.then_inc(x1_mm, 1)
                pe.wait_ge(x1_done, n * 2 + 4)
                pe.wait_ge(lg_done, n + 1)
                for s in range(TPC):
                    for k in range(2):
                        mm = pe.matmul(ps[:, 4, s * E:(s + 1) * E], x1T[par][:, k, s * P:(s + 1) * P],
                                       rw[:, k, :], start=(k == 0), stop=(k == 1))
                mm.then_inc(lg_mm, 1)

            project(0, 0)
            with pe.Fori(0, NCH // 2 - 1) as i:
                project(i, 1)
                route(i, 0)
                project(i + 1, 0)
                route(i, 1)
            last = NCH // 2 - 1
            project(last, 1)
            route(last, 0)
            route(last, 1)
            pe.wait_ge(step, 18)
            pe.wait_ge(c_step, 3)
            flat = mask[:, :, :].rearrange("p a b -> p (a b)")
            pe.matmul(ps[:, 5, 0:NT * E], upper[:, :], flat, start=True, stop=True).then_inc(cnt_mm, 1)
            pe.matmul(ps[:, 6, 0:NT * E], ones[:, :], flat, start=True, stop=True).then_inc(cnt_mm, 1)
            pe.sem_inc(met, HIT_SLOTS)
            pe.wait_ge(lots_done, (ST - POOL_TILES) * LOT)
            pe.wait_ge(lots_pool, POOL_TILES * LOT)
            with pe.Fori(0, EX) as e:
                for g in range(NT // HIT_TILES):
                    pe.wait_ge(hit, e * (NT // HIT_TILES) + g + 1)
                    for s in range(HIT_TILES):
                        n = g * HIT_TILES + s
                        mm = pe.matmul(ps[:, 7, bass.ds(e * (ST * LOT), ST * LOT)], hits[g % HIT_SLOTS][:, :, s],
                                       lots[:, n, bass.ds(e, 1), :].rearrange("p e l -> p (e l)"),
                                       start=(n == 0), stop=(n == NT - 1))
                    mm.then_inc(met, 1)

        @block.scalar
        def _(act):
            for par in range(2):
                act.sem_inc(x1_out[par], 16)
            act.sem_inc(x1_done, 2)
            act.sem_inc(row_done, 2)
            act.wait_ge(eps_done, 1)
            with act.Fori(0, NCH // 2) as i:
                for par in range(2):
                    n = i * 2 + par
                    act.wait_ge(mv_done, n * 4 + 4)
                    act.wait_ge(rs_done, n + 1)
                    act.activation(sd[:, :], mv[:, :, 1], ACT.Sqrt, bias=eps[:, 0:1]).then_inc(sd_done, 1)
                    act.wait_ge(ln_done, n * 4 + 8)
                    act.activation(x1[:, bass.ds(n * TPC, TPC), :], y[par][:, :, :], ACT.Copy).then_inc(row_done, 1)
                    for k in range(2):
                        act.wait_ge(x1_mm, n * 2 + k + 1)
                        act.activation(x1T[par][:, k, :], ps[:, 2 + k, :], ACT.Copy).then_inc(x1_done, 1)
                    act.dma_start(x1_dram[bass.ds(n * TPC, TPC), :, :].rearrange("t p n -> p t n"), y[par][:, :, :])\
                       .then_inc(x1_out[par], 16)
            act.wait_ge(step, 2)
            act.activation(ex[:, :, :], tmp[:, :, :], ACT.Exp).then_inc(exp_done, 1)
            act.wait_ge(kept, 1)
            act.wait_ge(row_done, NCH + 2)
            with act.Fori(0, NCH // 2) as i:
                for par in range(2):
                    n = i * 2 + par
                    act.wait_ge(acc_out[par], i * 16 + 16)
                    for s in range(TPC):
                        ins = act.activation(acc[par][:, s, :],
                                             x1[:, bass.ds(n * TPC + s, 1), :].rearrange("p a n -> p (a n)"),
                                             ACT.Copy, scale=keep[:, bass.ds(n * TPC + s, 1)])
                    ins.then_inc(acc_done, 1)
            for par in range(2):
                act.wait_ge(x1_out[par], 16 * (NCH // 2) + 16)

        @block.vector
        def _(dve):
            dve.sem_inc(y_done, 4)
            dve.sem_inc(rs_done, 1)
            dve.sem_inc(ln_done, 4)
            dve.sem_inc(lg_done, 1)
            for par in range(2):
                dve.sem_inc(acc_out[par], 16)
            dve.memset(eps[:, :], EPS).then_inc(eps_done, 1)
            dve.wait_ge(w_in, 16 * 11)
            def layernorm(i, par):
                n = i * 2 + par
                dve.wait_ge(biased, n + 1)
                dve.wait_ge(row_done, n + 1)
                dve.wait_ge(x1_out[par], i * 16 + 16)
                for pair in range(2):
                    dve.wait_ge(y_mm, n * 2 + pair + 5)
                    dve.tensor_tensor(y[par][:, 2 * pair:2 * pair + 2, :],
                                      ps[:, pair, :].rearrange("p (s n) -> p s n", s=2),
                                      xc[par][:, 2 * pair:2 * pair + 2, :], ALU.add).then_inc(y_done, 1)
                dve.wait_ge(y_done, n * 2 + 6)
                for s in range(TPC):
                    dve.bn_stats(stats[:, s, :], y[par][:, s, :]).then_inc(st_done, 1)
                dve.wait_ge(st_done, n * 4 + 4)
                dve.sem_inc(hold, 1)
                for s in range(TPC):
                    dve.bn_aggr(mv[:, s, :], stats[:, s, :]).then_inc(mv_done, 1)
                dve.wait_ge(sd_done, n + 1)
                dve.reciprocal(rstd[:, :], sd[:, :]).then_inc(rs_done, 1)
                dve.wait_ge(rs_done, n + 2)
                for s in range(TPC):
                    dve.tensor_scalar(y[par][:, s, :], y[par][:, s, :], mv[:, s, 0:1], rstd[:, s:s + 1],
                                      ALU.subtract, ALU.mult).then_inc(ln_done, 1)
                dve.wait_ge(ln_done, n * 4 + 8)

            def add_router_bias(n):
                dve.wait_ge(lg_mm, n + 1)
                dve.tensor_tensor(logits[:, bass.ds(n * TPC, TPC), :],
                                  ps[:, 4, 0:TPC * E].rearrange("p (s e) -> p s e", e=E), rb[:, :, :],
                                  ALU.add).then_inc(lg_done, 1)

            layernorm(0, 0)
            layernorm(0, 1)
            add_router_bias(0)
            with dve.Fori(1, NCH // 2) as i:
                layernorm(i, 0)
                add_router_bias(i * 2 - 1)
                layernorm(i, 1)
                add_router_bias(i * 2)
            add_router_bias(NCH - 1)
            count = [0]

            def link(ins):
                ins.then_inc(step, 1)
                count[0] += 1
                dve.wait_ge(step, count[0])

            dve.wait_ge(lg_done, NCH + 1)
            dve.wait_ge(c_step, 13)
            link(dve.tensor_reduce(top[:, :], logits[:, :, :], AX.X, ALU.max))
            link(dve.tensor_tensor(tmp[:, :, :], logits[:, :, :], wide(top), ALU.subtract))
            dve.wait_ge(exp_done, 1)
            link(dve.tensor_reduce(den[:, :], ex[:, :, :], AX.X, ALU.add))
            link(dve.reciprocal(keep[:, :], den[:, :]))
            link(dve.tensor_tensor(wgt[:, :, :], ex[:, :, :], wide(keep), ALU.mult))
            for k in range(2):
                src = (wgt, left)[k]
                link(dve.tensor_reduce(top[:, :], src[:, :, :], AX.X, ALU.max))
                link(dve.tensor_tensor(tmp[:, :, :], src[:, :, :], wide(top), ALU.is_lt))
                link(dve.scalar_tensor_tensor(out=tmp[:, :, :], in0=tmp[:, :, :], scalar=float(E),
                                              in1=expert_id[:, :, :], op0=ALU.mult, op1=ALU.add))
                link(dve.tensor_reduce(idx[k][:, :], tmp[:, :, :], AX.X, ALU.min))
                link(dve.tensor_tensor(pick[k][:, :, :], expert_id[:, :, :], wide(idx[k]), ALU.is_equal))
                if k == 0:
                    link(dve.scalar_tensor_tensor(out=left[:, :, :], in0=pick[0][:, :, :], scalar=-2.0,
                                                  in1=wgt[:, :, :], op0=ALU.mult, op1=ALU.add))
            link(dve.tensor_tensor(tmp[:, :, :], pick[0][:, :, :], pick[1][:, :, :], ALU.add))
            link(dve.scalar_tensor_tensor(out=mask[:, :, :], in0=wgt[:, :, :], scalar=0.0, in1=tmp[:, :, :],
                                          op0=ALU.is_gt, op1=ALU.mult))
            assert count[0] == 18
            link(dve.tensor_tensor(keep[:, :], wgt[:, :, EX], mask[:, :, EX], ALU.mult))
            dve.tensor_scalar(keep[:, :], keep[:, :], 1.0, None, ALU.add).then_inc(kept, 1)
            dve.wait_ge(cnt_mm, 2)
            link(dve.tensor_copy(tot[:, :, :], ps[:, 6, 0:NT * E].rearrange("p (a b) -> p a b", b=E)))
            for e in range(E):
                dve.tensor_tensor_scan(scan[:, :, e], scan_ones(ones, NT), tot[:, :, e], 0.0, ALU.mult, ALU.add)\
                   .then_inc(step, 1)
            count[0] += E
            dve.wait_ge(step, count[0])
            link(dve.tensor_tensor(before[:, :, :], scan[:, :, :], tot[:, :, :], ALU.subtract))
            link(dve.tensor_tensor(before[:, :, :], ps[:, 5, 0:NT * E].rearrange("p (a b) -> p a b", b=E),
                                   before[:, :, :], ALU.add))
            link(dve.scalar_tensor_tensor(out=valid[:, :, :], in0=before[:, :, :], scalar=float(CAP),
                                          in1=mask[:, :, :], op0=ALU.is_lt, op1=ALU.mult))
            link(dve.tensor_scalar(of_tile[:, :, :], before[:, :, :], float(P), None, ALU.is_ge))
            for n in range(2, ST):
                link(dve.scalar_tensor_tensor(out=of_tile[:, :, :], in0=before[:, :, :], scalar=float(n * P),
                                              in1=of_tile[:, :, :], op0=ALU.is_ge, op1=ALU.add))
            link(dve.scalar_tensor_tensor(out=in_tile[:, :, :].rearrange("p e t -> p t e"), in0=of_tile[:, :, :], scalar=-float(P),
                                          in1=before[:, :, :], op0=ALU.mult, op1=ALU.add))
            link(dve.tensor_tensor(left[:, :, :], wgt[:, :, :], mask[:, :, :], ALU.mult))
            for n in range(3):
                link(dve.tensor_copy(lot_w[n][:, :, :], left[:, :, :]))
                if n < 2:
                    link(dve.tensor_tensor(left[:, :, :], left[:, :, :], lot_w[n][:, :, :], ALU.subtract))
            for a in range(ST):
                dve.scalar_tensor_tensor(out=sel[a][:, :, :], in0=of_tile[:, :, :], scalar=float(a),
                                         in1=valid[:, :, :], op0=ALU.is_equal, op1=ALU.mult).then_inc(sel_done, 1)
            dve.wait_ge(sel_done, ST)
            for a in range(ST - POOL_TILES):
                for what, value in lot_values(a):
                    dve.tensor_tensor(lots[:, :, :, a * LOT + what], sel[a][:, :, :], value, ALU.mult)\
                       .then_inc(lots_done, 1)
                dve.tensor_copy(lots[:, :, :, a * LOT + LOT_TAKEN], sel[a][:, :, :]).then_inc(lots_done, 1)
            with dve.Fori(0, EX) as e:
                for g in range(NT // HIT_TILES):
                    dve.wait_ge(met, e * (NT // HIT_TILES) + g + 1)
                    dve.tensor_tensor(hits[g % HIT_SLOTS][:, :, :], columns[:, :, :],
                                      in_tile[:, bass.ds(e, 1), g * HIT_TILES:(g + 1) * HIT_TILES]
                                      .broadcast_to([P, P, HIT_TILES]), ALU.is_equal).then_inc(hit, 1)
            dve.wait_ge(met, EX * (NT // HIT_TILES) + HIT_SLOTS)
            dve.tensor_copy(lot[:, :, :, :], ps[:, 7, 0:EX * ST * LOT].rearrange("p (e a l) -> p e a l", e=EX, l=LOT))\
               .then_inc(lot_step, 1)
            dve.wait_ge(lot_step, 1)
            dve.tensor_tensor(lot[:, :, :, LOT_W], lot[:, :, :, LOT_W], lot[:, :, :, LOT_W + 1], ALU.add)\
               .then_inc(lot_step, 1)
            dve.scalar_tensor_tensor(out=lot[:, :, :, LOT_PLACE], in0=lot[:, :, :, LOT_TILE], scalar=float(P),
                                     in1=lot[:, :, :, LOT_PLACE], op0=ALU.mult, op1=ALU.add).then_inc(lot_step, 1)
            dve.scalar_tensor_tensor(out=free[:, :, :], in0=lot[:, :, :, LOT_TAKEN], scalar=-1.0,
                                     in1=t["beyond"][:, :].rearrange("p (o a) -> p o a", o=1)
                                     .broadcast_to([P, EX, ST]), op0=ALU.add, op1=ALU.mult).then_inc(lot_step, 1)
            dve.wait_ge(lot_step, 4)
            dve.tensor_tensor(t["slot_weight"][:, :, :], lot[:, :, :, LOT_W], lot[:, :, :, LOT_W + 2], ALU.add)\
               .then_inc(lot_step, 1)
            dve.tensor_tensor(lot[:, :, :, LOT_TILE], lot[:, :, :, LOT_PLACE], free[:, :, :], ALU.subtract)\
               .then_inc(lot_step, 1)
            dve.wait_ge(lot_step, 6)
            dve.tensor_copy(t["slot_token"][:, :, :], lot[:, :, :, LOT_TILE]).then_inc(lot_step, 1)
            dve.wait_ge(lot_step, 7)

        @block.gpsimd
        def _(pool):
            prefix_ones(pool, upper, ones, c_step)
            flat = iota_i[:, :, :]
            pool.iota(flat, [[0, NT], [1, E]], base=0, channel_multiplier=0).then_inc(c_step, 1)
            pool.wait_ge(c_step, 4)
            pool.tensor_copy(expert_id[:, :, :], flat).then_inc(c_step, 1)
            def numbers(dst, src, pattern, base, mult, at):
                pool.wait_ge(c_step, at)
                pool.iota(src, pattern, base=base, channel_multiplier=mult).then_inc(c_step, 1)
                pool.wait_ge(c_step, at + 1)
                pool.tensor_copy(dst, src).then_inc(c_step, 1)

            ids = t["token_ids"]
            numbers(tile_id[:, :], ids[:, 0:NT], [[1, NT]], 0, 0, 5)
            numbers(place[:, :], ids[:, 0:NT], [[0, NT]], 0, 1, 7)
            numbers(columns[:, :, :], column_ids[:, :, :], [[1, P], [0, HIT_TILES]], 0, 0, 9)
            numbers(t["beyond"][:, :], ids[:, 0:ST], [[P, ST]], T, 1, 11)
            pool.wait_ge(w_in, 16 * 11)
            with pool.Fori(0, NCH // 2) as i:
                for par in range(2):
                    pool.wait_ge(xc_in[par], i * 16 + 16)
                    pool.tensor_tensor(xc[par][:, :, :], xc[par][:, :, :], bo[:, :, :], ALU.add).then_inc(biased, 1)
            for a in range(ST - POOL_TILES, ST):
                pool.wait_ge(sel_done, a + 1)
                for what, value in lot_values(a):
                    pool.tensor_tensor(lots[:, :, :, a * LOT + what], sel[a][:, :, :], value, ALU.mult)\
                        .then_inc(lots_pool, 1)
                pool.tensor_copy(lots[:, :, :, a * LOT + LOT_TAKEN], sel[a][:, :, :]).then_inc(lots_pool, 1)


def scan_ones(ones, n):
    return ones[:, 0:n]


def expert_phase(nc, t, w1_dram, w2_dram, x1_rows, acc_dram, acc_rows, out, ps):
    with ExitStack() as ctx:
        def sb(name, shape, dt):
            return ctx.enter_context(nc.sbuf_tensor(name, shape, dt))

        def sem(name):
            return ctx.enter_context(nc.semaphore(name))

        w1, w2, w_in = t["w1"], t["w2"], t["expert_w_in"]
        xe = [sb(f"xe{p}", [P, ST, D], F32) for p in range(2)]
        tok = [sb(f"tok{p}", [P, ST], I32) for p in range(2)]
        xeT = sb("xeT", [P, 2, CAP], F32)
        hT = sb("hT", [P, F // P, CAP], F32)
        ye = [sb(f"ye{p}", [P, ST, D], F32) for p in range(2)]
        xe_in = [sem(f"xe_in{p}") for p in range(2)]
        xT_mm = sem("xeT_mm")
        xT_a = sem("xeT_done")
        up_mm = sem("up_mm")
        h_a = sem("relu_by_act")
        h_v = sem("relu_by_dve")
        dn_mm = sem("down_mm")
        ye_done = sem("ye_done")
        tok_done = sem("tok_done")
        added = sem("added")
        folded = sem("folded")
        hold = sem("expert_hold")
        FT = F // P

        def for_experts(eng, body):
            with eng.Fori(0, EX - 2, 2) as e:
                body(e, 0)
                body(e + 1, 1)
            body(EX - 1, 0)

        with nc.Block() as block:
            @block.sync
            def _(sp):
                def load(e, par):
                    sp.wait_ge(dn_mm, e * ST + ST)
                    load_expert(sp, t, w1_dram, w2_dram, e, par)

                with sp.Fori(2, EX - 1, 2) as e:
                    load(e, 0)
                    load(e + 1, 1)
                load(EX - 1, 0)

            @block.tensor
            def _(pe):
                pe.sem_inc(dn_mm, 2 * ST)

                def expert(e, par):
                    half = (e - par) * 8 + 16
                    pe.wait_ge(xe_in[par], half * ST)
                    for k in range(2):
                        pe.wait_ge(xT_a, e * 2 + k + 1)
                        for s in range(ST):
                            mm = pe.transpose(ps[:, k, s * P:(s + 1) * P], xe[par][:, s, k * P:(k + 1) * P],
                                              t["ident"][:, :])
                        mm.then_inc(xT_mm, 1)
                    pe.wait_ge(xT_a, e * 2 + 4)
                    pe.wait_ge(w_in[par], half * 2)
                    for j in range(FT):
                        pe.wait_ge((h_a, h_v)[j % 2], e * (FT // 2) + j // 2 + 1)
                        for k in range(2):
                            mm = pe.matmul(ps[:, 2 + j % 2, :], w1[par][:, k, j * P:(j + 1) * P], xeT[:, k, :],
                                           start=(k == 0), stop=(k == 1))
                        mm.then_inc(up_mm, 1)
                    pe.wait_ge(h_a, e * (FT // 2) + FT // 2 + 1)
                    pe.wait_ge(h_v, e * (FT // 2) + FT // 2 + 1)
                    for s in range(ST):
                        pe.wait_ge(ye_done, e * ST + s + 5)
                        for j in range(FT):
                            mm = pe.matmul(ps[:, 4 + s, 0:D], hT[:, j, s * P:(s + 1) * P], w2[par][:, j, :],
                                           start=(j == 0), stop=(j == FT - 1))
                        mm.then_inc(dn_mm, 1)

                for_experts(pe, expert)

            @block.scalar
            def _(act):
                act.sem_inc(xT_a, 2)
                act.sem_inc(h_a, 1)

                def expert(e, par):
                    for k in range(2):
                        act.wait_ge(xT_mm, e * 2 + k + 5)
                        act.activation(xeT[:, k, :], ps[:, k, :], ACT.Copy).then_inc(xT_a, 1)
                    act.wait_ge(dn_mm, e * ST + 2 * ST)
                    for j in range(0, FT, 2):
                        act.wait_ge(up_mm, e * FT + j + 1)
                        act.activation(hT[:, j, :], ps[:, 2, :], ACT.Relu).then_inc(h_a, 1)

                for_experts(act, expert)

            @block.vector
            def _(dve):
                dve.sem_inc(h_v, 1)
                dve.sem_inc(ye_done, 2 * ST)
                dve.sem_inc(folded, 2 * ST)

                def expert(e, par):
                    one = slice(e, e + 1) if isinstance(e, int) else bass.ds(e, 1)
                    dve.wait_ge(folded, e * ST + ST)
                    dve.wait_ge(dn_mm, e * ST + 2 * ST)
                    for j in range(1, FT, 2):
                        dve.wait_ge(up_mm, e * FT + j + 1)
                        dve.tensor_scalar(hT[:, j, :], ps[:, 3, :], 0.0, None, ALU.max).then_inc(h_v, 1)
                    for s in range(ST):
                        dve.wait_ge(dn_mm, e * ST + 2 * ST + s + 1)
                        dve.tensor_scalar(ye[par][:, s, :], ps[:, 4 + s, 0:D],
                                          t["slot_weight"][:, one, s:s + 1].rearrange("p e a -> p (e a)"), None,
                                          ALU.mult).then_inc(ye_done, 1)

                for_experts(dve, expert)

            @block.gpsimd
            def _(pool):
                def gather(e, par):
                    one = slice(e, e + 1) if isinstance(e, int) else bass.ds(e, 1)
                    pool.wait_ge(xT_mm, e * 2 + 2)
                    pool.sem_inc(hold, 1)
                    pool.tensor_copy(tok[par][:, :], t["slot_token"][:, one, :].rearrange("p e a -> p (e a)"))\
                        .then_inc(tok_done, 1)
                    pool.wait_ge(tok_done, e + 1)
                    pool.sem_inc(hold, 1)
                    for s in range(ST):
                        pool.indirect_dma_start(out=xe[par][:, s, :], out_offset=None, in_=x1_rows,
                                                in_offset=bass.IndirectOffsetOnAxis(ap=tok[par][:, s:s + 1], axis=0),
                                                bounds_check=T + CAP - 1, oob_is_err=False).then_inc(xe_in[par], 16)

                def add(e, par):
                    for s in range(ST):
                        pool.wait_ge(ye_done, e * ST + 2 * ST + s + 1)
                        pool.sem_inc(hold, 1)
                        pool.indirect_dma_start(out=acc_rows, out_offset=bass.IndirectOffsetOnAxis(
                            ap=tok[par][:, s:s + 1], axis=0), in_=ye[par][:, s, :], in_offset=None,
                            bounds_check=T + CAP - 1, oob_is_err=False, compute_op=ALU.add).then_inc(added, 16)
                        pool.wait_ge(added, e * (16 * ST) + 16 * (s + 1))
                        pool.sem_inc(folded, 1)

                pool.sem_inc(xT_mm, 4)
                gather(0, 0)
                with pool.Fori(0, EX - 2, 2) as e:
                    gather(e + 1, 1)
                    add(e, 0)
                    gather(e + 2, 0)
                    add(e + 1, 1)
                add(EX - 1, 0)
                pool.wait_ge(added, 16 * ST * EX)

        a_in = [sem(f"a_in{p}") for p in range(4)]
        sums = sb("sums", [P, NT, D], F32)
        stats = sb("stats2", [P, TPC, 6], F32)
        mv = sb("mean_var2", [P, TPC, 2], F32)
        sd = sb("std2", [P, TPC], F32)
        rstd = [sb(f"rstd2_{p}", [P, TPC], F32) for p in range(2)]
        shift = [sb(f"minus_mean_rstd{p}", [P, TPC], F32) for p in range(2)]
        eps = sb("eps2", [P, 1], F32)
        eps_done = sem("eps_done2")
        st_done = sem("stats_done2")
        mv_done = sem("mean_var_done2")
        sd_done = sem("std_done2")
        rs_done = sem("rstd_done2")
        shift_done = sem("minus_mean_rstd_done")
        ln_done = sem("ln_done2")
        stored = sem("stored")

        def one_tile(n, s):
            return sums[:, bass.ds(n * TPC + s, 1), :].rearrange("p a n -> p (a n)")

        with nc.Block() as block:
            @block.sync
            def _(sp):
                with sp.Fori(0, NCH // 4) as i:
                    for q in range(4):
                        n = i * 4 + q
                        sp.wait_ge(a_in[q], i * 16 + 16)
                        sp.dma_start(sums[:, bass.ds(n * TPC, TPC), :], acc_dram[bass.ds(n * TPC, TPC), :, :].rearrange("t p n -> p t n"))\
                          .then_inc(a_in[q], 16)

            @block.scalar
            def _(act):
                act.wait_ge(eps_done, 1)

                def root(n):
                    act.wait_ge(mv_done, n * 4 + 4)
                    act.wait_ge(rs_done, n + 1)
                    act.activation(sd[:, :], mv[:, :, 1], ACT.Sqrt, bias=eps[:, 0:1]).then_inc(sd_done, 1)

                def normalise(n, q):
                    act.wait_ge(shift_done, n + 1)
                    for s in range(TPC):
                        rows = one_tile(n, s)
                        act.activation(rows, rows, ACT.Identity, bias=shift[q % 2][:, s:s + 1],
                                       scale=rstd[q % 2][:, s:s + 1]).then_inc(ln_done, 1)
                    act.wait_ge(ln_done, n * 4 + 4 + 2 * TPC)
                    act.dma_start(out[bass.ds(n * TPC, TPC), :, :].rearrange("t p n -> p t n"),
                                  sums[:, bass.ds(n * TPC, TPC), :]).then_inc(stored, 16)

                root(0)
                with act.Fori(0, NCH // 4 - 1) as i:
                    for q in range(4):
                        root(i * 4 + q + 1)
                        normalise(i * 4 + q, q)
                for q in range(4):
                    n = NCH - 4 + q
                    if q < 3:
                        root(n + 1)
                    normalise(n, q)
                act.wait_ge(stored, 16 * NCH)

            @block.vector
            def _(dve):
                dve.sem_inc(rs_done, 1)
                dve.sem_inc(ln_done, 2 * TPC)
                for q in range(4):
                    dve.sem_inc(a_in[q], 16)
                dve.memset(eps[:, :], EPS).then_inc(eps_done, 1)
                with dve.Fori(0, NCH // 4) as i:
                    for q in range(4):
                        n = i * 4 + q
                        dve.wait_ge(a_in[q], i * 16 + 32)
                        for s in range(TPC):
                            dve.bn_stats(stats[:, s, :], one_tile(n, s)).then_inc(st_done, 1)
                        dve.wait_ge(st_done, n * 4 + 4)
                        dve.sem_inc(hold, 1)
                        for s in range(TPC):
                            dve.bn_aggr(mv[:, s, :], stats[:, s, :]).then_inc(mv_done, 1)
                        dve.wait_ge(sd_done, n + 1)
                        dve.wait_ge(ln_done, n * 4 + 4)
                        dve.reciprocal(rstd[q % 2][:, :], sd[:, :]).then_inc(rs_done, 1)
                        dve.wait_ge(rs_done, n + 2)
                        dve.scalar_tensor_tensor(out=shift[q % 2][:, :], in0=mv[:, :, 0], scalar=-1.0,
                                                 in1=rstd[q % 2][:, :], op0=ALU.mult, op1=ALU.mult)\
                           .then_inc(shift_done, 1)
                        dve.wait_ge(shift_done, n + 1)


def build(nc, x, wqkv, bqkv, wout, bout, router_w, router_b, w1, w2, q_pos, k_pos, slopes, out):
    def dram(name, shape, dt):
        return nc.dram_tensor(name, shape, dt, kind="Internal").ap()

    q_pos, k_pos = q_pos.bitcast(BF16), k_pos.bitcast(BF16)

    parts_dram = dram("qk_parts", (2, H, 3, HD, T), BF16)
    shift_dram = dram("shift_rows", (B, H, 3, CH), BF16)
    heads_dram = dram("head_outputs", (B, D, L), F32)
    x1 = dram("x1_rows", (T + CAP, D), F32)
    x1_dram = x1.rearrange("(t p) n -> t p n", p=P)
    acc = dram("token_sums", (T + CAP, D), F32)
    acc_dram = acc.rearrange("(t p) n -> t p n", p=P)
    x_t = x.rearrange("b (t p) n -> (b t) p n", p=P)
    out_t = out.rearrange("b (t p) n -> (b t) p n", p=P)
    with ExitStack() as ctx:
        t = {
            "bounded": ctx.enter_context(nc.sbuf_tensor("bounded", [1, 1], I32)),
            "ident": ctx.enter_context(nc.sbuf_tensor("ident", [P, P], F32)),
            "token_ids": ctx.enter_context(nc.sbuf_tensor("token_ids", [P, P], I32)),
            "beyond": ctx.enter_context(nc.sbuf_tensor("beyond", [P, ST], F32)),
            "slot_weight": ctx.enter_context(nc.sbuf_tensor("slot_weight", [P, EX, ST], F32)),
            "slot_token": ctx.enter_context(nc.sbuf_tensor("slot_token", [P, EX, ST], I32)),
            "w_out": ctx.enter_context(nc.sbuf_tensor("w_out", [P, 2, D], F32)),
            "b_out": ctx.enter_context(nc.sbuf_tensor("b_out", [P, TPC, D], F32)),
            "router_wT": ctx.enter_context(nc.sbuf_tensor("router_wT", [P, 2, E], F32)),
            "router_bias": ctx.enter_context(nc.sbuf_tensor("router_bias", [P, TPC, E], F32)),
            "route_w_in": ctx.enter_context(nc.semaphore("route_w_in")),
            "ident_done": ctx.enter_context(nc.semaphore("ident_done")),
        }
        ps = ctx.enter_context(nc.psum_tensor("ps", [P, 8, 512], F32))
        with ExitStack() as v_life:
            for name, shape in (("distance", [P, P]), ("minus_slopes", [P, H]), ("near_bias", [P, H, P])):
                t[name] = v_life.enter_context(nc.sbuf_tensor(name, shape, F32))
            t["v_heads"] = [v_life.enter_context(nc.sbuf_tensor(f"v_head{b}", [P, KB, 32], F32)) for b in range(B)]
            t["v"] = v_life.enter_context(nc.sbuf_tensor("v", [P, NT, D], F32))
            project_phase(nc, t, x_t, wqkv, bqkv, wout, bout, router_w, router_b, slopes, parts_dram,
                          shift_dram, x1_dram, acc_dram, ps)
            attention_phase(nc, t, parts_dram, shift_dram, heads_dram, q_pos, k_pos, ps)
        t["w1"] = [ctx.enter_context(nc.sbuf_tensor(f"w1_{p}", [P, 2, F], F32)) for p in range(2)]
        t["w2"] = [ctx.enter_context(nc.sbuf_tensor(f"w2_{p}", [P, F // P, D], F32)) for p in range(2)]
        t["expert_w_in"] = [ctx.enter_context(nc.semaphore(f"expert_w_in{p}")) for p in range(2)]
        route_phase(nc, t, x_t, heads_dram, w1, w2, x1_dram, acc_dram, ps)
        expert_phase(nc, t, w1, w2, x1, acc_dram, acc, out_t, ps)


_INS = ["L0_attn_x", "L0_attn_Wqkv", "L0_attn_bqkv", "L0_attn_Wout", "L0_attn_bout",
        "L0_ffn_router_w", "L0_ffn_router_b", "L0_ffn_experts_inter", "L0_ffn_experts_out"]


def bf16_bits(a):
    import numpy as np
    u = np.ascontiguousarray(a, np.float32).view(np.uint32)
    return ((u + 0x7FFF + ((u >> 16) & 1)) >> 16).astype(np.uint16)


def bf16_value(bits):
    import numpy as np
    return (bits.astype(np.uint32) << 16).view(np.float32)


def shape_constants():
    import numpy as np
    start = 2 ** (-2 ** (-(np.log2(H) - 3)))
    slopes = np.asarray([start ** i for i in range(H)], np.float32)
    parts, rest = [], slopes.copy()
    for _ in range(3):
        parts.append(bf16_value(bf16_bits(rest)))
        rest = rest - parts[-1]
    pos = np.arange(L)
    hi, lo = (pos // P) * P, pos % P
    q_pos = np.zeros((H, 3 + POS, L), np.float32)
    k_pos = np.zeros((H, 2, 3 + POS, L), np.float32)
    for p in range(3):
        for r, (part, of_query) in enumerate([(hi, True), (hi, False), (lo, True), (lo, False)]):
            row = 3 + 4 * p + r
            for h in range(H):
                s = float(parts[p][h])
                q_pos[h, row] = part if of_query else s
                for ver, sign in ((RIGHT, -1.0), (LEFT, 1.0)):
                    k_pos[h, ver, row] = sign * s if of_query else -sign * part
    k_pos[:, :, 0:3, :] = 1
    minus = np.ascontiguousarray(np.broadcast_to(-slopes[None, :], (P, H)), dtype=np.float32)
    return {"q_pos": bf16_bits(q_pos), "k_pos": bf16_bits(k_pos), "minus_slopes": minus}


def kernel(**inputs):
    import numpy as _np
    import concourse.bacc as _bacc
    from concourse import mybir as _mybir
    from concourse.bass_utils import run_bass_kernel_spmd as _run

    nc = _bacc.Bacc("TRN2", target_bir_lowering=False, num_devices=1)
    arrays, args = {}, []
    given = {n: _np.ascontiguousarray(inputs[n]) for n in _INS}
    given.update(shape_constants())
    for name, a in given.items():
        arrays[f"in_{name}_dram"] = a
        args.append(nc.dram_tensor(f"in_{name}_dram", a.shape, _mybir.dt.from_np(a.dtype), kind="ExternalInput").ap())
    args.append(nc.dram_tensor("out_0_dram", (B, L, D), _mybir.dt.float32, kind="ExternalOutput").ap())
    build(nc, *args)
    r = _run(nc, [arrays], core_ids=[0])
    return r.results[0]["out_0_dram"]
```
